# Optimizing a Trainium2 kernel written in Bass

```python
import numpy as np
import jax
import jax.numpy as jnp

def _softmax(x, axis=-1):
    return jax.nn.softmax(x, axis=axis)

def _gelu(x):
    return jax.nn.gelu(x, approximate=True)

def _silu(x):
    return jax.nn.silu(x)

def _sigmoid(x):
    return jax.nn.sigmoid(x)

def _layernorm(x, axis=-1, eps=1e-05):
    m = jnp.mean(x, axis=axis, keepdims=True)
    v = jnp.var(x, axis=axis, keepdims=True)
    return (x - m) / jnp.sqrt(v + eps)

def _scatter_add(tgt, idx, src, axis=0):
    return tgt.at[idx].add(src)

def _segment_sum(src, seg, n):
    return jax.ops.segment_sum(src, seg, n)
kernel_name = 'mk_gnn_ffn_d4_gnn_r32_087cbc'

def setup_inputs(seed: int=0):
    np.random.seed(seed)
    _w = jnp.asarray

    def _rec_inputs():
        import jax
        import jax.numpy as jnp
        _gk = jax.random.key(seed)
        x = -0.0005207 + 1.001 * jax.random.normal(jax.random.fold_in(_gk, 1), (128, 512), jnp.float32)
        _s = jax.random.randint(jax.random.fold_in(_gk, 2), (1024,), 0, 128, jnp.int32)
        _d = jax.random.randint(jax.random.fold_in(_gk, 3), (1024,), 0, 128, jnp.int32)
        _loop = jnp.arange(128, dtype=jnp.int32)
        src = jnp.concatenate([_s, _d, _loop])
        dst = jnp.concatenate([_d, _s, _loop])
        _o = jnp.argsort(dst, stable=True)
        src = src[_o]
        dst = dst[_o]
        return (x, src, dst)
    x, src, dst = _rec_inputs()

    def _L0_gnn_setup():
        import jax, jax.numpy as jnp
        import numpy as np
        ALPHA = 0.2
        NEG_INF = -9000000000000000.0
        key = jax.random.key(seed)
        k1, k2, k3, k4 = jax.random.split(key, 4)
        N, C, F, H, E = (128, 512, 64, 8, 4096)
        x = jax.random.normal(k1, (N, C), dtype=jnp.float32)
        edge_index = jax.random.randint(k2, (2, E), 0, N, dtype=jnp.int64)
        lim_W = 1.414 * np.sqrt(6.0 / (C + F))
        lim_a = 1.414 * np.sqrt(6.0 / (2 * F + 1))
        W = jax.random.uniform(k3, (H, C, F), minval=-lim_W, maxval=lim_W, dtype=jnp.float32)
        a = jax.random.uniform(k4, (H, 2 * F, 1), minval=-lim_a, maxval=lim_a, dtype=jnp.float32)
        return {'x': x, 'edge_index': edge_index, 'W': W, 'a': a}
    _L0_gnn_all = _L0_gnn_setup()
    _L0_gnn_in = {k: v for k, v in _L0_gnn_all.items() if k in ('W', 'a')}
    del _L0_gnn_all

    def _L0_ffn_setup():
        import jax, jax.numpy as jnp
        import numpy as np
        D_MODEL = 512
        N_HEADS = 8
        KV_OPTS = (8, 4, 1)
        D_K = D_MODEL // N_HEADS

        def gqa(x, wq, wk, wv, wo, n_kv):
            B, S, _ = x.shape
            groups = N_HEADS // n_kv
            q = (x @ wq).reshape(B, S, N_HEADS, D_K).transpose(0, 2, 1, 3)
            k = (x @ wk).reshape(B, S, n_kv, D_K).transpose(0, 2, 1, 3)
            v = (x @ wv).reshape(B, S, n_kv, D_K).transpose(0, 2, 1, 3)
            k = jnp.repeat(k, groups, axis=1)
            v = jnp.repeat(v, groups, axis=1)
            scores = jnp.einsum('bhqd,bhkd->bhqk', q, k) / jnp.sqrt(jnp.float32(D_K))
            attn = jax.nn.softmax(scores, axis=-1)
            out = jnp.einsum('bhqk,bhkd->bhqd', attn, v)
            out = out.transpose(0, 2, 1, 3).reshape(B, S, D_MODEL)
            return out @ wo
        key = jax.random.key(seed)
        ks = jax.random.split(key, 32)
        it = iter(ks)
        s = 0.02
        inp = {'x': jax.random.normal(next(it), (64, 1024, D_MODEL), dtype=jnp.float32)}
        inp['r_w1'] = jax.random.normal(next(it), (D_MODEL, D_MODEL // 4), jnp.float32) * s
        inp['r_b1'] = jnp.zeros((D_MODEL // 4,), jnp.float32)
        inp['r_w2'] = jax.random.normal(next(it), (D_MODEL // 4, len(KV_OPTS)), jnp.float32) * s
        inp['r_b2'] = jnp.zeros((len(KV_OPTS),), jnp.float32)
        for i, nkv in enumerate(KV_OPTS):
            inp[f'wq{i}'] = jax.random.normal(next(it), (D_MODEL, D_MODEL), jnp.float32) * s
            inp[f'wk{i}'] = jax.random.normal(next(it), (D_MODEL, nkv * D_K), jnp.float32) * s
            inp[f'wv{i}'] = jax.random.normal(next(it), (D_MODEL, nkv * D_K), jnp.float32) * s
            inp[f'wo{i}'] = jax.random.normal(next(it), (D_MODEL, D_MODEL), jnp.float32) * s
        return inp
    _L0_ffn_all = _L0_ffn_setup()
    _L0_ffn_in = {k: v for k, v in _L0_ffn_all.items() if k in ('r_w1', 'r_b1', 'r_w2', 'r_b2', 'wq0', 'wk0', 'wv0', 'wo0', 'wq1', 'wk1', 'wv1', 'wo1', 'wq2', 'wk2', 'wv2', 'wo2')}
    del _L0_ffn_all

    def _L1_gnn_setup():
        import jax, jax.numpy as jnp
        import numpy as np
        B = 32
        MAXN = 64
        HEADS = 8
        DH = 64
        M = 256
        D = 512
        EPS = 1e-05
        KEPS = 1e-06

        def _batchnorm(x, g, b):
            mu = jnp.mean(x, axis=0)
            var = jnp.mean((x - mu) ** 2, axis=0)
            return (x - mu) * jax.lax.rsqrt(var + EPS) * g + b

        def _forward(x, batch, edge_index, norm1_g, norm1_b, norm2_g, norm2_b, W_conv, b_conv, Wq, Wk, Wv, Wo, proj):
            N = x.shape[0]
            E = edge_index.shape[1]
            h = x
            xn = _batchnorm(x, norm1_g, norm1_b)
            msg = xn[edge_index[0]]
            agg = jax.ops.segment_sum(msg, edge_index[1], num_segments=N)
            deg = jax.ops.segment_sum(jnp.ones((E,), x.dtype), edge_index[1], num_segments=N)
            agg = agg / jnp.maximum(deg, 1.0)[:, None]
            conv_out = jax.nn.relu(agg @ W_conv + b_conv)
            counts = jax.ops.segment_sum(jnp.ones((N,), jnp.int32), batch, num_segments=B)
            offsets = jnp.concatenate([jnp.zeros((1,), jnp.int32), jnp.cumsum(counts)[:-1]])
            pos = jnp.arange(N, dtype=jnp.int32) - offsets[batch]
            h_dense = jnp.zeros((B, MAXN, D), x.dtype).at[batch, pos].set(h)
            mask = jnp.zeros((B, MAXN), bool).at[batch, pos].set(True)

            def heads(t, W):
                return (t @ W).reshape(B, MAXN, HEADS, DH).transpose(0, 2, 1, 3)
            q, k, v = (heads(h_dense, Wq), heads(h_dense, Wk), heads(h_dense, Wv))
            scale = DH ** (-0.25)

            def phi(t, is_query):
                t = t * scale
                u = jnp.einsum('bhnd,md->bhnm', t, proj)
                diag = 0.5 * jnp.sum(t * t, axis=-1, keepdims=True)
                if is_query:
                    m_ = jnp.max(u, axis=-1, keepdims=True)
                else:
                    m_ = jnp.max(u, axis=(-2, -1), keepdims=True)
                return jnp.exp(u - diag - jax.lax.stop_gradient(m_)) / np.sqrt(M) + KEPS
            qf = phi(q, True)
            kf = phi(k, False) * mask[:, None, :, None]
            vm = v * mask[:, None, :, None]
            kv = jnp.einsum('bhnm,bhnd->bhmd', kf, vm)
            z = 1.0 / (jnp.einsum('bhnm,bhm->bhn', qf, kf.sum(axis=2)) + KEPS)
            attn = jnp.einsum('bhnm,bhmd->bhnd', qf, kv) * z[..., None]
            attn = attn.transpose(0, 2, 1, 3).reshape(B, MAXN, D) @ Wo
            h_attn = attn[batch, pos]
            return _batchnorm(conv_out + h_attn + h, norm2_g, norm2_b)
        key = jax.random.key(seed)
        ks = jax.random.split(key, 10)
        sizes = 1024 + np.arange(B) * 131 % 1025
        N = int(sizes.sum())
        E = N * 8
        batch = jnp.asarray(np.repeat(np.arange(B), sizes), dtype=jnp.int32)
        edge_index = jax.random.randint(ks[0], (2, E), 0, N, dtype=jnp.int32)
        s = 1.0 / np.sqrt(D)
        return {'x': jax.random.normal(ks[1], (N, D), jnp.float32), 'batch': batch, 'edge_index': edge_index, 'norm1_g': jnp.ones((D,), jnp.float32), 'norm1_b': jnp.zeros((D,), jnp.float32), 'norm2_g': jnp.ones((D,), jnp.float32), 'norm2_b': jnp.zeros((D,), jnp.float32), 'W_conv': jax.random.normal(ks[2], (D, D), jnp.float32) * s, 'b_conv': jnp.zeros((D,), jnp.float32), 'Wq': jax.random.normal(ks[3], (D, D), jnp.float32) * s, 'Wk': jax.random.normal(ks[4], (D, D), jnp.float32) * s, 'Wv': jax.random.normal(ks[5], (D, D), jnp.float32) * s, 'Wo': jax.random.normal(ks[6], (D, D), jnp.float32) * s, 'proj': jax.random.normal(ks[7], (M, DH), jnp.float32)}
    _L1_gnn_all = _L1_gnn_setup()
    _L1_gnn_in = {k: v for k, v in _L1_gnn_all.items() if k in ('norm1_g', 'norm1_b', 'norm2_g', 'norm2_b', 'W_conv', 'b_conv', 'Wq', 'Wk', 'Wv', 'Wo', 'proj')}
    del _L1_gnn_all

    def _L1_ffn_setup():
        import jax, jax.numpy as jnp
        import numpy as np
        DIM = 512
        HEADS = 8
        DIM_KEY = 32
        NUM_EXPERTS = 2048
        NUM_KEYS = 256
        TOPK = 16
        BN_EPS = 1e-05

        def peer_forward(x, w_q, keys, weight_down_embed, weight_up_embed):
            b, n, _ = x.shape
            q = x @ w_q * (1.0 / np.sqrt(1.0 + BN_EPS))
            queries = q.reshape(b, n, 2, HEADS, DIM_KEY).transpose(2, 0, 1, 3, 4)
            sim = jnp.einsum('pbnhd,hkpd->pbnhk', queries, keys)
            v0, i0 = jax.lax.top_k(sim[0], TOPK)
            v1, i1 = jax.lax.top_k(sim[1], TOPK)
            all_scores = v0[..., :, None] + i0[..., None, :].astype(v0.dtype)
            all_scores = all_scores.reshape(*all_scores.shape[:-2], -1)
            scores, pk_indices = jax.lax.top_k(all_scores, TOPK)
            weights_down = jnp.take(weight_down_embed, pk_indices, axis=0)
            weights_up = jnp.take(weight_up_embed, pk_indices, axis=0)
            h = jnp.einsum('bnd,bnhkd->bnhk', q, weights_down)
            h = jax.nn.gelu(h)
            h = h * jax.nn.softmax(scores, axis=-1)
            out = jnp.einsum('bnhk,bnhkd->bnd', h, weights_up)
            return out
        key = jax.random.key(seed)
        k1, k2, k3, k4, k5 = jax.random.split(key, 5)
        b, n = (2, 512)
        x = jax.random.normal(k1, (b, n, DIM), dtype=jnp.float32)
        w_q = jax.random.normal(k2, (DIM, DIM_KEY * HEADS * 2), dtype=jnp.float32) / np.sqrt(DIM)
        keys = jax.random.normal(k3, (HEADS, NUM_KEYS, 2, DIM_KEY), dtype=jnp.float32) * 0.01
        weight_down_embed = jax.random.normal(k4, (NUM_EXPERTS, DIM), dtype=jnp.float32) * 0.01
        weight_up_embed = jax.random.normal(k5, (NUM_EXPERTS, DIM), dtype=jnp.float32) * 0.01
        return {'x': x, 'w_q': w_q, 'keys': keys, 'weight_down_embed': weight_down_embed, 'weight_up_embed': weight_up_embed}
    _L1_ffn_all = _L1_ffn_setup()
    _L1_ffn_in = {k: v for k, v in _L1_ffn_all.items() if k in ('w_q', 'keys', 'weight_down_embed', 'weight_up_embed')}
    del _L1_ffn_all

    def _L2_gnn_setup():
        import jax, jax.numpy as jnp
        import numpy as np
        N_NODES = 1250
        N_EDGES = 20000
        DIM_H = 512
        N_HEADS = 8
        D_HEAD = DIM_H // N_HEADS

        def _exphormer_attn(x, edge_index, Wq, Wk, Wv):
            N, D = x.shape
            H, d = (N_HEADS, D_HEAD)
            Q = (x @ Wq).reshape(N, H, d)
            K = (x @ Wk).reshape(N, H, d)
            V = (x @ Wv).reshape(N, H, d)
            src, dst = (edge_index[0], edge_index[1])
            scale = np.float32(1.0 / np.sqrt(d))
            score = jnp.einsum('ehd,ehd->eh', K[src], Q[dst]) * scale
            score = jnp.exp(jnp.clip(score, -5.0, 5.0))[..., None]
            msg = V[src] * score
            wV = jax.ops.segment_sum(msg, dst, num_segments=N)
            Z = jax.ops.segment_sum(score, dst, num_segments=N)
            return (wV / (Z + 1e-06)).reshape(N, D)
        key = jax.random.key(seed)
        ks = jax.random.split(key, 8)
        x = jax.random.normal(ks[0], (N_NODES, DIM_H), dtype=jnp.float32)
        edge_index = jax.random.randint(ks[1], (2, N_EDGES), 0, N_NODES, dtype=jnp.int32)
        virt_h = jax.random.normal(ks[2], (1, DIM_H), dtype=jnp.float32)
        virt_edge_index = jnp.zeros((2, 1), dtype=jnp.int32)
        s = 1.0 / np.sqrt(DIM_H)
        Wq = jax.random.normal(ks[3], (DIM_H, DIM_H), dtype=jnp.float32) * s
        Wk = jax.random.normal(ks[4], (DIM_H, DIM_H), dtype=jnp.float32) * s
        Wv = jax.random.normal(ks[5], (DIM_H, DIM_H), dtype=jnp.float32) * s
        bn_gamma = jnp.ones((DIM_H,), dtype=jnp.float32)
        bn_beta = jnp.zeros((DIM_H,), dtype=jnp.float32)
        return {'x': x, 'edge_index': edge_index, 'virt_h': virt_h, 'virt_edge_index': virt_edge_index, 'Wq': Wq, 'Wk': Wk, 'Wv': Wv, 'bn_gamma': bn_gamma, 'bn_beta': bn_beta}
    _L2_gnn_all = _L2_gnn_setup()
    _L2_gnn_in = {k: v for k, v in _L2_gnn_all.items() if k in ('virt_h', 'virt_edge_index', 'Wq', 'Wk', 'Wv', 'bn_gamma', 'bn_beta')}
    del _L2_gnn_all

    def _L2_ffn_setup():
        import jax, jax.numpy as jnp
        import numpy as np
        B, S, D, F, E, K, H = (4, 1024, 512, 64, 8, 2, 8)
        HEAD_DIM = D // H

        def _layernorm(x, g, b):
            m = x.mean(-1, keepdims=True)
            v = ((x - m) ** 2).mean(-1, keepdims=True)
            return (x - m) * jax.lax.rsqrt(v + 1e-05) * g + b

        def _expert(x, Wqkv, bqkv, Wo, bo, g1, be1, W1, bf1, W2, bf2, g2, be2):
            b, s, d = x.shape
            qkv = x @ Wqkv.T + bqkv
            q, k, v = jnp.split(qkv, 3, axis=-1)
            to_heads = lambda t: t.reshape(b, s, H, HEAD_DIM).transpose(0, 2, 1, 3)
            q, k, v = (to_heads(q), to_heads(k), to_heads(v))
            scale = 1.0 / np.sqrt(HEAD_DIM).astype(np.float32)
            attn = jax.nn.softmax(jnp.einsum('bhqd,bhkd->bhqk', q * scale, k), axis=-1)
            ctx = jnp.einsum('bhqk,bhkd->bhqd', attn, v).transpose(0, 2, 1, 3).reshape(b, s, d)
            ctx = ctx @ Wo.T + bo
            x = _layernorm(x + ctx, g1, be1)
            h = jax.nn.gelu(x @ W1.T + bf1, approximate=False)
            h = jax.nn.gelu(h @ W2.T + bf2, approximate=False)
            return _layernorm(x + h, g2, be2)
        key = jax.random.key(seed)
        ks = jax.random.split(key, 8)
        s = 0.02
        return {'x': jax.random.normal(ks[0], (B, S, D), jnp.float32), 'gate_Wk': jax.random.normal(ks[1], (D, D), jnp.float32) * s, 'gate_bk': jnp.zeros((D,), jnp.float32), 'expert_queries': jax.random.normal(ks[2], (E, D), jnp.float32), 'Wqkv': jax.random.normal(ks[3], (E, 3 * D, D), jnp.float32) * s, 'bqkv': jnp.zeros((E, 3 * D), jnp.float32), 'Wo': jax.random.normal(ks[4], (E, D, D), jnp.float32) * s, 'bo': jnp.zeros((E, D), jnp.float32), 'g1': jnp.ones((E, D), jnp.float32), 'be1': jnp.zeros((E, D), jnp.float32), 'W1': jax.random.normal(ks[5], (E, F, D), jnp.float32) * s, 'bf1': jnp.zeros((E, F), jnp.float32), 'W2': jax.random.normal(ks[6], (E, D, F), jnp.float32) * s, 'bf2': jnp.zeros((E, D), jnp.float32), 'g2': jnp.ones((E, D), jnp.float32), 'be2': jnp.zeros((E, D), jnp.float32)}
    _L2_ffn_all = _L2_ffn_setup()
    _L2_ffn_in = {k: v for k, v in _L2_ffn_all.items() if k in ('gate_Wk', 'gate_bk', 'expert_queries', 'Wqkv', 'bqkv', 'Wo', 'bo', 'g1', 'be1', 'W1', 'bf1', 'W2', 'bf2', 'g2', 'be2')}
    del _L2_ffn_all

    def _L3_gnn_setup():
        import jax, jax.numpy as jnp
        import numpy as np
        N = 10000
        E = 5000
        IN = 512
        HID = 512
        OUT = 512

        def _gcn_norm(edge_index, n):
            loops = jnp.arange(n, dtype=edge_index.dtype)
            row = jnp.concatenate([edge_index[0], loops])
            col = jnp.concatenate([edge_index[1], loops])
            deg = jax.ops.segment_sum(jnp.ones_like(col, jnp.float32), col, num_segments=n)
            dis = jnp.where(deg > 0, jax.lax.rsqrt(jnp.maximum(deg, 1.0)), 0.0)
            norm = dis[row] * dis[col]
            return (row, col, norm)

        def _gcn_layer(x, row, col, norm, W, b, n):
            h = x @ W
            msg = h[row] * norm[:, None]
            out = jax.ops.segment_sum(msg, col, num_segments=n)
            return out + b
        key = jax.random.key(seed)
        ks = jax.random.split(key, 8)
        x = jax.random.normal(ks[0], (N, IN), dtype=jnp.float32)
        edge_index = jax.random.randint(ks[1], (2, E), 0, N, dtype=jnp.int64)

        def w(k, fi, fo):
            return jax.random.normal(k, (fi, fo), dtype=jnp.float32) * (1.0 / np.sqrt(fi)).astype(np.float32)
        return {'x': x, 'edge_index': edge_index, 'W1': w(ks[2], IN, HID), 'b1': jnp.zeros((HID,), jnp.float32), 'W2': w(ks[3], HID, HID), 'b2': jnp.zeros((HID,), jnp.float32), 'W3': w(ks[4], HID, OUT), 'b3': jnp.zeros((OUT,), jnp.float32)}
    _L3_gnn_all = _L3_gnn_setup()
    _L3_gnn_in = {k: v for k, v in _L3_gnn_all.items() if k in ('W1', 'b1', 'W2', 'b2', 'W3', 'b3')}
    del _L3_gnn_all

    def _L3_ffn_setup():
        import jax, jax.numpy as jnp
        import numpy as np
        S, B, I, O, H, E, K = (128, 32, 512, 512, 512, 8, 2)

        def _expert(x_seq, Wi, Wh, b, Wo, bo):
            Bsz = x_seq.shape[1]
            Hd = Wh.shape[0]

            def step(carry, xt):
                h, c = carry
                gates = xt @ Wi + h @ Wh + b
                i_, f_, g_, o_ = jnp.split(gates, 4, axis=-1)
                c = jax.nn.sigmoid(f_) * c + jax.nn.sigmoid(i_) * jnp.tanh(g_)
                h = jax.nn.sigmoid(o_) * jnp.tanh(c)
                return ((h, c), h @ Wo + bo)
            init = (jnp.zeros((Bsz, Hd), x_seq.dtype), jnp.zeros((Bsz, Hd), x_seq.dtype))
            _, ys = jax.lax.scan(step, init, x_seq)
            return ys
        key = jax.random.key(seed)
        ks = jax.random.split(key, 6)
        s = 0.02
        return {'x': jax.random.normal(ks[0], (S, B, I), dtype=jnp.float32), 'router_w': jax.random.normal(ks[1], (I, E), dtype=jnp.float32) * s, 'router_b': jnp.zeros((E,), dtype=jnp.float32), 'Wi': jax.random.normal(ks[2], (E, I, 4 * H), dtype=jnp.float32) * s, 'Wh': jax.random.normal(ks[3], (E, H, 4 * H), dtype=jnp.float32) * s, 'b': jnp.zeros((E, 4 * H), dtype=jnp.float32), 'Wo': jax.random.normal(ks[4], (E, H, O), dtype=jnp.float32) * s, 'bo': jnp.zeros((E, O), dtype=jnp.float32)}
    _L3_ffn_all = _L3_ffn_setup()
    _L3_ffn_in = {k: v for k, v in _L3_ffn_all.items() if k in ('router_w', 'router_b', 'Wi', 'Wh', 'b', 'Wo', 'bo')}
    del _L3_ffn_all
    return {'x': x, 'src': src, 'dst': dst, 'L0_gnn_W': _L0_gnn_in['W'], 'L0_gnn_a': _L0_gnn_in['a'], 'L0_ffn_r_w1': _L0_ffn_in['r_w1'], 'L0_ffn_r_b1': _L0_ffn_in['r_b1'], 'L0_ffn_r_w2': _L0_ffn_in['r_w2'], 'L0_ffn_r_b2': _L0_ffn_in['r_b2'], 'L0_ffn_wq0': _L0_ffn_in['wq0'], 'L0_ffn_wk0': _L0_ffn_in['wk0'], 'L0_ffn_wv0': _L0_ffn_in['wv0'], 'L0_ffn_wo0': _L0_ffn_in['wo0'], 'L0_ffn_wq1': _L0_ffn_in['wq1'], 'L0_ffn_wk1': _L0_ffn_in['wk1'], 'L0_ffn_wv1': _L0_ffn_in['wv1'], 'L0_ffn_wo1': _L0_ffn_in['wo1'], 'L0_ffn_wq2': _L0_ffn_in['wq2'], 'L0_ffn_wk2': _L0_ffn_in['wk2'], 'L0_ffn_wv2': _L0_ffn_in['wv2'], 'L0_ffn_wo2': _L0_ffn_in['wo2'], 'L1_gnn_norm1_g': _L1_gnn_in['norm1_g'], 'L1_gnn_norm1_b': _L1_gnn_in['norm1_b'], 'L1_gnn_norm2_g': _L1_gnn_in['norm2_g'], 'L1_gnn_norm2_b': _L1_gnn_in['norm2_b'], 'L1_gnn_W_conv': _L1_gnn_in['W_conv'], 'L1_gnn_b_conv': _L1_gnn_in['b_conv'], 'L1_gnn_Wq': _L1_gnn_in['Wq'], 'L1_gnn_Wk': _L1_gnn_in['Wk'], 'L1_gnn_Wv': _L1_gnn_in['Wv'], 'L1_gnn_Wo': _L1_gnn_in['Wo'], 'L1_gnn_proj': _L1_gnn_in['proj'], 'L1_ffn_w_q': _L1_ffn_in['w_q'], 'L1_ffn_keys': _L1_ffn_in['keys'], 'L1_ffn_weight_down_embed': _L1_ffn_in['weight_down_embed'], 'L1_ffn_weight_up_embed': _L1_ffn_in['weight_up_embed'], 'L2_gnn_virt_h': _L2_gnn_in['virt_h'], 'L2_gnn_virt_edge_index': _L2_gnn_in['virt_edge_index'], 'L2_gnn_Wq': _L2_gnn_in['Wq'], 'L2_gnn_Wk': _L2_gnn_in['Wk'], 'L2_gnn_Wv': _L2_gnn_in['Wv'], 'L2_gnn_bn_gamma': _L2_gnn_in['bn_gamma'], 'L2_gnn_bn_beta': _L2_gnn_in['bn_beta'], 'L2_ffn_gate_Wk': _L2_ffn_in['gate_Wk'], 'L2_ffn_gate_bk': _L2_ffn_in['gate_bk'], 'L2_ffn_expert_queries': _L2_ffn_in['expert_queries'], 'L2_ffn_Wqkv': _L2_ffn_in['Wqkv'], 'L2_ffn_bqkv': _L2_ffn_in['bqkv'], 'L2_ffn_Wo': _L2_ffn_in['Wo'], 'L2_ffn_bo': _L2_ffn_in['bo'], 'L2_ffn_g1': _L2_ffn_in['g1'], 'L2_ffn_be1': _L2_ffn_in['be1'], 'L2_ffn_W1': _L2_ffn_in['W1'], 'L2_ffn_bf1': _L2_ffn_in['bf1'], 'L2_ffn_W2': _L2_ffn_in['W2'], 'L2_ffn_bf2': _L2_ffn_in['bf2'], 'L2_ffn_g2': _L2_ffn_in['g2'], 'L2_ffn_be2': _L2_ffn_in['be2'], 'L3_gnn_W1': _L3_gnn_in['W1'], 'L3_gnn_b1': _L3_gnn_in['b1'], 'L3_gnn_W2': _L3_gnn_in['W2'], 'L3_gnn_b2': _L3_gnn_in['b2'], 'L3_gnn_W3': _L3_gnn_in['W3'], 'L3_gnn_b3': _L3_gnn_in['b3'], 'L3_ffn_router_w': _L3_ffn_in['router_w'], 'L3_ffn_router_b': _L3_ffn_in['router_b'], 'L3_ffn_Wi': _L3_ffn_in['Wi'], 'L3_ffn_Wh': _L3_ffn_in['Wh'], 'L3_ffn_b': _L3_ffn_in['b'], 'L3_ffn_Wo': _L3_ffn_in['Wo'], 'L3_ffn_bo': _L3_ffn_in['bo']}

def reference(x, src, dst, L0_gnn_W, L0_gnn_a, L0_ffn_r_w1, L0_ffn_r_b1, L0_ffn_r_w2, L0_ffn_r_b2, L0_ffn_wq0, L0_ffn_wk0, L0_ffn_wv0, L0_ffn_wo0, L0_ffn_wq1, L0_ffn_wk1, L0_ffn_wv1, L0_ffn_wo1, L0_ffn_wq2, L0_ffn_wk2, L0_ffn_wv2, L0_ffn_wo2, L1_gnn_norm1_g, L1_gnn_norm1_b, L1_gnn_norm2_g, L1_gnn_norm2_b, L1_gnn_W_conv, L1_gnn_b_conv, L1_gnn_Wq, L1_gnn_Wk, L1_gnn_Wv, L1_gnn_Wo, L1_gnn_proj, L1_ffn_w_q, L1_ffn_keys, L1_ffn_weight_down_embed, L1_ffn_weight_up_embed, L2_gnn_virt_h, L2_gnn_virt_edge_index, L2_gnn_Wq, L2_gnn_Wk, L2_gnn_Wv, L2_gnn_bn_gamma, L2_gnn_bn_beta, L2_ffn_gate_Wk, L2_ffn_gate_bk, L2_ffn_expert_queries, L2_ffn_Wqkv, L2_ffn_bqkv, L2_ffn_Wo, L2_ffn_bo, L2_ffn_g1, L2_ffn_be1, L2_ffn_W1, L2_ffn_bf1, L2_ffn_W2, L2_ffn_bf2, L2_ffn_g2, L2_ffn_be2, L3_gnn_W1, L3_gnn_b1, L3_gnn_W2, L3_gnn_b2, L3_gnn_W3, L3_gnn_b3, L3_ffn_router_w, L3_ffn_router_b, L3_ffn_Wi, L3_ffn_Wh, L3_ffn_b, L3_ffn_Wo, L3_ffn_bo):
    import jax
    import jax.numpy as jnp

    def _L0_gnn_ref(x, edge_index, W, a):
        import jax, jax.numpy as jnp
        import numpy as np
        ALPHA = 0.2
        NEG_INF = -9000000000000000.0
        N = x.shape[0]
        H, C, F = W.shape
        adj = jnp.zeros((N, N), dtype=bool).at[edge_index[0], edge_index[1]].set(True)
        diag = jnp.arange(N)
        adj = adj.at[diag, diag].set(True)
        h = jnp.einsum('nc,hcf->hnf', x, W)
        a_src = a[:, :F, 0]
        a_dst = a[:, F:, 0]
        s_src = jnp.einsum('hnf,hf->hn', h, a_src)
        s_dst = jnp.einsum('hnf,hf->hn', h, a_dst)
        e = s_src[:, :, None] + s_dst[:, None, :]
        e = jnp.where(e > 0, e, ALPHA * e)
        e = jnp.where(adj[None, :, :], e, NEG_INF)
        att = jax.nn.softmax(e, axis=-1)
        out = jnp.einsum('hij,hjf->hif', att, h)
        out = jnp.transpose(out, (1, 0, 2)).reshape(N, H * F)
        return jax.nn.softmax(out, axis=1)

    def _L0_ffn_ref(x, r_w1, r_b1, r_w2, r_b2, wq0, wk0, wv0, wo0, wq1, wk1, wv1, wo1, wq2, wk2, wv2, wo2):
        import jax, jax.numpy as jnp
        import numpy as np
        D_MODEL = 512
        N_HEADS = 8
        KV_OPTS = (8, 4, 1)
        D_K = D_MODEL // N_HEADS

        def gqa(x, wq, wk, wv, wo, n_kv):
            B, S, _ = x.shape
            groups = N_HEADS // n_kv
            q = (x @ wq).reshape(B, S, N_HEADS, D_K).transpose(0, 2, 1, 3)
            k = (x @ wk).reshape(B, S, n_kv, D_K).transpose(0, 2, 1, 3)
            v = (x @ wv).reshape(B, S, n_kv, D_K).transpose(0, 2, 1, 3)
            k = jnp.repeat(k, groups, axis=1)
            v = jnp.repeat(v, groups, axis=1)
            scores = jnp.einsum('bhqd,bhkd->bhqk', q, k) / jnp.sqrt(jnp.float32(D_K))
            attn = jax.nn.softmax(scores, axis=-1)
            out = jnp.einsum('bhqk,bhkd->bhqd', attn, v)
            out = out.transpose(0, 2, 1, 3).reshape(B, S, D_MODEL)
            return out @ wo
        routing_input = x.mean(axis=1)
        logits = jax.nn.relu(routing_input @ r_w1 + r_b1) @ r_w2 + r_b2
        sel = jnp.argmax(jax.nn.softmax(logits, axis=-1), axis=-1)
        params = [(wq0, wk0, wv0, wo0), (wq1, wk1, wv1, wo1), (wq2, wk2, wv2, wo2)]
        out = jnp.zeros_like(x)
        for i, nkv in enumerate(KV_OPTS):
            yi = gqa(x, *params[i], nkv)
            mask = (sel == i)[:, None, None]
            out = jnp.where(mask, yi, out)
        return out

    def _L1_gnn_ref(x, batch, edge_index, norm1_g, norm1_b, norm2_g, norm2_b, W_conv, b_conv, Wq, Wk, Wv, Wo, proj):
        import jax, jax.numpy as jnp
        import numpy as np
        B = 32
        MAXN = 64
        HEADS = 8
        DH = 64
        M = 256
        D = 512
        EPS = 1e-05
        KEPS = 1e-06

        def _batchnorm(x, g, b):
            mu = jnp.mean(x, axis=0)
            var = jnp.mean((x - mu) ** 2, axis=0)
            return (x - mu) * jax.lax.rsqrt(var + EPS) * g + b

        def _forward(x, batch, edge_index, norm1_g, norm1_b, norm2_g, norm2_b, W_conv, b_conv, Wq, Wk, Wv, Wo, proj):
            N = x.shape[0]
            E = edge_index.shape[1]
            h = x
            xn = _batchnorm(x, norm1_g, norm1_b)
            msg = xn[edge_index[0]]
            agg = jax.ops.segment_sum(msg, edge_index[1], num_segments=N)
            deg = jax.ops.segment_sum(jnp.ones((E,), x.dtype), edge_index[1], num_segments=N)
            agg = agg / jnp.maximum(deg, 1.0)[:, None]
            conv_out = jax.nn.relu(agg @ W_conv + b_conv)
            counts = jax.ops.segment_sum(jnp.ones((N,), jnp.int32), batch, num_segments=B)
            offsets = jnp.concatenate([jnp.zeros((1,), jnp.int32), jnp.cumsum(counts)[:-1]])
            pos = jnp.arange(N, dtype=jnp.int32) - offsets[batch]
            h_dense = jnp.zeros((B, MAXN, D), x.dtype).at[batch, pos].set(h)
            mask = jnp.zeros((B, MAXN), bool).at[batch, pos].set(True)

            def heads(t, W):
                return (t @ W).reshape(B, MAXN, HEADS, DH).transpose(0, 2, 1, 3)
            q, k, v = (heads(h_dense, Wq), heads(h_dense, Wk), heads(h_dense, Wv))
            scale = DH ** (-0.25)

            def phi(t, is_query):
                t = t * scale
                u = jnp.einsum('bhnd,md->bhnm', t, proj)
                diag = 0.5 * jnp.sum(t * t, axis=-1, keepdims=True)
                if is_query:
                    m_ = jnp.max(u, axis=-1, keepdims=True)
                else:
                    m_ = jnp.max(u, axis=(-2, -1), keepdims=True)
                return jnp.exp(u - diag - jax.lax.stop_gradient(m_)) / np.sqrt(M) + KEPS
            qf = phi(q, True)
            kf = phi(k, False) * mask[:, None, :, None]
            vm = v * mask[:, None, :, None]
            kv = jnp.einsum('bhnm,bhnd->bhmd', kf, vm)
            z = 1.0 / (jnp.einsum('bhnm,bhm->bhn', qf, kf.sum(axis=2)) + KEPS)
            attn = jnp.einsum('bhnm,bhmd->bhnd', qf, kv) * z[..., None]
            attn = attn.transpose(0, 2, 1, 3).reshape(B, MAXN, D) @ Wo
            h_attn = attn[batch, pos]
            return _batchnorm(conv_out + h_attn + h, norm2_g, norm2_b)
        return _forward(x, batch, edge_index, norm1_g, norm1_b, norm2_g, norm2_b, W_conv, b_conv, Wq, Wk, Wv, Wo, proj)

    def _L1_ffn_ref(x, w_q, keys, weight_down_embed, weight_up_embed):
        import jax, jax.numpy as jnp
        import numpy as np
        DIM = 512
        HEADS = 8
        DIM_KEY = 32
        NUM_EXPERTS = 2048
        NUM_KEYS = 256
        TOPK = 16
        BN_EPS = 1e-05

        def peer_forward(x, w_q, keys, weight_down_embed, weight_up_embed):
            b, n, _ = x.shape
            q = x @ w_q * (1.0 / np.sqrt(1.0 + BN_EPS))
            queries = q.reshape(b, n, 2, HEADS, DIM_KEY).transpose(2, 0, 1, 3, 4)
            sim = jnp.einsum('pbnhd,hkpd->pbnhk', queries, keys)
            v0, i0 = jax.lax.top_k(sim[0], TOPK)
            v1, i1 = jax.lax.top_k(sim[1], TOPK)
            all_scores = v0[..., :, None] + i0[..., None, :].astype(v0.dtype)
            all_scores = all_scores.reshape(*all_scores.shape[:-2], -1)
            scores, pk_indices = jax.lax.top_k(all_scores, TOPK)
            weights_down = jnp.take(weight_down_embed, pk_indices, axis=0)
            weights_up = jnp.take(weight_up_embed, pk_indices, axis=0)
            h = jnp.einsum('bnd,bnhkd->bnhk', q, weights_down)
            h = jax.nn.gelu(h)
            h = h * jax.nn.softmax(scores, axis=-1)
            out = jnp.einsum('bnhk,bnhkd->bnd', h, weights_up)
            return out
        return peer_forward(x, w_q, keys, weight_down_embed, weight_up_embed)

    def _L2_gnn_ref(x, edge_index, virt_h, virt_edge_index, Wq, Wk, Wv, bn_gamma, bn_beta):
        import jax, jax.numpy as jnp
        import numpy as np
        N_NODES = 1250
        N_EDGES = 20000
        DIM_H = 512
        N_HEADS = 8
        D_HEAD = DIM_H // N_HEADS

        def _exphormer_attn(x, edge_index, Wq, Wk, Wv):
            N, D = x.shape
            H, d = (N_HEADS, D_HEAD)
            Q = (x @ Wq).reshape(N, H, d)
            K = (x @ Wk).reshape(N, H, d)
            V = (x @ Wv).reshape(N, H, d)
            src, dst = (edge_index[0], edge_index[1])
            scale = np.float32(1.0 / np.sqrt(d))
            score = jnp.einsum('ehd,ehd->eh', K[src], Q[dst]) * scale
            score = jnp.exp(jnp.clip(score, -5.0, 5.0))[..., None]
            msg = V[src] * score
            wV = jax.ops.segment_sum(msg, dst, num_segments=N)
            Z = jax.ops.segment_sum(score, dst, num_segments=N)
            return (wV / (Z + 1e-06)).reshape(N, D)
        h_attn = _exphormer_attn(x, edge_index, Wq, Wk, Wv)
        h = x + h_attn
        mean = jnp.mean(h, axis=0)
        var = jnp.mean(jnp.square(h - mean), axis=0)
        return (h - mean) * jax.lax.rsqrt(var + 1e-05) * bn_gamma + bn_beta

    def _L2_ffn_ref(x, gate_Wk, gate_bk, expert_queries, Wqkv, bqkv, Wo, bo, g1, be1, W1, bf1, W2, bf2, g2, be2):
        import jax, jax.numpy as jnp
        import numpy as np
        B, S, D, F, E, K, H = (4, 1024, 512, 64, 8, 2, 8)
        HEAD_DIM = D // H

        def _layernorm(x, g, b):
            m = x.mean(-1, keepdims=True)
            v = ((x - m) ** 2).mean(-1, keepdims=True)
            return (x - m) * jax.lax.rsqrt(v + 1e-05) * g + b

        def _expert(x, Wqkv, bqkv, Wo, bo, g1, be1, W1, bf1, W2, bf2, g2, be2):
            b, s, d = x.shape
            qkv = x @ Wqkv.T + bqkv
            q, k, v = jnp.split(qkv, 3, axis=-1)
            to_heads = lambda t: t.reshape(b, s, H, HEAD_DIM).transpose(0, 2, 1, 3)
            q, k, v = (to_heads(q), to_heads(k), to_heads(v))
            scale = 1.0 / np.sqrt(HEAD_DIM).astype(np.float32)
            attn = jax.nn.softmax(jnp.einsum('bhqd,bhkd->bhqk', q * scale, k), axis=-1)
            ctx = jnp.einsum('bhqk,bhkd->bhqd', attn, v).transpose(0, 2, 1, 3).reshape(b, s, d)
            ctx = ctx @ Wo.T + bo
            x = _layernorm(x + ctx, g1, be1)
            h = jax.nn.gelu(x @ W1.T + bf1, approximate=False)
            h = jax.nn.gelu(h @ W2.T + bf2, approximate=False)
            return _layernorm(x + h, g2, be2)
        keys = x @ gate_Wk.T + gate_bk
        scores = jnp.einsum('bsd,ed->bse', keys, expert_queries) * D ** (-0.5)
        probs = jax.nn.softmax(scores, axis=-1)
        _, idx = jax.lax.top_k(probs, K)
        mask = jax.nn.one_hot(idx, E, dtype=probs.dtype).sum(-2)
        gated = probs * mask
        gated = gated / (gated.sum(-1, keepdims=True) + 1e-09)
        eo = jax.vmap(_expert, in_axes=(None,) + (0,) * 12)(x, Wqkv, bqkv, Wo, bo, g1, be1, W1, bf1, W2, bf2, g2, be2)
        return jnp.einsum('ebsd,bse->bsd', eo, gated)

    def _L3_gnn_ref(x, edge_index, W1, b1, W2, b2, W3, b3):
        import jax, jax.numpy as jnp
        import numpy as np
        N = 10000
        E = 5000
        IN = 512
        HID = 512
        OUT = 512

        def _gcn_norm(edge_index, n):
            loops = jnp.arange(n, dtype=edge_index.dtype)
            row = jnp.concatenate([edge_index[0], loops])
            col = jnp.concatenate([edge_index[1], loops])
            deg = jax.ops.segment_sum(jnp.ones_like(col, jnp.float32), col, num_segments=n)
            dis = jnp.where(deg > 0, jax.lax.rsqrt(jnp.maximum(deg, 1.0)), 0.0)
            norm = dis[row] * dis[col]
            return (row, col, norm)

        def _gcn_layer(x, row, col, norm, W, b, n):
            h = x @ W
            msg = h[row] * norm[:, None]
            out = jax.ops.segment_sum(msg, col, num_segments=n)
            return out + b
        n = x.shape[0]
        row, col, norm = _gcn_norm(edge_index, n)
        h = _gcn_layer(x, row, col, norm, W1, b1, n)
        h = jax.nn.relu(h)
        h = _gcn_layer(h, row, col, norm, W2, b2, n)
        h = jax.nn.relu(h)
        h = _gcn_layer(h, row, col, norm, W3, b3, n)
        return h

    def _L3_ffn_ref(x, router_w, router_b, Wi, Wh, b, Wo, bo):
        import jax, jax.numpy as jnp
        import numpy as np
        S, B, I, O, H, E, K = (128, 32, 512, 512, 512, 8, 2)

        def _expert(x_seq, Wi, Wh, b, Wo, bo):
            Bsz = x_seq.shape[1]
            Hd = Wh.shape[0]

            def step(carry, xt):
                h, c = carry
                gates = xt @ Wi + h @ Wh + b
                i_, f_, g_, o_ = jnp.split(gates, 4, axis=-1)
                c = jax.nn.sigmoid(f_) * c + jax.nn.sigmoid(i_) * jnp.tanh(g_)
                h = jax.nn.sigmoid(o_) * jnp.tanh(c)
                return ((h, c), h @ Wo + bo)
            init = (jnp.zeros((Bsz, Hd), x_seq.dtype), jnp.zeros((Bsz, Hd), x_seq.dtype))
            _, ys = jax.lax.scan(step, init, x_seq)
            return ys
        S_, B_, I_ = x.shape
        N = S_ * B_
        flat_x = x.reshape(N, I_)
        logits = flat_x @ router_w + router_b
        top_vals, top_idx = jax.lax.top_k(logits, K)
        rw = jax.nn.softmax(top_vals, axis=1)
        mask = (top_idx.T[:, None, :] == jnp.arange(E)[None, :, None]).astype(x.dtype)
        expert_x = (mask[..., None] * flat_x[None, None]).reshape(K, E, S_, B_, I_)
        run_e = jax.vmap(_expert, in_axes=(0, 0, 0, 0, 0, 0))
        run_ke = jax.vmap(run_e, in_axes=(0, None, None, None, None, None))
        out = run_ke(expert_x, Wi, Wh, b, Wo, bo)
        out = out.reshape(K, E, N, -1)
        y = jnp.einsum('ken,nk,keno->no', mask, rw, out)
        return y.reshape(S_, B_, -1)
    edge_index = jnp.stack([src, dst])
    batch0 = jnp.zeros((128,), jnp.int32)
    x = x + _L0_gnn_ref(_layernorm(x, axis=-1), edge_index, L0_gnn_W, L0_gnn_a)
    x = x + _L0_ffn_ref(_layernorm(x, axis=-1)[None], L0_ffn_r_w1, L0_ffn_r_b1, L0_ffn_r_w2, L0_ffn_r_b2, L0_ffn_wq0, L0_ffn_wk0, L0_ffn_wv0, L0_ffn_wo0, L0_ffn_wq1, L0_ffn_wk1, L0_ffn_wv1, L0_ffn_wo1, L0_ffn_wq2, L0_ffn_wk2, L0_ffn_wv2, L0_ffn_wo2)[0]
    x = x + _L1_gnn_ref(_layernorm(x, axis=-1), batch0, edge_index, L1_gnn_norm1_g, L1_gnn_norm1_b, L1_gnn_norm2_g, L1_gnn_norm2_b, L1_gnn_W_conv, L1_gnn_b_conv, L1_gnn_Wq, L1_gnn_Wk, L1_gnn_Wv, L1_gnn_Wo, L1_gnn_proj)
    x = x + _L1_ffn_ref(_layernorm(x, axis=-1)[None], L1_ffn_w_q, L1_ffn_keys, L1_ffn_weight_down_embed, L1_ffn_weight_up_embed)[0]
    x = x + _L2_gnn_ref(_layernorm(x, axis=-1), edge_index, L2_gnn_virt_h, L2_gnn_virt_edge_index, L2_gnn_Wq, L2_gnn_Wk, L2_gnn_Wv, L2_gnn_bn_gamma, L2_gnn_bn_beta)
    x = x + _L2_ffn_ref(_layernorm(x, axis=-1)[None], L2_ffn_gate_Wk, L2_ffn_gate_bk, L2_ffn_expert_queries, L2_ffn_Wqkv, L2_ffn_bqkv, L2_ffn_Wo, L2_ffn_bo, L2_ffn_g1, L2_ffn_be1, L2_ffn_W1, L2_ffn_bf1, L2_ffn_W2, L2_ffn_bf2, L2_ffn_g2, L2_ffn_be2)[0]
    x = x + _L3_gnn_ref(_layernorm(x, axis=-1), edge_index, L3_gnn_W1, L3_gnn_b1, L3_gnn_W2, L3_gnn_b2, L3_gnn_W3, L3_gnn_b3)
    x = x + _L3_ffn_ref(_layernorm(x, axis=-1)[None], L3_ffn_router_w, L3_ffn_router_b, L3_ffn_Wi, L3_ffn_Wh, L3_ffn_b, L3_ffn_Wo, L3_ffn_bo)[0]
    return x

_drawn_inputs = setup_inputs


def setup_inputs(seed=0):
    import zlib

    import numpy as np

    out = dict(_drawn_inputs(seed))
    spreads = {'L0_ffn_r_b1': (0.0, 0.1),
     'L0_ffn_r_b2': (0.0, 0.628),
     'L1_gnn_norm1_g': (1.0, 0.6),
     'L1_gnn_norm1_b': (0.0, 0.33),
     'L1_gnn_norm2_g': (1.0, 0.2),
     'L1_gnn_norm2_b': (0.0, 0.1),
     'L1_gnn_b_conv': (0.0, 0.38),
     'L2_gnn_bn_gamma': (1.0, 0.6),
     'L2_gnn_bn_beta': (0.0, 0.717),
     'L2_ffn_gate_bk': (0.0, 0.392),
     'L2_ffn_bqkv': (0.0, 0.8),
     'L2_ffn_bo': (0.0, 2.0),
     'L2_ffn_g1': (1.0, 0.6),
     'L2_ffn_be1': (0.0, 0.439),
     'L2_ffn_bf1': (0.0, 2.0),
     'L2_ffn_bf2': (0.0, 2.0),
     'L2_ffn_g2': (1.0, 0.6),
     'L2_ffn_be2': (0.0, 0.449),
     'L3_gnn_b1': (0.0, 0.8),
     'L3_gnn_b2': (0.0, 1.535),
     'L3_gnn_b3': (0.0, 0.892),
     'L3_ffn_router_b': (0.0, 0.8),
     'L3_ffn_b': (0.0, 2.0),
     'L3_ffn_bo': (0.0, 1.238)}
    factors = {'L0_gnn_W': 8.0,
     'L0_gnn_a': 8.0,
     'L0_ffn_r_w2': 5.685,
     'L0_ffn_wq2': 8.0,
     'L0_ffn_wk2': 8.0,
     'L0_ffn_wv2': 6.394,
     'L0_ffn_wo2': 8.0,
     'L1_ffn_w_q': 8.0,
     'L1_ffn_keys': 8.0,
     'L1_ffn_weight_down_embed': 8.0,
     'L1_ffn_weight_up_embed': 8.0,
     'L2_ffn_Wqkv': 8.0,
     'L2_ffn_Wo': 6.455,
     'L2_ffn_W1': 8.0,
     'L2_ffn_W2': 8.0,
     'L3_gnn_W1': 8.0,
     'L3_gnn_W2': 3.21,
     'L3_ffn_router_w': 3.362,
     'L3_ffn_Wi': 7.193,
     'L3_ffn_Wo': 7.061}
    for name, (base, spread) in spreads.items():
        noise = np.random.default_rng([zlib.crc32(name.encode()), seed]).standard_normal(out[name].shape)
        drawn = base * np.exp(spread * noise) if base else spread * noise
        out[name] = jnp.asarray(drawn.astype(out[name].dtype))
    for name, factor in factors.items():
        out[name] = (out[name] * factor).astype(out[name].dtype)
    return out
```

```python
from contextlib import ExitStack

import concourse.bass as bass
from concourse import mybir

F32 = mybir.dt.float32
BF16 = mybir.dt.bfloat16
I32 = mybir.dt.int32
U32 = mybir.dt.uint32
ALU = mybir.AluOpType
ACT = mybir.ActivationFunctionType
AX = mybir.AxisListType

P = 128
D = 512
CH = D // P
H = 8
DH = D // H
EDGES_PER_PARTITION = 2176 // P
EPS = 1e-5
SUBLAYERS = 8

PERF_N = 64
PERF_M = 256
PERF_EPS = 1e-6
KEYS = 256
TOPK = 16
PICKS = TOPK * TOPK
E = 8
F2 = 64
NEG = -3.0e38
GAT_NEG = -9000000000000000.0

BV, BO, G1, BE1, G2 = range(5)
N1G, N1B, N2G, N2B, BCONV, BNG, BNB, GATEB, GCNB1, GCNB2 = range(10)

DENSE_USED = {
    "l0_W": ("gat_h_projected", 1),
    "wq0": ("gqa_q_projected", 1), "wk0": ("gqa_k_projected", 1), "wv0": ("gqa_v_projected", 1),
    "wq1": ("gqa_q_projected", 2), "wkv1": ("gqa_v_projected", 2), "wo0": ("gqa_o_projected", 1),
    "wq2": ("gqa_q_projected", 3), "wkv2": ("gqa_v_projected", 3), "wo1": ("gqa_o_projected", 2),
    "wo2": ("gqa_o_projected", 3),
    "perf_wq": ("perf_qk_projected", 1), "perf_wk": ("perf_qk_projected", 1), "perf_wv": ("perf_v_projected", 1),
    "conv": ("conv_h_projected", 1), "perf_wo": ("perf_o_projected", 1),
    "peer_wq": ("peer_q_projected", 1), "peer_tables": ("peer_up_projected", 1),
    "exph_wq": ("exph_q_projected", 1), "exph_wk": ("exph_k_projected", 1), "exph_wv": ("exph_v_projected", 1),
    "gate_wk": ("gate_keys_projected", 1),
    "gcn_w1": ("gcn_h_projected", 1), "gcn_w2": ("gcn_h_projected", 2), "gcn_w3": ("gcn_h_projected", 3),
}
DENSE = list(DENSE_USED)
SLOTS = 6


STEPS = {
    "gat_tensor_steps": [("edges_counted", 1), ("gat_h_projected", 1), ("degrees_summed", 1), ("gat_s_transposed", 1),
                         ("gat_scored", 1), ("gat_prob_transposed", 2), ("gat_attended", 1)],
    "gat_vector_steps": [("one_hot_ready", 2), ("counts_ready", 2), ("gat_s_ready", 2), ("gat_a_used", 1),
                         ("gcn_deg_ready", 1), ("gat_lr_ready", 2), ("mean_sd_ready", 1), ("gat_max_ready", 1),
                         ("gat_prob_t_ready0", 1), ("gat_out_ready", 1), ("gcn_sd_ready", 1)],
    "gat_scalar_steps": [("gat_h_ready", 1), ("gat_leak_ready", 2), ("gat_prob_ready", 8), ("gat_prob_t_ready1", 1),
                         ("gat_exp_ready", 1), ("route_exp_ready", 1)],
    "route_tensor_steps": [("route_hidden_summed", 1), ("route_logits_summed", 1)],
    "route_vector_steps": [("route_mean_ready", 1), ("route_hidden_ready", 1), ("route_logits_ready", 1)],
    "gps_tensor_steps": [("perf_qk_projected", 1), ("perf_v_projected", 1), ("conv_h_projected", 1), ("perf_u_ready", 2),
                         ("perf_diag_summed", 1), ("conv_mixed", 1), ("perf_kmax_transposed", 1),
                         ("perf_kmax_spread", 1), ("perf_kv_done", 1), ("perf_q_transposed", 1), ("perf_attended", 1),
                         ("perf_ctx_transposed", 1), ("perf_o_projected", 1), ("gps_out_transposed", 1)],
    "gps_vector_steps": [("v_free", 1), ("perf_rows_ready", 1), ("perf_t_scaled", 2), ("perf_sq_ready", 1),
                         ("perf_t_ready", 1), ("perf_bias_ready0", 1), ("perf_kmax_ready", 1),
                         ("perf_kmax_rows_ready", 1), ("perf_bias_ready1", 1), ("perf_features_ready", 2),
                         ("perf_kv_ready", 2), ("perf_q_t_ready0", 1), ("perf_ctx_ready", 1), ("perf_ctx_t_ready", 1)],
    "gps_scalar_steps": [("perf_v_ready", 1), ("conv_h_ready", 1), ("conv_t_ready", 1), ("perf_exp_ready", 2),
                         ("perf_kv_ready_act", 2), ("perf_q_t_ready1", 1)],
    "exph_tensor_steps": [("exph_q_projected", 1), ("exph_k_projected", 1), ("exph_scored", 2), ("exph_v_projected", 1),
                          ("exph_attended", 1), ("exph_h_transposed", 1), ("exph_out_transposed", 1),
                          ("gate_keys_projected", 1), ("gate_scored", 1), ("gated_transposed", 1), ("be2_shared", 1)],
    "exph_vector_steps": [("exph_k_ready", 1), ("exph_clipped", 2), ("exph_weights_ready", 2), ("exph_h_ready", 1),
                          ("gate_max_ready", 1), ("gated_ready", 1), ("gated_t_ready", 1), ("acc_ready", 1)],
    "exph_scalar_steps": [("exph_q_ready", 1), ("exph_v_ready", 1), ("exph_exp_ready", 2), ("gate_keys_ready", 1),
                          ("gate_exp_ready", 1), ("router_exp_ready", 1)],
    "router_tensor_steps": [("router_scored", 1), ("lstm_gated_transposed", 1), ("lstm_bo_shared", 1)],
    "router_vector_steps": [("lstm_hb_ready", 1), ("router_max_ready", 1), ("lstm_gated_ready", 1),
                            ("lstm_gated_t_ready", 1)],
}
STEP_BASE = {}
for _semaphore, _steps in STEPS.items():
    _n = 0
    for _step, _times in _steps:
        STEP_BASE[_step] = (_semaphore, _n)
        _n += _times


def build(nc, A, out):
    ctx = ExitStack()
    signals = {}

    def sig(name):
        name = STEP_BASE.get(name, (name, 0))[0]
        if name not in signals:
            signals[name] = ctx.enter_context(nc.semaphore(name))
        return signals[name]

    def at(name, value):
        return sig(name), STEP_BASE.get(name, (name, 0))[1] + value

    with ctx:
        def sb(name, shape, dt=F32):
            return ctx.enter_context(nc.sbuf_tensor(name, shape, dt))

        ps = ctx.enter_context(nc.psum_tensor("ps", [P, 8, 512], F32))

        dense = sb("dense", [P, SLOTS, CH * D])
        ew = sb("ew", [P, 2, 4 * CH * D])
        ew1 = sb("ew1", [P, 2, CH, F2])
        ew2 = sb("ew2", [F2 + 1, 2, D])
        erows = sb("erows", [P, 2, 5, D])
        r_w1 = erows[:, 1, 0, :].rearrange("p (c n) -> p c n", c=CH)
        r_w2 = sb("r_w2", [P, 3])
        r_b1 = sb("r_b1", [P, 1])
        r_b2 = sb("r_b2", [P, 3])
        attn_a = erows[:, 0, 0:2, :]
        cols = sb("cols", [P, 10, CH])
        proj_t = sb("proj_t", [P, PERF_M])
        keys_t = sb("keys_t", [P, 2, KEYS])
        bqk = sb("bqk", [P, E * 8])
        bf1 = sb("bf1", [F2, E])
        eq_t = sb("eq_t", [P, CH, E])
        be2 = sb("be2", [E, D])
        gcn_b3 = sb("gcn_b3", [P, D])
        router_w = sb("router_w", [P, CH, E])
        router_b = sb("router_b", [P, E])
        lstm_b = sb("lstm_b", [P, E * 16])
        lstm_hb = sb("lstm_hb", [P, E * 16])
        lstm_bo = sb("lstm_bo", [E, D])

        ident = sb("ident", [P, P])
        iota_i = sb("iota_i", [P, P], I32)
        iota_f = sb("iota_f", [P, P])
        minus_half = sb("minus_half", [P, P])
        ones = sb("ones", [P, P])

        src_i = sb("src_i", [P, EDGES_PER_PARTITION], I32)
        dst_i = sb("dst_i", [P, EDGES_PER_PARTITION], I32)
        src_f = sb("src_f", [P, EDGES_PER_PARTITION])
        dst_f = sb("dst_f", [P, EDGES_PER_PARTITION])
        one_hot = ew[:, 1, 0:EDGES_PER_PARTITION * P].bitcast(BF16).rearrange("p (a t n) -> p a t n", a=2, n=P)
        cnt_sd = sb("cnt_sd", [P, P])
        cnt_ds = sb("cnt_ds", [P, P])
        gat_cap = sb("gat_cap", [P, P])
        mean_sd = sb("mean_sd", [P, P])
        gcn_sd = sb("gcn_sd", [P, P])
        deg = sb("deg", [P, P])
        deg_col = sb("deg_col", [P, 1])
        dis_col = sb("dis_col", [P, 1])

        x = sb("x", [P, D])
        y = sb("y", [P, D])
        y_t = sb("y_t", [P, CH, P])
        z_t = sb("z_t", [P, CH, P])
        acc = sb("acc", [P, D])
        qk_t = sb("qk_t", [P, 2 * CH, P])
        v = sb("v", [P, H * (DH + 1)])
        prob_store = sb("prob_store", [P, 4 * 4 * (DH + 1)])
        prob = prob_store[:, 0:H * P].rearrange("p (h n) -> p h n", h=H)
        prob_t = sb("prob_t", [P, H, P])
        ctxv = sb("ctxv", [P, D])
        ctx_t = sb("ctx_t", [P, CH, P])
        t1 = sb("t1", [P, D])
        x1 = sb("x1", [P, D])
        x1_t = sb("x1_t", [P, CH, P])
        h1_t = sb("h1_t", [F2 + 1, P])
        h2 = sb("h2", [P, D])
        big = sb("big", [P, 2 * H * P])

        ln_st = sb("ln_st", [P, 6])
        ln_mv = sb("ln_mv", [P, 2])
        ln_var = sb("ln_var", [P, 1])
        ln_rstd = sb("ln_rstd", [P, 1])
        bn_st = sb("bn_st", [P, CH, 6])
        bn_mv = sb("bn_mv", [P, CH, 2])
        bn_var = sb("bn_var", [P, CH])
        bn_rstd = sb("bn_rstd", [P, CH])
        bn_scale = sb("bn_scale", [P, CH])
        bn_shift = sb("bn_shift", [P, CH])
        nmax = sb("nmax", [P, H])
        nmax_s = sb("nmax_s", [P, H])
        rsum = sb("rsum", [P, H])
        rinv = sb("rinv", [P, H])
        s_cat = sb("s_cat", [P, 40])
        gat_l = sb("gat_l", [40, P])
        gat_r = sb("gat_r", [40, H, P])
        r_mean = sb("r_mean", [P, CH])
        r_hcol = sb("r_hcol", [P, 1])
        r_h = sb("r_h", [P, P])
        r_p = sb("r_p", [P, 8])
        r_mask = sb("r_mask", [P, 4])
        small = sb("small", [P, 32])
        perf_r = sb("perf_r", [4, 2, PERF_N])
        perf_k2 = sb("perf_k2", [4, 2])
        topv = sb("topv", [P, 2, TOPK])
        topi = sb("topi", [P, 2, TOPK], U32)
        topif = sb("topif", [P, 2, TOPK])
        best = sb("best", [P, 2, TOPK])
        negbest = sb("negbest", [P, 2])
        picksum = sb("picksum", [P, H])
        pickinv = sb("pickinv", [P, H])
        gate8 = sb("gate8", [P, E])
        gated = sb("gated", [P, E])
        gidx = sb("gidx", [P, 8], U32)
        gidxf = sb("gidxf", [P, 8])
        gtop = sb("gtop", [P, 8])
        gated_t = sb("gated_t", [E, P])
        rg = sb("rg", [P, 1])

        def l2_wqk(u):
            return ew[:, u, 0:2 * CH * D].rearrange("p (c n) -> p c n", c=CH)

        def l2_wv(u):
            return ew[:, u, 2 * CH * D:3 * CH * D].rearrange("p (c n) -> p c n", c=CH)

        def wo_of(u):
            return ew[:, u, 3 * CH * D:4 * CH * D].rearrange("p (c n) -> p c n", c=CH)

        def l3_wi(u):
            return ew[:, u, 0:CH * D].rearrange("p (c n) -> p c n", c=CH)

        def l3_wgo(u):
            return ew[:, u, CH * D:3 * CH * D].rearrange("p (c n) -> p c n", c=CH)

        two_part = {"wkv1", "wkv2", "peer_tables"}
        landed, so_far = {}, [0] * SLOTS
        for n, name in enumerate(DENSE):
            so_far[n % SLOTS] += 32 if name in two_part else 16
            landed[name] = so_far[n % SLOTS]

        def slot(name):
            return dense[:, DENSE.index(name) % SLOTS, :]

        def matrix(name, n=D):
            return slot(name)[:, 0:CH * n].rearrange("p (c n) -> p c n", c=CH)

        def kv_matrices(name, n):
            return (slot(name)[:, 0:CH * n].rearrange("p (c n) -> p c n", c=CH),
                    slot(name)[:, CH * n:2 * CH * n].rearrange("p (c n) -> p c n", c=CH))

        peer_down = slot("peer_tables")[:, 0:CH * PICKS].rearrange("p (c n) -> p c n", c=CH)
        peer_up = slot("peer_tables")[:, CH * PICKS:CH * PICKS + 2 * D].rearrange("p (c n) -> p c n", c=2)

        heads_v = v[:, :].rearrange("p (h e) -> p h e", h=H)
        hd = ctxv[:, :].rearrange("p (g a d) -> p g a d", g=4, a=2)
        deg_rec = t1[:, 0:P]
        peer_work = t1[:, 0:PICKS]
        wide = big[:, :].rearrange("p (a n) -> p a n", a=2)
        kv_sb = prob_store[:, :].rearrange("p (b n) -> p b n", b=4)
        peer_all, peer_exp, peer_rest, peer_pick = (
            big[:, 2 * k * PICKS:2 * (k + 1) * PICKS].rearrange("p (b n) -> p b n", b=2) for k in range(4))
        h_t = (ctx_t, x1_t)

        def bank(b):
            return ps[:, b, :]

        def bank_heads(b):
            return ps[:, b, :].rearrange("p (h d) -> p h d", h=H)

        def bank_chunks(b):
            return ps[:, b, :].rearrange("p (c n) -> p c n", c=CH)

        block = ctx.enter_context(nc.Block())

        @block.sync
        def _(sp):
            def load_dense(name):
                n = DENSE.index(name)
                if n >= SLOTS:
                    done, value = DENSE_USED[DENSE[n - SLOTS]]
                    sp.wait_ge(*at(done, value))
                s = sig(f"dense_landed{n % SLOTS}")
                if name in ("wkv1", "wkv2"):
                    k, vv = kv_matrices(name, 256 if name == "wkv1" else 64)
                    sp.dma_start(k, A["wk" + name[-1]]).then_inc(s, 16)
                    sp.dma_start(vv, A["wv" + name[-1]]).then_inc(s, 16)
                elif name == "peer_tables":
                    sp.dma_start(peer_down, A["peer_down"][:, :, 0:PICKS]).then_inc(s, 16)
                    sp.dma_start(peer_up, A["peer_up"][0:PICKS, :].rearrange("(c p) n -> p c n", p=P)).then_inc(s, 16)
                else:
                    sp.dma_start(slot(name), A[name].rearrange("p c n -> p (c n)")).then_inc(s, 16)

            def load_l2(e, u):
                sp.dma_start(l2_wqk(u), A["l2_wqk"][e]).then_inc(sig(f"l2_wqk_landed{u}"), 16)
                sp.dma_start(l2_wv(u), A["l2_wv"][e]).then_inc(sig(f"l2_wv_landed{u}"), 16)
                sp.dma_start(wo_of(u), A["l2_wo"][e]).then_inc(sig(f"l2_wo_landed{u}"), 16)

            def load_l2_small(e, u):
                sp.dma_start(ew1[:, u], A["l2_w1"][e]).then_inc(sig(f"l2_small_landed{u}"), 16)
                sp.dma_start(ew2[:, u], A["l2_w2"][e]).then_inc(sig(f"l2_small_landed{u}"), 16)
                sp.dma_start(erows[:, u], A["l2_rows"][e].rearrange("(a r) n -> a r n", a=1)
                             .broadcast_to([P, 5, D])).then_inc(sig(f"l2_rows_landed{u}"), 16)

            def load_l3(e, u):
                sp.dma_start(l3_wi(u), A["l3_wi"][e][:, :, 0:D]).then_inc(sig(f"l3_wi_landed{u}"), 16)
                sp.dma_start(l3_wgo(u), A["l3_wi"][e][:, :, 2 * D:4 * D]).then_inc(sig(f"l3_wgo_landed{u}"), 16)
                sp.dma_start(wo_of(u), A["l3_wo"][e]).then_inc(sig(f"l3_wo_landed{u}"), 16)

            sp.dma_start(x[:], A["x"]).then_inc(sig("x_landed"), 16)
            sp.dma_start(attn_a, A["gat_a"].rearrange("(a r) n -> a r n", a=1).broadcast_to([P, 2, D])) \
                .then_inc(sig("gat_a_landed"), 16)
            for name in DENSE[:SLOTS]:
                load_dense(name)
            sp.wait_ge(*at("gat_a_used", 1))
            for name in DENSE[SLOTS:20]:
                load_dense(name)
            sp.wait_ge(*at("edges_counted", 1))
            sp.wait_ge(*at("route_hidden_summed", 1))
            for u in range(2):
                load_l2(u, u)
                load_l2_small(u, u)
            for name in DENSE[20:]:
                load_dense(name)
            with sp.Fori(1, E // 2) as i:
                for u in range(2):
                    n = i * 2 + u
                    sp.wait_ge(*at("l2_qk_projected", n * 2 - 2))
                    sp.dma_start(l2_wqk(u), A["l2_wqk"][n]).then_inc(sig(f"l2_wqk_landed{u}"), 16)
                    sp.wait_ge(*at("l2_v_projected", n - 1))
                    sp.dma_start(l2_wv(u), A["l2_wv"][n]).then_inc(sig(f"l2_wv_landed{u}"), 16)
                    sp.wait_ge(*at("l2_o_projected", n - 1))
                    sp.dma_start(wo_of(u), A["l2_wo"][n]).then_inc(sig(f"l2_wo_landed{u}"), 16)
                    sp.wait_ge(*at("l2_h2_projected", n - 1))
                    sp.dma_start(ew1[:, u], A["l2_w1"][n]).then_inc(sig(f"l2_small_landed{u}"), 16)
                    sp.dma_start(ew2[:, u], A["l2_w2"][n]).then_inc(sig(f"l2_small_landed{u}"), 16)
                    sp.wait_ge(*at("l2_expert_added", n - 1))
                    sp.dma_start(erows[:, u], A["l2_rows"][n].rearrange("(a r) n -> a r n", a=1)
                                 .broadcast_to([P, 5, D])).then_inc(sig(f"l2_rows_landed{u}"), 16)
            for u in range(2):
                sp.wait_ge(*at("l2_qk_projected", 2 * (E - 1 + u)))
                sp.wait_ge(*at("l2_v_projected", E - 1 + u))
                sp.wait_ge(*at("l2_o_projected", E - 1 + u))
                load_l3(u, u)
            with sp.Fori(1, E // 2) as i:
                for u in range(2):
                    n = i * 2 + u
                    sp.wait_ge(*at("l3_gates_projected", n * 3 - 3))
                    sp.dma_start(l3_wi(u), A["l3_wi"][n][:, :, 0:D]).then_inc(sig(f"l3_wi_landed{u}"), 16)
                    sp.dma_start(l3_wgo(u), A["l3_wi"][n][:, :, 2 * D:4 * D]).then_inc(sig(f"l3_wgo_landed{u}"), 16)
                    sp.wait_ge(*at("l3_o_projected", n - 1))
                    sp.dma_start(wo_of(u), A["l3_wo"][n]).then_inc(sig(f"l3_wo_landed{u}"), 16)
            for s, value in (("router_landed", 64), ("params_landed", 48), ("late_params_landed", 160)):
                sp.wait_ge(*at(s, value))
            sp.wait_ge(*at("x_updated", SUBLAYERS))
            sp.dma_start(out, x[:]).then_inc(sig("out_written"), 16)
            sp.wait_ge(*at("out_written", 16))

        @block.gpsimd
        def _(pool):
            pool.memset(ident[:], 0.0).then_inc(sig("pool_cleared"), 1)
            pool.memset(gat_r[:], 0.0).then_inc(sig("pool_cleared"), 1)
            pool.memset(minus_half[:], -0.5).then_inc(sig("const_ready"), 1)
            pool.memset(ones[:], 1.0).then_inc(sig("const_ready"), 1)
            pool.iota(iota_i[:], pattern=[[1, P]], base=0, channel_multiplier=0).then_inc(sig("iota_ready"), 1)
            pool.wait_ge(*at("pool_cleared", 2))
            pool.affine_select(out=ident[:], in_=ident[:], compare_op=ALU.not_equal, fill=1.0, base=0,
                               pattern=[[-1, P]], channel_multiplier=1).then_inc(sig("const_ready"), 1)
            pool.wait_ge(*at("const_ready", 3))
            for p0 in (0, 32):
                if p0:
                    pool.wait_ge(*at("gat_r_ready", 1))
                pool.affine_select(out=gat_r[p0:p0 + H], in_=gat_r[p0:p0 + H], compare_op=ALU.not_equal,
                                   fill=1.0, base=0, pattern=[[-1, H], [0, P]], channel_multiplier=1) \
                    .then_inc(sig("gat_r_ready"), 1)
            pool.wait_ge(*at("gat_r_ready", 2))

            def layer_norm_rstd(k):
                pool.wait_ge(*at("ln_var_ready", k + 1))
                pool.tensor_tensor(ln_rstd[:], ln_var[:], minus_half[:, 0:1], ALU.pow).then_inc(sig("ln_rstd_ready"), 1)

            def batch_norm_rstd(k):
                pool.wait_ge(*at("bn_var_ready", k + 1))
                pool.tensor_tensor(bn_rstd[:], bn_var[:], minus_half[:, 0:CH], ALU.pow).then_inc(sig("bn_rstd_ready"), 1)

            layer_norm_rstd(0)
            pool.wait_ge(*at("gcn_deg_ready", 1))
            pool.tensor_tensor(deg[:], deg[:], minus_half[:], ALU.pow).then_inc(sig("gcn_dis_ready"), 1)
            pool.tensor_tensor(dis_col[:], deg_col[:], minus_half[:, 0:1], ALU.pow).then_inc(sig("gcn_dis_ready"), 1)
            layer_norm_rstd(1)
            layer_norm_rstd(2)
            batch_norm_rstd(0)
            batch_norm_rstd(1)
            layer_norm_rstd(3)
            for h in range(H):
                pool.wait_ge(*at("peer_inv_ready", h + 1))
                if h >= 2:
                    pool.wait_ge(*at("peer_head_added", h - 1))
                pool.tensor_scalar(x1_t[:, h % 2, :], ident[:], pickinv[:, h:h + 1], None, ALU.mult) \
                    .then_inc(sig("peer_diag_ready"), 1)
            layer_norm_rstd(4)
            batch_norm_rstd(2)
            layer_norm_rstd(5)

            def residual_rows(n, rows_value, u):
                pool.wait_ge(*at(f"l2_rows_landed{u}", rows_value))
                pool.tensor_tensor(erows[:, u, BO, :], erows[:, u, BO, :], y[:], ALU.add) \
                    .then_inc(sig("l2_residual_ready"), 1)

            def inner_norms(n, first):
                pool.wait_ge(*at("l2_var_ready", n * 2 + first))
                pool.tensor_tensor(ln_rstd[:], ln_var[:], minus_half[:, 0:1], ALU.pow).then_inc(sig("l2_rstd_ready"), 1)

            pool.wait_ge(*at("y_ready", 6))
            residual_rows(0, 16, 0)
            with pool.Fori(0, E // 2 - 1) as i:
                for u in range(2):
                    inner_norms(i * 2 + u, 1)
                    residual_rows(i * 2 + u + 1, i * 16 + 16 * (u + 1), 1 - u)
                    inner_norms(i * 2 + u, 2)
            inner_norms(E - 2, 1)
            residual_rows(E - 1, 16 * (E // 2), 1)
            inner_norms(E - 2, 2)
            inner_norms(E - 1, 1)
            inner_norms(E - 1, 2)
            layer_norm_rstd(6)
            layer_norm_rstd(7)

        @block.scalar
        def _(act):
            for tile, name in ((src_i[:], "src"), (dst_i[:], "dst")):
                act.dma_start(tile, A[name]).then_inc(sig("edges_landed"), 16)
            for tile, name in ((r_w1[:], "r_w1"), (r_w2[:], "r_w2"), (r_b1[:], "r_b1")):
                act.dma_start(tile, A[name]).then_inc(sig("router_landed"), 16)
            act.dma_start(r_b2[:], A["r_b2"].broadcast_to([P, 3])).then_inc(sig("router_landed"), 16)
            act.dma_start(cols[:], A["cols"]).then_inc(sig("params_landed"), 16)
            act.dma_start(proj_t[0:DH], A["proj_t"]).then_inc(sig("params_landed"), 16)
            act.dma_start(proj_t[DH:P], A["proj_t"]).then_inc(sig("params_landed"), 16)
            for tile, name in ((keys_t[:], "keys_t"), (bqk[:], "bqk"), (bf1[:], "bf1"), (eq_t[:], "eq_t"),
                               (be2[:], "be2"), (router_w[:], "router_w"), (lstm_b[:], "lstm_b"),
                               (lstm_bo[:], "lstm_bo")):
                act.dma_start(tile, A[name][0] if name == "keys_t" else A[name]).then_inc(sig("late_params_landed"), 16)
            act.dma_start(gcn_b3[:], A["gcn_b3"].broadcast_to([P, D])).then_inc(sig("late_params_landed"), 16)
            act.dma_start(router_b[:], A["router_b"].broadcast_to([P, E])).then_inc(sig("late_params_landed"), 16)

            def layer_norm_t(k):
                act.wait_ge(*at("y_transposed", k + 1))
                nc.scalar.copy(y_t[:].rearrange("p c n -> p (c n)"), bank(7)).then_inc(sig("y_t_ready"), 1)

            def exps(scores_max, done, n, scale):
                for a in range(2):
                    act.wait_ge(*at(scores_max, n * 2 + (a + 1)))
                    for g in range(4):
                        s = 4 * a + g
                        last = nc.scalar.activation(prob[:, s, :], ps[:, 3 + a, g * P:(g + 1) * P], ACT.Exp,
                                                    bias=nmax_s[:, s:s + 1], scale=scale, accum_out=rsum[:, s:s + 1])
                    last.then_inc(sig(done), 1)

            layer_norm_t(0)
            act.wait_ge(*at("gat_h_projected", 1))
            act.wait_ge(*at("gat_s_ready", 1))
            nc.scalar.copy(v[:, 0:D], bank(0)).then_inc(sig("gat_h_ready"), 1)
            act.wait_ge(*at("gat_scored", 1))
            for a in range(2):
                nc.scalar.mul(wide[:, a, 0:512], ps[:, 3 + a, :], 0.2).then_inc(sig("gat_leak_ready"), 1)
            act.wait_ge(*at("gat_max_ready", 1))
            for h in range(H):
                nc.scalar.activation(prob[:, h, :], prob[:, h, :], ACT.Exp, bias=nmax[:, h:h + 1],
                                     accum_out=rsum[:, h:h + 1]).then_inc(sig("gat_prob_ready"), 1)
            act.wait_ge(*at("gat_prob_transposed", 2))
            nc.scalar.copy(prob_t[:, 4:8, :].rearrange("p h n -> p (h n)"), bank(6)).then_inc(sig("gat_prob_t_ready1"), 1)
            act.wait_ge(*at("gat_out_ready", 1))
            nc.scalar.activation(t1[:], ctxv[:], ACT.Exp, bias=small[:, 0:1], accum_out=small[:, 1:2]) \
                .then_inc(sig("gat_exp_ready"), 1)

            layer_norm_t(1)
            act.wait_ge(*at("route_logits_ready", 1))
            nc.scalar.activation(r_p[:, 0:3], r_p[:, 0:3], ACT.Exp, bias=small[:, 0:1], accum_out=small[:, 1:2]) \
                .then_inc(sig("route_exp_ready"), 1)
            for n in range(3):
                act.wait_ge(*at("gqa_q_projected", n + 1))
                nc.scalar.copy(qk_t[:, 0:CH, :].rearrange("p c n -> p (c n)"), bank(0)).then_inc(sig("gqa_q_ready"), 1)
                if n:
                    act.wait_ge(*at("gqa_prob_transposed", 2 * n))
                    nc.scalar.copy(prob_t[:, 4:8, :].rearrange("p h n -> p (h n)"), bank(7)) \
                        .then_inc(sig("gqa_prob_t_ready1"), 1)
                    act.wait_ge(*at("gqa_ctx_transposed", n))
                    nc.scalar.copy(ctx_t[:].rearrange("p c n -> p (c n)"), bank(4)).then_inc(sig("gqa_ctx_t_ready"), 1)
                exps("gqa_max_ready", "gqa_prob_ready", n, DH ** -0.5)
            act.wait_ge(*at("gqa_prob_transposed", 6))
            nc.scalar.copy(prob_t[:, 4:8, :].rearrange("p h n -> p (h n)"), bank(7)).then_inc(sig("gqa_prob_t_ready1"), 1)
            act.wait_ge(*at("gqa_ctx_transposed", 3))
            nc.scalar.copy(ctx_t[:].rearrange("p c n -> p (c n)"), bank(4)).then_inc(sig("gqa_ctx_t_ready"), 1)

            layer_norm_t(2)
            act.wait_ge(*at("perf_v_projected", 1))
            act.wait_ge(*at("v_free", 1))
            nc.scalar.copy(heads_v[:, :, 0:DH], bank_heads(1)).then_inc(sig("perf_v_ready"), 1)
            act.wait_ge(*at("conv_h_projected", 1))
            nc.scalar.copy(ctxv[:], bank(2)).then_inc(sig("conv_h_ready"), 1)
            act.wait_ge(*at("conv_mixed", 1))
            for c in range(CH):
                last = nc.scalar.activation(ctx_t[:, c, :], ps[:, 3, c * P:(c + 1) * P], ACT.Relu,
                                            bias=cols[:, BCONV, c:c + 1])
            last.then_inc(sig("conv_t_ready"), 1)
            for w in range(2):
                act.wait_ge(*at(f"perf_bias_ready{w}", 1))
                for g in range(4):
                    last = nc.scalar.activation(wide[:, w, g * PERF_M:(g + 1) * PERF_M],
                                                ps[:, 4 + 2 * w + g // 2, (g % 2) * PERF_M:(g % 2 + 1) * PERF_M],
                                                ACT.Exp, bias=small[:, 16 + 4 * w + g:17 + 4 * w + g])
                last.then_inc(sig("perf_exp_ready"), 1)
            act.wait_ge(*at("perf_kv_done", 1))
            for b in (1, 3):
                nc.scalar.copy(kv_sb[:, b, :], ps[:, b, 0:4 * (DH + 1)]).then_inc(sig("perf_kv_ready_act"), 1)
            act.wait_ge(*at("perf_q_transposed", 1))
            nc.scalar.copy(prob_t[:, 4:8, :].rearrange("p h n -> p (h n)"), bank(5)).then_inc(sig("perf_q_t_ready1"), 1)

            layer_norm_t(3)
            act.wait_ge(*at("peer_down_projected", 1))
            nc.scalar.activation(x1_t[:, 2:4, :].rearrange("p c n -> p (c n)"), ps[:, 5, 0:2 * P],
                                 ACT.Gelu_apprx_tanh).then_inc(sig("peer_gelu_ready"), 1)
            for h in range(H):
                act.wait_ge(*at("peer_best_ready", h + 1))
                if h >= 2:
                    act.wait_ge(*at("peer_masked", h - 1))
                nc.scalar.activation(peer_exp[:, h % 2, :], peer_all[:, h % 2, :], ACT.Exp,
                                     bias=negbest[:, h % 2:h % 2 + 1]).then_inc(sig("peer_exp_ready"), 1)

            layer_norm_t(4)
            act.wait_ge(*at("exph_q_projected", 1))
            nc.scalar.copy(qk_t[:, 0:CH, :].rearrange("p c n -> p (c n)"), bank(0)).then_inc(sig("exph_q_ready"), 1)
            act.wait_ge(*at("exph_v_projected", 1))
            nc.scalar.copy(heads_v[:, :, 0:DH], bank_heads(2)).then_inc(sig("exph_v_ready"), 1)
            for a in range(2):
                act.wait_ge(*at("exph_clipped", a + 1))
                nc.scalar.activation(prob[:, 4 * a:4 * a + 4, :], prob[:, 4 * a:4 * a + 4, :], ACT.Exp,
                                     scale=DH ** -0.5).then_inc(sig("exph_exp_ready"), 1)

            layer_norm_t(5)
            act.wait_ge(*at("gate_keys_projected", 1))
            for c in range(CH):
                last = nc.scalar.activation(z_t[:, c, :], ps[:, 0, c * P:(c + 1) * P], ACT.Identity,
                                            bias=cols[:, GATEB, c:c + 1])
            last.then_inc(sig("gate_keys_ready"), 1)
            act.wait_ge(*at("gate_max_ready", 1))
            nc.scalar.activation(gate8[:], ps[:, 5, 0:E], ACT.Exp, bias=small[:, 0:1], scale=D ** -0.5,
                                 accum_out=small[:, 1:2]).then_inc(sig("gate_exp_ready"), 1)

            def q_bias(n):
                act.wait_ge(*at("l2_qk_projected", n * 2 + 1))
                for c in range(CH):
                    last = nc.scalar.activation(qk_t[:, c, :], ps[:, 0, c * P:(c + 1) * P], ACT.Identity,
                                                bias=bqk[:, bass.ds(n * 8 + c, 1)])
                last.then_inc(sig("l2_q_ready"), 1)

            def expert_act(n, has_next):
                exps("l2_max_ready", "l2_prob_ready", n, DH ** -0.5)
                if has_next:
                    q_bias(n + 1)
                act.wait_ge(*at("l2_prob_transposed", n * 2 + 2))
                nc.scalar.copy(prob_t[:, 4:8, :].rearrange("p h n -> p (h n)"), bank(6)).then_inc(sig("l2_prob_t_ready1"), 1)
                act.wait_ge(*at("l2_ctx_transposed", n + 1))
                nc.scalar.copy(ctx_t[:].rearrange("p c n -> p (c n)"), bank(3)).then_inc(sig("l2_ctx_t_ready"), 1)
                act.wait_ge(*at("l2_x1_transposed", n + 1))
                nc.scalar.copy(x1_t[:].rearrange("p c n -> p (c n)"), bank(5)).then_inc(sig("l2_x1_t_ready"), 1)
                act.wait_ge(*at("l2_h1_projected", n + 1))
                nc.scalar.activation(h1_t[0:F2, :], ps[0:F2, 6, 0:P], ACT.Gelu, bias=bf1[:, bass.ds(n, 1)]) \
                    .then_inc(sig("l2_h1_ready"), 1)
                act.wait_ge(*at("l2_h2_projected", n + 1))
                nc.scalar.activation(h2[:], bank(7), ACT.Gelu).then_inc(sig("l2_h2_ready"), 1)

            act.sem_inc(sig("l2_h2_ready"), 1)
            q_bias(0)
            with act.Fori(0, E // 2 - 1) as i:
                for u in range(2):
                    expert_act(i * 2 + u, True)
            expert_act(E - 2, True)
            expert_act(E - 1, False)

            layer_norm_t(6)
            for k in range(3):
                act.wait_ge(*at("gcn_h_projected", k + 1))
                nc.scalar.copy(ctxv[:], bank(0)).then_inc(sig("gcn_h_ready"), 1)
                if k < 2:
                    act.wait_ge(*at("gcn_mixed", k + 1))
                    for c in range(CH):
                        last = nc.scalar.activation(z_t[:, c, :], ps[:, 1, c * P:(c + 1) * P], ACT.Relu,
                                                    bias=cols[:, GCNB1 + k, c:c + 1])
                    last.then_inc(sig("gcn_z_ready"), 1)

            layer_norm_t(7)
            act.wait_ge(*at("router_max_ready", 1))
            nc.scalar.activation(gate8[:], gated[:], ACT.Exp, bias=small[:, 0:1]).then_inc(sig("router_exp_ready"), 1)

            def lstm_act(n):
                for j, (tile, bias, scale, first) in enumerate((
                        (prob[:, 0:4, :], lstm_hb, 0.5, 0), (prob[:, 4:8, :], lstm_b, 1.0, 8),
                        (prob_t[:, 0:4, :], lstm_hb, 0.5, 12))):
                    act.wait_ge(*at("l3_gates_projected", n * 3 + (j + 1)))
                    if j == 2:
                        act.wait_ge(*at("l3_h_ready", n + 1))
                    for c in range(CH):
                        last = nc.scalar.activation(tile[:, c, :], ps[:, j, c * P:(c + 1) * P], ACT.Tanh,
                                                    bias=bias[:, bass.ds(n * 16 + (first + c), 1)], scale=scale)
                    last.then_inc(sig("l3_gate_ready"), 1)
                act.wait_ge(*at("l3_cell_ready", n + 1))
                nc.scalar.activation(prob_t[:, 4:8, :].rearrange("p c n -> p (c n)"), t1[:], ACT.Tanh, scale=0.5) \
                    .then_inc(sig("l3_cell_tanh_ready"), 1)

            with act.Fori(0, E) as n:
                lstm_act(n)

        @block.tensor
        def _(pe):
            def weights(name):
                pe.wait_ge(*at(f"dense_landed{DENSE.index(name) % SLOTS}", landed[name]))

            def layer_norm_transpose(k):
                pe.wait_ge(*at("y_ready", k + 1))
                for c in range(CH):
                    last = pe.transpose(ps[:, 7, c * P:(c + 1) * P], y[:, c * P:(c + 1) * P], ident[:])
                last.then_inc(sig("y_transposed"), 1)
                pe.wait_ge(*at("y_t_ready", k + 1))

            def project(b, in_t, w, n=D):
                for c in range(CH):
                    last = pe.matmul(ps[:, b, 0:n], in_t[:, c, :], w[:, c, 0:n], start=(c == 0), stop=(c == CH - 1))
                return last

            def project_t(b, in_t, w, chunks=CH, first=0, n=P):
                for m in range(chunks):
                    for c in range(CH):
                        last = pe.matmul(ps[:, b, m * n:(m + 1) * n], w[:, c, (first + m) * P:(first + m + 1) * P],
                                         in_t[:, c, 0:n], start=(c == 0), stop=(c == CH - 1))
                return last

            def scores(done, k_chunk):
                for a in range(2):
                    r = slice(DH * a, DH * a + DH)
                    for g in range(4):
                        last = pe.matmul(ps[:, 3 + a, g * P:(g + 1) * P], qk_t[r, g, :], qk_t[r, CH + k_chunk(g), :],
                                         start=True, stop=True)
                    last.then_inc(sig(done), 1)

            def transpose_probs(ready, done, n, banks):
                for a in range(2):
                    pe.wait_ge(*at(ready, n * 2 + (a + 1)))
                    for g in range(4):
                        last = pe.transpose(ps[:, banks[a], g * P:(g + 1) * P], prob[:, 4 * a + g, :], ident[:])
                    last.then_inc(sig(done), 1)

            def attend(b, ready0, ready1, n, v_head):
                for a in range(2):
                    pe.wait_ge(*at((ready0, ready1)[a], n + 1))
                    for g in range(4):
                        h = 2 * g + a
                        last = pe.matmul(ps[:, b, h * DH:(h + 1) * DH], prob_t[:, 4 * a + g, :], v_head(h),
                                         start=True, stop=True)
                return last

            def transpose_rows(b, rows):
                for c in range(CH):
                    last = pe.transpose(ps[:, b, c * P:(c + 1) * P], rows[:, c * P:(c + 1) * P], ident[:])
                return last

            pe.wait_ge(*at("const_ready", 3))
            pe.wait_ge(*at("one_hot_ready", 2))
            for b, (l, r) in ((5, (0, 1)), (6, (1, 0))):
                for t in range(EDGES_PER_PARTITION):
                    last = pe.matmul(ps[:, b, 0:P], one_hot[:, l, t, :], one_hot[:, r, t, :],
                                     start=(t == 0), stop=(t == EDGES_PER_PARTITION - 1))
            last.then_inc(sig("edges_counted"), 1)

            layer_norm_transpose(0)
            weights("l0_W")
            last = project(0, y_t, matrix("l0_W"))
            last.then_inc(sig("gat_h_projected"), 1)
            pe.wait_ge(*at("counts_ready", 2))
            pe.matmul(ps[:, 2, 0:P], ones[:], cnt_sd[:], start=True, stop=True).then_inc(sig("degrees_summed"), 1)
            pe.wait_ge(*at("gat_s_ready", 2))
            pe.transpose(ps[0:40, 1, 0:P], s_cat[:], ident[:]).then_inc(sig("gat_s_transposed"), 1)
            pe.wait_ge(*at("gat_lr_ready", 2))
            for a in range(2):
                last = pe.matmul(ps[:, 3 + a, :], gat_l[:], gat_r[:, 4 * a:4 * a + 4, :], start=True, stop=True)
            last.then_inc(sig("gat_scored"), 1)
            pe.wait_ge(*at("gat_prob_ready", 4))
            for h in range(H):
                if h >= 4:
                    pe.wait_ge(*at("gat_prob_ready", h + 1))
                last = pe.transpose(ps[:, 5 + h // 4, h % 4 * P:(h % 4 + 1) * P], prob[:, h, :], ident[:])
                if h % 4 == 3:
                    last.then_inc(sig("gat_prob_transposed"), 1)
            pe.wait_ge(*at("gat_h_ready", 1))
            for h in range(H):
                if h % 4 == 0:
                    pe.wait_ge(*at(f"gat_prob_t_ready{h // 4}", 1))
                last = pe.matmul(ps[:, 0, h * DH:(h + 1) * DH], prob_t[:, h, :], v[:, h * DH:(h + 1) * DH],
                                 start=True, stop=True)
            last.then_inc(sig("gat_attended"), 1)

            layer_norm_transpose(1)
            pe.wait_ge(*at("router_landed", 64))
            pe.wait_ge(*at("route_mean_ready", 1))
            for c in range(CH):
                last = pe.matmul(ps[:, 2, 0:1], r_w1[:, c, :], r_mean[:, c:c + 1], start=(c == 0), stop=(c == CH - 1))
            last.then_inc(sig("route_hidden_summed"), 1)
            kv_heads = (8, 4, 1)

            def project_qk(n):
                weights(f"wq{n}")
                if n:
                    pe.wait_ge(*at("gqa_q_ready", n))
                project_t(0, y_t, matrix(f"wq{n}")).then_inc(sig("gqa_q_projected"), 1)
                if n == 0:
                    weights("wk0")
                    last = project_t(1, y_t, matrix("wk0"))
                else:
                    weights(f"wkv{n}")
                    wk = kv_matrices(f"wkv{n}", kv_heads[n] * DH)[0]
                    for m in range(kv_heads[n]):
                        for a in range(2):
                            for c in range(CH):
                                last = pe.matmul(ps[DH * a:DH * a + DH, 1, m * P:(m + 1) * P],
                                                 wk[:, c, m * DH:(m + 1) * DH], y_t[:, c, :],
                                                 start=(c == 0), stop=(c == CH - 1))
                last.then_inc(sig("gqa_k_projected"), 1)

            def project_v(n):
                if n == 0:
                    weights("wv0")
                    last = project(2, y_t, matrix("wv0"))
                else:
                    last = project(2, y_t, kv_matrices(f"wkv{n}", kv_heads[n] * DH)[1], kv_heads[n] * DH)
                last.then_inc(sig("gqa_v_projected"), 1)

            project_qk(0)
            pe.wait_ge(*at("route_hidden_ready", 1))
            pe.matmul(ps[:, 5, 0:3], r_h[:], r_w2[:], start=True, stop=True).then_inc(sig("route_logits_summed"), 1)
            project_v(0)
            for n in range(3):
                pe.wait_ge(*at("gqa_q_ready", n + 1))
                pe.wait_ge(*at("gqa_k_ready", n + 1))
                scores("gqa_scored", (lambda g: g) if n < 2 else (lambda g: 0))
                if n < 2:
                    project_qk(n + 1)
                transpose_probs("gqa_prob_ready", "gqa_prob_transposed", n, (5, 7))
                pe.wait_ge(*at("gqa_v_ready", n + 1))
                group = H // kv_heads[n]
                attend(3, "gqa_prob_t_ready0", "gqa_prob_t_ready1", n,
                       lambda h: v[:, (h // group) * DH:(h // group + 1) * DH]).then_inc(sig("gqa_attended"), 1)
                if n < 2:
                    project_v(n + 1)
                pe.wait_ge(*at("gqa_ctx_ready", n + 1))
                transpose_rows(4, ctxv).then_inc(sig("gqa_ctx_transposed"), 1)
                pe.wait_ge(*at("gqa_ctx_t_ready", n + 1))
                weights(f"wo{n}")
                for c in range(CH):
                    last = pe.matmul(bank(6), ctx_t[:, c, :], matrix(f"wo{n}")[:, c, :],
                                     start=(n == 0 and c == 0), stop=(n == 2 and c == CH - 1))
                last.then_inc(sig("gqa_o_projected"), 1)

            layer_norm_transpose(2)
            weights("perf_wq")
            project_t(0, y_t, matrix("perf_wq"), n=PERF_N)
            weights("perf_wk")
            for m in range(CH):
                for c in range(CH):
                    last = pe.matmul(ps[:, 0, 256 + m * PERF_N:256 + (m + 1) * PERF_N],
                                     matrix("perf_wk")[:, c, m * P:(m + 1) * P], y_t[:, c, 0:PERF_N],
                                     start=(c == 0), stop=(c == CH - 1))
            last.then_inc(sig("perf_qk_projected"), 1)
            pe.wait_ge(*at("perf_rows_ready", 1))
            weights("perf_wv")
            project(1, x1_t, matrix("perf_wv")).then_inc(sig("perf_v_projected"), 1)
            pe.wait_ge(*at("bn_out_ready", 1))
            weights("conv")
            project(2, z_t, matrix("conv")).then_inc(sig("conv_h_projected"), 1)
            pe.wait_ge(*at("perf_t_ready", 1))
            pe.wait_ge(*at("params_landed", 48))
            for w in range(2):
                for g in range(4):
                    last = pe.matmul(ps[:, 4 + 2 * w + g // 2, (g % 2) * PERF_M:(g % 2 + 1) * PERF_M],
                                     qk_t[:, 4 * w + g, :], proj_t[:], start=True, stop=True)
                last.then_inc(sig("perf_u_ready"), 1)
            pe.wait_ge(*at("perf_sq_ready", 1))
            for s in range(8):
                last = pe.matmul(ps[:, 0, s:s + 1], prob[:, s, :], ones[:, 0:1], start=True, stop=True)
            last.then_inc(sig("perf_diag_summed"), 1)
            pe.wait_ge(*at("conv_h_ready", 1))
            pe.wait_ge(*at("mean_sd_ready", 1))
            for c in range(CH):
                last = pe.matmul(ps[:, 3, c * P:(c + 1) * P], ctxv[:, c * P:(c + 1) * P], mean_sd[:],
                                 start=True, stop=True)
            last.then_inc(sig("conv_mixed"), 1)
            pe.wait_ge(*at("perf_kmax_ready", 1))
            pe.transpose(ps[0:4, 0, P:2 * P], small[:, 4:8], ident[:]).then_inc(sig("perf_kmax_transposed"), 1)
            pe.wait_ge(*at("perf_kmax_rows_ready", 1))
            pe.matmul(ps[:, 0, 2 * P:2 * P + 4], perf_r[:].rearrange("g a n -> g (a n)"), ident[0:4, 0:4],
                      start=True, stop=True).then_inc(sig("perf_kmax_spread"), 1)
            pe.wait_ge(*at("perf_features_ready", 1))
            pe.wait_ge(*at("conv_t_ready", 1))
            pe.wait_ge(*at("perf_features_ready", 2))
            pe.wait_ge(*at("perf_v_ready", 1))
            for a in range(2):
                r = slice(DH * a, DH * a + DH)
                for m in range(2):
                    for g in range(4):
                        h = 2 * g + a
                        last = pe.matmul(ps[:, 2 * m + a, g * (DH + 1):(g + 1) * (DH + 1)],
                                         wide[r, 1, g * PERF_M + m * P:g * PERF_M + (m + 1) * P], heads_v[r, h, :],
                                         start=True, stop=True)
            last.then_inc(sig("perf_kv_done"), 1)
            for g in range(4):
                for m in range(2):
                    s = 2 * g + m
                    last = pe.transpose(ps[:, 4 + s // 4, s % 4 * P:(s % 4 + 1) * P],
                                        wide[:, 0, g * PERF_M + m * P:g * PERF_M + (m + 1) * P], ident[:])
            last.then_inc(sig("perf_q_transposed"), 1)
            pe.wait_ge(*at("perf_kv_ready", 2))
            pe.wait_ge(*at("perf_kv_ready_act", 2))
            pe.wait_ge(*at("perf_q_t_ready0", 1))
            pe.wait_ge(*at("perf_q_t_ready1", 1))
            for a in range(2):
                for g in range(4):
                    for m in range(2):
                        last = pe.matmul(ps[0:PERF_N, 6 + a, g * (DH + 1):(g + 1) * (DH + 1)],
                                         prob_t[:, 2 * g + m, PERF_N * a:PERF_N * (a + 1)],
                                         kv_sb[:, 2 * m + a, g * (DH + 1):(g + 1) * (DH + 1)],
                                         start=(m == 0), stop=(m == 1))
            last.then_inc(sig("perf_attended"), 1)
            pe.wait_ge(*at("perf_ctx_ready", 1))
            for c in range(CH):
                last = pe.transpose(ps[:, 0, c * PERF_N:(c + 1) * PERF_N], ctxv[0:PERF_N, c * P:(c + 1) * P],
                                    ident[0:PERF_N, 0:PERF_N])
            last.then_inc(sig("perf_ctx_transposed"), 1)
            pe.wait_ge(*at("perf_ctx_t_ready", 1))
            weights("perf_wo")
            project_t(1, x1_t, matrix("perf_wo")).then_inc(sig("perf_o_projected"), 1)
            pe.wait_ge(*at("bn_out_ready", 2))
            for c in range(CH):
                last = pe.transpose(ps[:, 2, c * P:(c + 1) * P], z_t[:, c, :], ident[:])
            last.then_inc(sig("gps_out_transposed"), 1)

            layer_norm_transpose(3)
            weights("peer_wq")
            project_t(0, y_t, matrix("peer_wq")).then_inc(sig("peer_q_projected"), 1)
            pe.wait_ge(*at("peer_q_ready", 1))
            pe.wait_ge(*at("late_params_landed", 160))
            for r in range(4):
                rows = slice(32 * r, 32 * r + 32)
                for q in range(2):
                    last = pe.matmul(ps[:, 1 + r, q * KEYS:(q + 1) * KEYS], qk_t[rows, q, :], keys_t[rows, q, :],
                                     start=True, stop=True, tile_position=(32 * r, 0))
                last.then_inc(sig("peer_sim_ready"), 1)
            weights("peer_tables")
            for m in range(2):
                for c in range(CH):
                    last = pe.matmul(ps[:, 5, m * P:(m + 1) * P], peer_down[:, c, m * P:(m + 1) * P], qk_t[:, c, :],
                                     start=(c == 0), stop=(c == CH - 1))
            last.then_inc(sig("peer_down_projected"), 1)
            for h in range(H):
                pe.wait_ge(*at("peer_masked", h + 1))
                pe.wait_ge(*at("peer_diag_ready", h + 1))
                for m in range(2):
                    last = pe.matmul(ps[:, 6 + m, 0:P], peer_pick[:, h % 2, m * P:(m + 1) * P], x1_t[:, h % 2, :],
                                     start=(h == 0), stop=(h == H - 1))
                last.then_inc(sig("peer_head_added"), 1)
            pe.wait_ge(*at("peer_weights_ready", 1))
            for m in range(2):
                last = pe.matmul(bank(0), z_t[:, m, :], peer_up[:, m, :], start=(m == 0), stop=(m == 1))
            last.then_inc(sig("peer_up_projected"), 1)

            layer_norm_transpose(4)
            weights("exph_wq")
            project_t(0, y_t, matrix("exph_wq")).then_inc(sig("exph_q_projected"), 1)
            weights("exph_wk")
            project_t(1, y_t, matrix("exph_wk")).then_inc(sig("exph_k_projected"), 1)
            pe.wait_ge(*at("exph_q_ready", 1))
            pe.wait_ge(*at("exph_k_ready", 1))
            for a in range(2):
                r = slice(DH * a, DH * a + DH)
                for g in range(4):
                    last = pe.matmul(ps[:, 3 + a, g * P:(g + 1) * P], qk_t[r, CH + g, :], qk_t[r, g, :],
                                     start=True, stop=True)
                last.then_inc(sig("exph_scored"), 1)
            weights("exph_wv")
            project(2, y_t, matrix("exph_wv")).then_inc(sig("exph_v_projected"), 1)
            pe.wait_ge(*at("exph_v_ready", 1))
            for a in range(2):
                pe.wait_ge(*at("exph_weights_ready", a + 1))
                for g in range(4):
                    last = pe.matmul(ps[:, 5 + a, g * (DH + 1):(g + 1) * (DH + 1)], prob_t[:, 4 * a + g, :],
                                     heads_v[:, 2 * g + a, :], start=True, stop=True)
            last.then_inc(sig("exph_attended"), 1)
            pe.wait_ge(*at("exph_h_ready", 1))
            transpose_rows(0, ctxv).then_inc(sig("exph_h_transposed"), 1)
            pe.wait_ge(*at("bn_out_ready", 3))
            for c in range(CH):
                last = pe.transpose(ps[:, 1, c * P:(c + 1) * P], z_t[:, c, :], ident[:])
            last.then_inc(sig("exph_out_transposed"), 1)

            layer_norm_transpose(5)
            weights("gate_wk")
            project_t(0, y_t, matrix("gate_wk")).then_inc(sig("gate_keys_projected"), 1)
            pe.wait_ge(*at("gate_keys_ready", 1))
            for c in range(CH):
                last = pe.matmul(ps[:, 5, 0:E], z_t[:, c, :], eq_t[:, c, :], start=(c == 0), stop=(c == CH - 1))
            last.then_inc(sig("gate_scored"), 1)

            def expert_q(n, u, it):
                pe.wait_ge(*at(f"l2_wqk_landed{u}", it * 16 + 16))
                project_t(0, y_t, l2_wqk(u)).then_inc(sig("l2_qk_projected"), 1)

            def expert_k(u):
                project_t(1, y_t, l2_wqk(u), first=CH).then_inc(sig("l2_qk_projected"), 1)

            def expert_v(u, it):
                pe.wait_ge(*at(f"l2_wv_landed{u}", it * 16 + 16))
                project(2, y_t, l2_wv(u)).then_inc(sig("l2_v_projected"), 1)

            def expert_scores(n):
                pe.wait_ge(*at("l2_q_ready", n + 1))
                pe.wait_ge(*at("l2_k_ready", n + 1))
                scores("l2_scored", lambda g: g)

            def expert_pe(n, u, it, next_it, has_next):
                if has_next:
                    expert_q(n + 1, 1 - u, next_it)
                transpose_probs("l2_prob_ready", "l2_prob_transposed", n, (5, 6))
                pe.wait_ge(*at("l2_v_ready", n + 1))
                pe.wait_ge(*at("l2_h2_ready", n + 1))
                attend(7, "l2_prob_t_ready0", "l2_prob_t_ready1", n, lambda h: v[:, h * DH:(h + 1) * DH]) \
                    .then_inc(sig("l2_attended"), 1)
                if has_next:
                    expert_k(1 - u)
                pe.wait_ge(*at("l2_ctx_ready", n + 1))
                transpose_rows(3, ctxv).then_inc(sig("l2_ctx_transposed"), 1)
                pe.wait_ge(*at("l2_ctx_t_ready", n + 1))
                pe.wait_ge(*at(f"l2_wo_landed{u}", it * 16 + 16))
                project(4, ctx_t, wo_of(u)).then_inc(sig("l2_o_projected"), 1)
                if has_next:
                    expert_v(1 - u, next_it)
                pe.wait_ge(*at("l2_x1_ready", n + 1))
                transpose_rows(5, x1).then_inc(sig("l2_x1_transposed"), 1)
                pe.wait_ge(*at("l2_x1_t_ready", n + 1))
                pe.wait_ge(*at(f"l2_small_landed{u}", it * 32 + 32))
                for c in range(CH):
                    last = pe.matmul(ps[0:F2, 6, 0:P], ew1[:, u, c, :], x1_t[:, c, :], start=(c == 0), stop=(c == CH - 1))
                last.then_inc(sig("l2_h1_projected"), 1)
                if has_next:
                    expert_scores(n + 1)
                pe.wait_ge(*at("l2_h1_ready", n + 1))
                pe.matmul(bank(7), h1_t[:], ew2[:, u, :], start=True, stop=True).then_inc(sig("l2_h2_projected"), 1)

            expert_q(0, 0, 0)
            expert_k(0)
            pe.wait_ge(*at("gated_ready", 1))
            pe.transpose(ps[0:E, 5, 0:P], gated[:], ident[:]).then_inc(sig("gated_transposed"), 1)
            pe.wait_ge(*at("gated_t_ready", 1))
            pe.matmul(bank(6), gated_t[:], be2[:], start=True, stop=True).then_inc(sig("be2_shared"), 1)
            expert_v(0, 0)
            expert_scores(0)
            pe.wait_ge(*at("acc_ready", 1))
            with pe.Fori(0, E // 2 - 1) as i:
                for u in range(2):
                    expert_pe(i * 2 + u, u, i, i + u, True)
            expert_pe(E - 2, 0, E // 2 - 1, E // 2 - 1, True)
            expert_pe(E - 1, 1, E // 2 - 1, None, False)

            layer_norm_transpose(6)
            pe.wait_ge(*at("gcn_sd_ready", 1))
            for k in range(3):
                weights(f"gcn_w{k + 1}")
                if k:
                    pe.wait_ge(*at("gcn_z_ready", k))
                project(0, z_t if k else y_t, matrix(f"gcn_w{k + 1}")).then_inc(sig("gcn_h_projected"), 1)
                pe.wait_ge(*at("gcn_h_ready", k + 1))
                if k < 2:
                    for c in range(CH):
                        last = pe.matmul(ps[:, 1, c * P:(c + 1) * P], ctxv[:, c * P:(c + 1) * P], gcn_sd[:],
                                         start=True, stop=True)
                else:
                    last = pe.matmul(bank(1), gcn_sd[:], ctxv[:], start=True, stop=True)
                last.then_inc(sig("gcn_mixed"), 1)

            layer_norm_transpose(7)
            for c in range(CH):
                last = pe.matmul(ps[:, 6, 0:E], y_t[:, c, :], router_w[:, c, :], start=(c == 0), stop=(c == CH - 1))
            last.then_inc(sig("router_scored"), 1)

            def lstm_gates(n, u, it):
                for j, (w, first, landed_by) in enumerate(((l3_wi(u), 0, "l3_wi_landed"), (l3_wgo(u), 0, "l3_wgo_landed"),
                                                           (l3_wgo(u), CH, "l3_wgo_landed"))):
                    if j < 2:
                        pe.wait_ge(*at(f"{landed_by}{u}", it * 16 + 16))
                    if not isinstance(n, int) or n > 0:
                        pe.wait_ge(*at("l3_gate_ready", n * 3 + (j - 2)))
                    project_t(j, y_t, w, first=first).then_inc(sig("l3_gates_projected"), 1)

            def lstm_out(n, u, it):
                pe.wait_ge(*at("l3_h_ready", n + 2))
                pe.wait_ge(*at(f"l3_wo_landed{u}", it * 16 + 16))
                if not isinstance(n, int) or n > 0:
                    pe.wait_ge(*at("l3_expert_added", n))
                project(3 + u, h_t[u], wo_of(u)).then_inc(sig("l3_o_projected"), 1)

            lstm_gates(0, 0, 0)
            pe.wait_ge(*at("lstm_gated_ready", 1))
            pe.transpose(ps[0:E, 5, 0:P], gated[:], ident[:]).then_inc(sig("lstm_gated_transposed"), 1)
            pe.wait_ge(*at("lstm_gated_t_ready", 1))
            pe.matmul(bank(7), gated_t[:], lstm_bo[:], start=True, stop=True).then_inc(sig("lstm_bo_shared"), 1)
            lstm_gates(1, 1, 0)
            lstm_out(0, 0, 0)
            with pe.Fori(1, E // 2) as i:
                for u in range(2):
                    lstm_gates(i * 2 + u, u, i)
                    lstm_out(i * 2 + (u - 1), 1 - u, i + (u - 1))
            lstm_out(E - 1, 1, E // 2 - 1)

        @block.vector
        def _(dve):
            settle = dve.drain

            def layer_norm(k):
                settle()
                dve.bn_stats(ln_st[:], x[:])
                settle()
                dve.bn_aggr(ln_mv[:], ln_st[:])
                settle()
                dve.tensor_scalar_add(ln_var[:], ln_mv[:, 1:2], EPS).then_inc(sig("ln_var_ready"), 1)
                dve.wait_ge(*at("ln_rstd_ready", k + 1))
                dve.tensor_scalar(y[:], x[:], ln_mv[:, 0:1], ln_rstd[:], ALU.subtract, ALU.mult).then_inc(sig("y_ready"), 1)

            def batch_norm(k, in_t, gamma, beta):
                settle()
                for c in range(CH):
                    dve.bn_stats(bn_st[:, c, :], in_t[:, c, :])
                settle()
                for c in range(CH):
                    dve.bn_aggr(bn_mv[:, c, :], bn_st[:, c, :])
                settle()
                dve.tensor_scalar_add(bn_var[:], bn_mv[:, :, 1], EPS).then_inc(sig("bn_var_ready"), 1)
                dve.wait_ge(*at("bn_rstd_ready", k + 1))
                dve.tensor_tensor(bn_scale[:], bn_rstd[:], cols[:, gamma, :], ALU.mult)
                settle()
                dve.tensor_tensor(bn_shift[:], bn_mv[:, :, 0], bn_scale[:], ALU.mult)
                settle()
                dve.tensor_tensor(bn_shift[:], cols[:, beta, :], bn_shift[:], ALU.subtract)
                settle()
                for c in range(CH):
                    last = dve.tensor_scalar(z_t[:, c, :], in_t[:, c, :], bn_scale[:, c:c + 1], bn_shift[:, c:c + 1],
                                             ALU.mult, ALU.add)
                last.then_inc(sig("bn_out_ready"), 1)

            def maxima(scored, done, n, scale):
                for a in range(2):
                    s = slice(4 * a, 4 * a + 4)
                    dve.wait_ge(*at(scored, n * 2 + (a + 1)))
                    dve.tensor_reduce(nmax[:, s], bank_chunks(3 + a), AX.X, ALU.max, negate=True)
                    settle()
                    dve.tensor_scalar(nmax_s[:, s], nmax[:, s], scale, None, ALU.mult).then_inc(sig(done), 1)

            def normalise(b):
                return dve.tensor_tensor(hd, ps[:, b, :].rearrange("p (g a d) -> p g a d", g=4, a=2),
                                         rinv[:].rearrange("p (a g) -> p g a", a=2).unsqueeze(3).broadcast_to([P, 4, 2, DH]),
                                         ALU.mult)

            dve.memset(s_cat[:], 0.0)
            dve.memset(gat_l[:], 0.0)
            dve.memset(h1_t[:], 1.0)
            settle()
            dve.memset(gat_l[32:40], 1.0)
            dve.wait_ge(*at("x_landed", 16))
            layer_norm(0)
            dve.wait_ge(*at("edges_landed", 32))
            dve.wait_ge(*at("iota_ready", 1))
            dve.tensor_copy(src_f[:], src_i[:])
            dve.tensor_copy(dst_f[:], dst_i[:])
            dve.tensor_copy(iota_f[:], iota_i[:])
            settle()
            for k, ends in enumerate((src_f, dst_f)):
                dve.tensor_tensor(one_hot[:, k, :, :],
                                  iota_f[:].unsqueeze(1).broadcast_to([P, EDGES_PER_PARTITION, P]),
                                  ends[:].unsqueeze(2).broadcast_to([P, EDGES_PER_PARTITION, P]),
                                  ALU.is_equal).then_inc(sig("one_hot_ready"), 1)
            dve.wait_ge(*at("edges_counted", 1))
            dve.tensor_copy(cnt_sd[:], ps[:, 5, 0:P]).then_inc(sig("counts_ready"), 1)
            dve.tensor_copy(cnt_ds[:], ps[:, 6, 0:P]).then_inc(sig("counts_ready"), 1)
            settle()
            dve.wait_ge(*at("const_ready", 3))
            dve.tensor_tensor(gat_cap[:], cnt_sd[:], ident[:], ALU.add)
            dve.tensor_reduce(deg_col[:], cnt_ds[:], AX.X, ALU.add)
            settle()
            dve.tensor_scalar(gat_cap[:], gat_cap[:], 1.0, -2.0 * GAT_NEG, ALU.min, ALU.mult)
            dve.tensor_scalar_add(deg_col[:], deg_col[:], 1.0)
            settle()
            dve.tensor_scalar(gat_cap[:], gat_cap[:], GAT_NEG, None, ALU.add)

            dve.wait_ge(*at("gat_h_projected", 1))
            dve.wait_ge(*at("gat_a_landed", 16))
            for k in range(2):
                dve.tensor_tensor(wide[:, k, 0:D], bank(0), attn_a[:, k, :], ALU.mult)
            settle()
            for k in range(2):
                dve.tensor_reduce(s_cat[:, 32 * k:32 * k + H], wide[:, k, 0:D].rearrange("p (h d) -> p h d", h=H),
                                  AX.X, ALU.add).then_inc(sig("gat_s_ready"), 1)
            settle()
            dve.memset(small[:, 2:3], 0.0).then_inc(sig("gat_a_used"), 1)
            dve.wait_ge(*at("degrees_summed", 1))
            dve.tensor_scalar(mean_sd[:], ps[:, 2, 0:P], 1.0, None, ALU.max)
            dve.tensor_scalar(deg[:], ps[:, 2, 0:P], 1.0, None, ALU.add).then_inc(sig("gcn_deg_ready"), 1)
            dve.wait_ge(*at("gat_s_transposed", 1))
            dve.tensor_copy(gat_l[0:H], ps[0:H, 1, 0:P]).then_inc(sig("gat_lr_ready"), 1)
            dve.wait_ge(*at("gat_r_ready", 2))
            dve.tensor_tensor(gat_r[32:32 + H], gat_r[32:32 + H],
                              ps[32:32 + H, 1, 0:P].unsqueeze(1).broadcast_to([H, H, P]), ALU.mult) \
                .then_inc(sig("gat_lr_ready"), 1)
            settle()
            dve.reciprocal(deg_rec, mean_sd[:])
            settle()
            dve.tensor_tensor(mean_sd[:], deg_rec, cnt_sd[:], ALU.mult).then_inc(sig("mean_sd_ready"), 1)
            dve.wait_ge(*at("gat_scored", 1))
            for a in range(2):
                s = prob[:, 4 * a:4 * a + 4, :]
                dve.wait_ge(*at("gat_leak_ready", a + 1))
                dve.tensor_tensor(s.rearrange("p h n -> p (h n)"), ps[:, 3 + a, :], wide[:, a, 0:512], ALU.max)
                settle()
                dve.tensor_tensor(s, s, gat_cap[:].unsqueeze(1).broadcast_to([P, 4, P]), ALU.min)
            settle()
            dve.tensor_reduce(nmax[:], prob[:], AX.X, ALU.max, negate=True).then_inc(sig("gat_max_ready"), 1)
            dve.wait_ge(*at("gat_prob_transposed", 1))
            dve.tensor_copy(prob_t[:, 0:4, :].rearrange("p h n -> p (h n)"), bank(5)).then_inc(sig("gat_prob_t_ready0"), 1)
            dve.wait_ge(*at("gat_prob_ready", 8))
            dve.reciprocal(rinv[:], rsum[:])
            settle()
            dve.wait_ge(*at("gat_attended", 1))
            dve.tensor_tensor(ctxv[:].rearrange("p (h d) -> p h d", h=H), bank_heads(0),
                              rinv[:].unsqueeze(2).broadcast_to([P, H, DH]), ALU.mult)
            settle()
            dve.tensor_reduce(small[:, 0:1], ctxv[:], AX.X, ALU.max, negate=True).then_inc(sig("gat_out_ready"), 1)
            dve.wait_ge(*at("gat_exp_ready", 1))
            dve.reciprocal(small[:, 2:3], small[:, 1:2])
            settle()
            dve.scalar_tensor_tensor(x[:], t1[:], small[:, 2:3], x[:], ALU.mult, ALU.add).then_inc(sig("x_updated"), 1)
            dve.wait_ge(*at("gcn_dis_ready", 2))
            dve.tensor_tensor(gcn_sd[:], cnt_sd[:], ident[:], ALU.add)
            settle()
            dve.scalar_tensor_tensor(gcn_sd[:], gcn_sd[:], dis_col[:], deg[:], ALU.mult, ALU.mult) \
                .then_inc(sig("gcn_sd_ready"), 1)

            layer_norm(1)
            dve.wait_ge(*at("y_t_ready", 2))
            dve.tensor_reduce(r_mean[:], y_t[:], AX.X, ALU.add)
            settle()
            dve.tensor_scalar(r_mean[:], r_mean[:], 1.0 / P, None, ALU.mult).then_inc(sig("route_mean_ready"), 1)
            dve.wait_ge(*at("router_landed", 64))
            dve.wait_ge(*at("route_hidden_summed", 1))
            dve.tensor_scalar(r_hcol[:], ps[:, 2, 0:1], r_b1[:], 0.0, ALU.add, ALU.max)
            settle()
            dve.tensor_copy(r_h[:], r_hcol[:].broadcast_to([P, P])).then_inc(sig("route_hidden_ready"), 1)
            dve.wait_ge(*at("gqa_k_projected", 1))
            dve.tensor_copy(qk_t[:, CH:, :].rearrange("p c n -> p (c n)"), bank(1)).then_inc(sig("gqa_k_ready"), 1)
            dve.wait_ge(*at("route_logits_summed", 1))
            dve.tensor_tensor(r_p[:, 0:3], ps[:, 5, 0:3], r_b2[:], ALU.add)
            settle()
            dve.tensor_reduce(small[:, 0:1], r_p[:, 0:3], AX.X, ALU.max, negate=True).then_inc(sig("route_logits_ready"), 1)
            dve.wait_ge(*at("gqa_v_projected", 1))
            dve.tensor_copy(v[:, 0:D], bank(2)).then_inc(sig("gqa_v_ready"), 1)
            dve.wait_ge(*at("route_exp_ready", 1))
            dve.reciprocal(small[:, 2:3], small[:, 1:2])
            settle()
            dve.tensor_scalar(r_p[:, 0:3], r_p[:, 0:3], small[:, 2:3], None, ALU.mult)
            settle()
            dve.tensor_reduce(small[:, 3:4], r_p[:, 0:3], AX.X, ALU.max)
            settle()
            dve.tensor_scalar(r_mask[:, 0:3], r_p[:, 0:3], small[:, 3:4], None, ALU.is_equal)
            settle()
            dve.tensor_scalar(r_p[:, 3:5], r_mask[:, 0:2], -1.0, 1.0, ALU.mult, ALU.add)
            settle()
            dve.tensor_scalar(r_mask[:, 1:3], r_mask[:, 1:3], r_p[:, 3:4], None, ALU.mult)
            settle()
            dve.tensor_scalar(r_mask[:, 2:3], r_mask[:, 2:3], r_p[:, 4:5], None, ALU.mult)
            for n in range(3):
                maxima("gqa_scored", "gqa_max_ready", n, DH ** -0.5)
                if n < 2:
                    dve.wait_ge(*at("gqa_k_projected", n + 2))
                    kc = CH if n == 0 else 1
                    dve.tensor_copy(qk_t[:, CH:CH + kc, :].rearrange("p c n -> p (c n)"), ps[:, 1, 0:kc * P]) \
                        .then_inc(sig("gqa_k_ready"), 1)
                dve.wait_ge(*at("gqa_prob_transposed", 2 * n + 1))
                dve.tensor_copy(prob_t[:, 0:4, :].rearrange("p h n -> p (h n)"), bank(5)).then_inc(sig("gqa_prob_t_ready0"), 1)
                dve.wait_ge(*at("gqa_prob_ready", 2 * n + 2))
                dve.reciprocal(rinv[:], rsum[:])
                settle()
                dve.tensor_scalar(rinv[:], rinv[:], r_mask[:, n:n + 1], None, ALU.mult)
                settle()
                dve.wait_ge(*at("gqa_attended", n + 1))
                if n < 2:
                    pass
                normalise(3).then_inc(sig("gqa_ctx_ready"), 1)
                if n < 2:
                    nv = (256, 64)[n]
                    dve.wait_ge(*at("gqa_v_projected", n + 2))
                    dve.tensor_copy(v[:, 0:nv], ps[:, 2, 0:nv]).then_inc(sig("gqa_v_ready"), 1)
            dve.wait_ge(*at("gqa_o_projected", 3))
            dve.memset(heads_v[:, :, DH:DH + 1], 1.0).then_inc(sig("v_free"), 1)
            dve.tensor_tensor(x[:], x[:], bank(6), ALU.add).then_inc(sig("x_updated"), 1)

            layer_norm(2)
            dve.memset(qk_t[:], 0.0)
            dve.wait_ge(*at("y_t_ready", 3))
            dve.tensor_copy(x1_t[:].rearrange("p c (a n) -> p c a n", a=2),
                            y_t[:, :, 0:PERF_N].unsqueeze(2).broadcast_to([P, CH, 2, PERF_N])).then_inc(sig("perf_rows_ready"), 1)
            dve.wait_ge(*at("params_landed", 48))
            batch_norm(0, y_t, N1G, N1B)
            dve.wait_ge(*at("perf_qk_projected", 1))
            for a in range(2):
                r = slice(DH * a, DH * a + DH)
                last = dve.tensor_scalar(qk_t[r, :, PERF_N * a:PERF_N * (a + 1)],
                                         ps[r, 0, :].rearrange("p (s n) -> p s n", s=8), DH ** -0.25, None, ALU.mult)
                last.then_inc(sig("perf_t_scaled"), 1)
            settle()
            dve.tensor_tensor(prob[:], qk_t[:], qk_t[:], ALU.mult).then_inc(sig("perf_sq_ready"), 1)
            dve.memset(small[:, 3:4], 0.0).then_inc(sig("perf_t_ready"), 1)
            for w in range(2):
                dve.wait_ge(*at("perf_u_ready", w + 1))
                dve.tensor_reduce(small[:, 4 + 0:8] if w else small[:, 8:12],
                                  ps[:, 4 + 2 * w:6 + 2 * w, :].rearrange("p b (g m) -> p (b g) m", m=PERF_M),
                                  AX.X, ALU.max)
                settle()
                if w:
                    dve.memset(small[:, 3:4], 0.0).then_inc(sig("perf_kmax_ready"), 1)
                else:
                    dve.wait_ge(*at("perf_diag_summed", 1))
                    dve.scalar_tensor_tensor(small[:, 16:20], ps[:, 0, 0:4], -0.5, small[:, 8:12], ALU.mult, ALU.subtract) \
                        .then_inc(sig("perf_bias_ready0"), 1)
            dve.wait_ge(*at("perf_kmax_transposed", 1))
            dve.tensor_reduce(perf_k2[:], ps[0:4, 0, P:2 * P].rearrange("g (a n) -> g a n", a=2), AX.X, ALU.max)
            settle()
            dve.tensor_copy(perf_r[:], perf_k2[:].unsqueeze(2).broadcast_to([4, 2, PERF_N])) \
                .then_inc(sig("perf_kmax_rows_ready"), 1)
            dve.wait_ge(*at("perf_kmax_spread", 1))
            dve.tensor_copy(small[:, 12:16], ps[:, 0, 2 * P:2 * P + 4])
            settle()
            dve.scalar_tensor_tensor(small[:, 20:24], ps[:, 0, 4:8], -0.5, small[:, 12:16], ALU.mult, ALU.subtract) \
                .then_inc(sig("perf_bias_ready1"), 1)
            for w in range(2):
                dve.wait_ge(*at("perf_exp_ready", w + 1))
                dve.tensor_scalar(wide[:, w, :], wide[:, w, :], PERF_M ** -0.5, PERF_EPS, ALU.mult, ALU.add) \
                    .then_inc(sig("perf_features_ready"), 1)
            dve.wait_ge(*at("perf_kv_done", 1))
            for b in (0, 2):
                dve.tensor_copy(kv_sb[:, b, :], ps[:, b, 0:4 * (DH + 1)]).then_inc(sig("perf_kv_ready"), 1)
            dve.wait_ge(*at("perf_q_transposed", 1))
            dve.tensor_copy(prob_t[:, 0:4, :].rearrange("p h n -> p (h n)"), bank(4)).then_inc(sig("perf_q_t_ready0"), 1)
            dve.wait_ge(*at("conv_t_ready", 1))
            dve.tensor_tensor(ctx_t[:], ctx_t[:], y_t[:], ALU.add)
            dve.wait_ge(*at("perf_attended", 1))
            for a in range(2):
                num = ps[0:PERF_N, 6 + a, 0:4 * (DH + 1)].rearrange("p (g e) -> p g e", g=4)
                zz = small[0:PERF_N, 24 + 4 * a:28 + 4 * a]
                dve.tensor_scalar(zz, num[:, :, DH], PERF_EPS, None, ALU.add)
                settle()
                dve.reciprocal(zz, zz)
                settle()
                dve.tensor_tensor(hd[0:PERF_N, :, a, :], num[:, :, 0:DH], zz.unsqueeze(2).broadcast_to([PERF_N, 4, DH]),
                                  ALU.mult)
            settle()
            dve.memset(small[:, 3:4], 0.0).then_inc(sig("perf_ctx_ready"), 1)
            dve.wait_ge(*at("perf_ctx_transposed", 1))
            pt = ps[:, 0, 0:CH * PERF_N].rearrange("p (c n) -> p c n", c=CH)
            dve.tensor_copy(x1_t[:, :, 0:PERF_N], pt)
            dve.tensor_copy(x1_t[:, :, PERF_N:P], pt[:, :, PERF_N - 1:PERF_N].broadcast_to([P, CH, P - PERF_N]))
            settle()
            dve.memset(small[:, 3:4], 0.0).then_inc(sig("perf_ctx_t_ready"), 1)
            dve.wait_ge(*at("perf_o_projected", 1))
            dve.tensor_tensor(ctx_t[:].rearrange("p c n -> p (c n)"), ctx_t[:].rearrange("p c n -> p (c n)"), bank(1), ALU.add)
            batch_norm(1, ctx_t, N2G, N2B)
            dve.wait_ge(*at("gps_out_transposed", 1))
            dve.tensor_tensor(x[:], x[:], bank(2), ALU.add).then_inc(sig("x_updated"), 1)

            layer_norm(3)
            dve.wait_ge(*at("peer_q_projected", 1))
            dve.tensor_scalar(qk_t[:, 0:CH, :].rearrange("p c n -> p (c n)"), bank(0), (1.0 + EPS) ** -0.5, None, ALU.mult) \
                .then_inc(sig("peer_q_ready"), 1)

            def merge(h):
                b = h % 2
                dve.wait_ge(*at("peer_exp_ready", h + 1))
                if h >= 2:
                    dve.wait_ge(*at("peer_head_added", h - 1))
                dve.scalar_tensor_tensor(peer_pick[:, b, :], peer_rest[:, b, :], NEG, peer_exp[:, b, :], ALU.is_equal,
                                         ALU.mult, accum_out=picksum[:, h:h + 1]).then_inc(sig("peer_masked"), 1)
                settle()
                dve.reciprocal(pickinv[:, h:h + 1], picksum[:, h:h + 1]).then_inc(sig("peer_inv_ready"), 1)

            for h in range(H):
                b = h % 2
                sim = ps[:, 1 + h // 2, (h % 2) * KEYS:(h % 2 + 1) * KEYS]
                dve.wait_ge(*at("peer_sim_ready", h // 2 + 1))
                dve.max(topv[:, b, 0:8], sim)
                settle()
                dve.match_replace(peer_work, topv[:, b, 0:8], sim, NEG)
                dve.max_index(topi[:, b, 0:8], topv[:, b, 0:8], sim)
                settle()
                dve.max(topv[:, b, 8:16], peer_work)
                settle()
                dve.max_index(topi[:, b, 8:16], topv[:, b, 8:16], peer_work)
                settle()
                dve.tensor_copy(topif[:, b, :], topi[:, b, :])
                settle()
                if h >= 2:
                    dve.wait_ge(*at("peer_exp_ready", h - 1))
                dve.tensor_tensor(peer_all[:, b, :].rearrange("p (i j) -> p i j", i=TOPK),
                                  topv[:, b, :].unsqueeze(2).broadcast_to([P, TOPK, TOPK]),
                                  topif[:, b, :].unsqueeze(1).broadcast_to([P, TOPK, TOPK]), ALU.add)
                settle()
                dve.max(best[:, b, 0:8], peer_all[:, b, :])
                settle()
                dve.tensor_scalar(negbest[:, b:b + 1], best[:, b, 0:1], -1.0, None, ALU.mult).then_inc(sig("peer_best_ready"), 1)
                dve.match_replace(peer_work, best[:, b, 0:8], peer_all[:, b, :], NEG)
                settle()
                dve.max(best[:, b, 8:16], peer_work)
                settle()
                dve.match_replace(peer_rest[:, b, :], best[:, b, 8:16], peer_work, NEG)
                settle()
                merge(h)
            dve.wait_ge(*at("peer_head_added", H))
            dve.wait_ge(*at("peer_gelu_ready", 1))
            for m in range(2):
                last = dve.tensor_tensor(z_t[:, m, :], ps[:, 6 + m, 0:P], x1_t[:, 2 + m, :], ALU.mult)
            last.then_inc(sig("peer_weights_ready"), 1)
            dve.wait_ge(*at("peer_up_projected", 1))
            dve.tensor_tensor(x[:], x[:], bank(0), ALU.add).then_inc(sig("x_updated"), 1)

            layer_norm(4)
            dve.wait_ge(*at("exph_k_projected", 1))
            dve.tensor_copy(qk_t[:, CH:, :].rearrange("p c n -> p (c n)"), bank(1)).then_inc(sig("exph_k_ready"), 1)
            clip = 5.0 * DH ** 0.5
            for a in range(2):
                dve.wait_ge(*at("exph_scored", a + 1))
                dve.tensor_scalar(prob[:, 4 * a:4 * a + 4, :].rearrange("p h n -> p (h n)"), bank(3 + a), -clip, clip,
                                  ALU.max, ALU.min).then_inc(sig("exph_clipped"), 1)
            for a in range(2):
                s = slice(4 * a, 4 * a + 4)
                dve.wait_ge(*at("exph_exp_ready", a + 1))
                dve.tensor_tensor(prob_t[:, s, :], prob[:, s, :], cnt_sd[:].unsqueeze(1).broadcast_to([P, 4, P]), ALU.mult) \
                    .then_inc(sig("exph_weights_ready"), 1)
            dve.wait_ge(*at("exph_attended", 1))
            for a in range(2):
                num = ps[:, 5 + a, 0:4 * (DH + 1)].rearrange("p (g e) -> p g e", g=4)
                zz = small[:, 24 + 4 * a:28 + 4 * a]
                dve.tensor_scalar(zz, num[:, :, DH], 1e-6, None, ALU.add)
                settle()
                dve.reciprocal(zz, zz)
                settle()
                dve.tensor_tensor(hd[:, :, a, :], num[:, :, 0:DH], zz.unsqueeze(2).broadcast_to([P, 4, DH]), ALU.mult)
            settle()
            dve.tensor_tensor(ctxv[:], ctxv[:], y[:], ALU.add).then_inc(sig("exph_h_ready"), 1)
            dve.wait_ge(*at("exph_h_transposed", 1))
            dve.tensor_copy(ctx_t[:].rearrange("p c n -> p (c n)"), bank(0))
            batch_norm(2, ctx_t, BNG, BNB)
            dve.wait_ge(*at("exph_out_transposed", 1))
            dve.tensor_tensor(x[:], x[:], bank(1), ALU.add).then_inc(sig("x_updated"), 1)

            layer_norm(5)

            def top2():
                dve.max(gtop[:], gate8[:])
                settle()
                dve.max_index(gidx[:], gtop[:], gate8[:])
                settle()
                dve.tensor_copy(gidxf[:], gidx[:])
                settle()

            dve.wait_ge(*at("gate_scored", 1))
            dve.tensor_reduce(small[:, 2:3], ps[:, 5, 0:E], AX.X, ALU.max, negate=True)
            settle()
            dve.tensor_scalar(small[:, 0:1], small[:, 2:3], D ** -0.5, None, ALU.mult).then_inc(sig("gate_max_ready"), 1)
            dve.wait_ge(*at("gate_exp_ready", 1))
            dve.reciprocal(small[:, 2:3], small[:, 1:2])
            settle()
            dve.tensor_scalar(gate8[:], gate8[:], small[:, 2:3], None, ALU.mult)
            settle()
            top2()
            dve.tensor_scalar(gated[:], iota_f[:, 0:E], gidxf[:, 0:1], gtop[:, 0:1], ALU.is_equal, ALU.mult)
            dve.tensor_scalar(small[:, 8:16], iota_f[:, 0:E], gidxf[:, 1:2], gtop[:, 1:2], ALU.is_equal, ALU.mult)
            dve.tensor_tensor(small[:, 4:5], gtop[:, 0:1], gtop[:, 1:2], ALU.add)
            settle()
            dve.tensor_scalar(small[:, 4:5], small[:, 4:5], 1e-9, None, ALU.add)
            dve.tensor_tensor(gated[:], gated[:], small[:, 8:16], ALU.add)
            settle()
            dve.reciprocal(small[:, 4:5], small[:, 4:5])
            settle()
            dve.tensor_scalar(gated[:], gated[:], small[:, 4:5], None, ALU.mult).then_inc(sig("gated_ready"), 1)

            def k_bias(n):
                dve.wait_ge(*at("l2_qk_projected", n * 2 + 2))
                for c in range(CH):
                    last = dve.tensor_scalar(qk_t[:, CH + c, :], ps[:, 1, c * P:(c + 1) * P],
                                             bqk[:, bass.ds(n * 8 + (CH + c), 1)], None, ALU.add)
                last.then_inc(sig("l2_k_ready"), 1)

            def v_bias(n, u, it):
                dve.wait_ge(*at(f"l2_rows_landed{u}", it * 16 + 16))
                dve.wait_ge(*at("l2_v_projected", n + 1))
                dve.tensor_tensor(v[:, 0:D], bank(2), erows[:, u, BV, :], ALU.add).then_inc(sig("l2_v_ready"), 1)

            def statistics(rows):
                settle()
                dve.bn_stats(ln_st[:], rows[:])
                settle()
                dve.bn_aggr(ln_mv[:], ln_st[:])
                settle()
                dve.tensor_scalar_add(ln_var[:], ln_mv[:, 1:2], EPS).then_inc(sig("l2_var_ready"), 1)

            def expert_dve(n, u, next_it, has_next):
                dve.wait_ge(*at("l2_prob_transposed", n * 2 + 1))
                dve.tensor_copy(prob_t[:, 0:4, :].rearrange("p h n -> p (h n)"), bank(5)).then_inc(sig("l2_prob_t_ready0"), 1)
                dve.wait_ge(*at("l2_prob_ready", n * 2 + 2))
                dve.reciprocal(rinv[:], rsum[:])
                settle()
                dve.wait_ge(*at("l2_attended", n + 1))
                normalise(7).then_inc(sig("l2_ctx_ready"), 1)
                if has_next:
                    k_bias(n + 1)
                dve.wait_ge(*at("l2_residual_ready", n + 1))
                dve.wait_ge(*at("l2_o_projected", n + 1))
                dve.tensor_tensor(t1[:], bank(4), erows[:, u, BO, :], ALU.add)
                statistics(t1)
                dve.scalar_tensor_tensor(x1[:], t1[:], ln_mv[:, 0:1], erows[:, u, G1, :], ALU.subtract, ALU.mult)
                settle()
                dve.wait_ge(*at("l2_rstd_ready", n * 2 + 1))
                dve.scalar_tensor_tensor(x1[:], x1[:], ln_rstd[:], erows[:, u, BE1, :], ALU.mult, ALU.add) \
                    .then_inc(sig("l2_x1_ready"), 1)
                if has_next:
                    v_bias(n + 1, 1 - u, next_it)
                    maxima("l2_scored", "l2_max_ready", n + 1, DH ** -0.5)
                dve.wait_ge(*at("l2_h2_ready", n + 2))
                dve.tensor_tensor(t1[:], x1[:], h2[:], ALU.add)
                statistics(t1)
                dve.scalar_tensor_tensor(t1[:], t1[:], ln_mv[:, 0:1], erows[:, u, G2, :], ALU.subtract, ALU.mult)
                dve.wait_ge(*at("l2_rstd_ready", n * 2 + 2))
                dve.tensor_tensor(rg[:], ln_rstd[:], gated[:, bass.ds(n, 1)], ALU.mult)
                settle()
                dve.scalar_tensor_tensor(acc[:], t1[:], rg[:], acc[:], ALU.mult, ALU.add).then_inc(sig("l2_expert_added"), 1)

            k_bias(0)
            dve.wait_ge(*at("gated_transposed", 1))
            dve.tensor_copy(gated_t[:], ps[0:E, 5, 0:P]).then_inc(sig("gated_t_ready"), 1)
            dve.wait_ge(*at("be2_shared", 1))
            dve.tensor_copy(acc[:], bank(6)).then_inc(sig("acc_ready"), 1)
            v_bias(0, 0, 0)
            maxima("l2_scored", "l2_max_ready", 0, DH ** -0.5)
            with dve.Fori(0, E // 2 - 1) as i:
                for u in range(2):
                    expert_dve(i * 2 + u, u, i + u, True)
            expert_dve(E - 2, 0, E // 2 - 1, True)
            expert_dve(E - 1, 1, None, False)
            settle()
            dve.tensor_tensor(x[:], x[:], acc[:], ALU.add).then_inc(sig("x_updated"), 1)

            layer_norm(6)
            dve.tensor_tensor(x[:], x[:], gcn_b3[:], ALU.add)
            settle()
            dve.wait_ge(*at("gcn_mixed", 3))
            dve.tensor_tensor(x[:], x[:], bank(1), ALU.add).then_inc(sig("x_updated"), 1)

            layer_norm(7)
            dve.tensor_scalar(lstm_hb[:], lstm_b[:], 0.5, None, ALU.mult).then_inc(sig("lstm_hb_ready"), 1)
            dve.wait_ge(*at("router_scored", 1))
            dve.tensor_tensor(gate8[:], ps[:, 6, 0:E], router_b[:], ALU.add)
            settle()
            top2()
            dve.tensor_scalar(small[:, 0:1], gtop[:, 0:1], -1.0, None, ALU.mult)
            dve.tensor_copy(gated[:], gtop[:]).then_inc(sig("router_max_ready"), 1)
            dve.wait_ge(*at("router_exp_ready", 1))
            dve.tensor_tensor(small[:, 4:5], gate8[:, 0:1], gate8[:, 1:2], ALU.add)
            dve.tensor_scalar(gated[:], iota_f[:, 0:E], gidxf[:, 0:1], gate8[:, 0:1], ALU.is_equal, ALU.mult)
            dve.tensor_scalar(small[:, 8:16], iota_f[:, 0:E], gidxf[:, 1:2], gate8[:, 1:2], ALU.is_equal, ALU.mult)
            settle()
            dve.reciprocal(small[:, 4:5], small[:, 4:5])
            dve.tensor_tensor(gated[:], gated[:], small[:, 8:16], ALU.add)
            settle()
            dve.tensor_scalar(gated[:], gated[:], small[:, 4:5], None, ALU.mult).then_inc(sig("lstm_gated_ready"), 1)
            settle()
            dve.tensor_scalar(gate8[:], gated[:], 0.5, None, ALU.mult)

            def lstm_cell(n, u):
                dve.wait_ge(*at("l3_gate_ready", n * 3 + 2))
                dve.scalar_tensor_tensor(t1[:], prob[:, 0:4, :].rearrange("p c n -> p (c n)"), 1.0,
                                         prob[:, 4:8, :].rearrange("p c n -> p (c n)"), ALU.add, ALU.mult) \
                    .then_inc(sig("l3_cell_ready"), 1)
                dve.wait_ge(*at("l3_cell_tanh_ready", n + 1))
                dve.scalar_tensor_tensor(h_t[u][:].rearrange("p c n -> p (c n)"),
                                         prob_t[:, 0:4, :].rearrange("p c n -> p (c n)"), 1.0,
                                         prob_t[:, 4:8, :].rearrange("p c n -> p (c n)"), ALU.add, ALU.mult) \
                    .then_inc(sig("l3_h_ready"), 1)

            def lstm_add(n, u):
                settle()
                dve.wait_ge(*at("l3_o_projected", n + 1))
                dve.scalar_tensor_tensor(acc[:], bank(3 + u), gate8[:, bass.ds(n, 1)], acc[:], ALU.mult, ALU.add) \
                    .then_inc(sig("l3_expert_added"), 1)

            dve.sem_inc(sig("l3_h_ready"), 1)
            dve.sem_inc(sig("l3_expert_added"), 1)
            lstm_cell(0, 0)
            dve.wait_ge(*at("lstm_gated_transposed", 1))
            dve.tensor_copy(gated_t[:], ps[0:E, 5, 0:P]).then_inc(sig("lstm_gated_t_ready"), 1)
            dve.wait_ge(*at("lstm_bo_shared", 1))
            dve.tensor_tensor(acc[:], x[:], bank(7), ALU.add)
            settle()
            lstm_cell(1, 1)
            lstm_add(0, 0)
            with dve.Fori(1, E // 2) as i:
                for u in range(2):
                    lstm_cell(i * 2 + u, u)
                    lstm_add(i * 2 + (u - 1), 1 - u)
            lstm_add(E - 1, 1)
            settle()
            dve.tensor_copy(x[:], acc[:]).then_inc(sig("x_updated"), 1)


def lay_out(inputs):
    import numpy as np

    a = {k: np.asarray(v) for k, v in inputs.items()}

    def by_partition(w):
        s = w.shape
        w = w.reshape(*s[:-2], s[-2] // P, P, s[-1])
        return np.moveaxis(w, -3, -2)

    def columns(w):
        return np.moveaxis(w.reshape(*w.shape[:-1], -1, P), -1, 0)

    swap = lambda w: np.swapaxes(w, -1, -2)
    o = {"x": a["x"], "src": a["src"].reshape(P, -1), "dst": a["dst"].reshape(P, -1)}
    o["l0_W"] = by_partition(a["L0_gnn_W"].transpose(1, 0, 2).reshape(D, D))
    o["gat_a"] = a["L0_gnn_a"].reshape(H, 2, DH).transpose(1, 0, 2).reshape(2, D)
    for n in range(3):
        for k in ("wq", "wk", "wv", "wo"):
            o[f"{k}{n}"] = by_partition(a[f"L0_ffn_{k}{n}"])
    o["r_w1"] = by_partition(a["L0_ffn_r_w1"])
    o["r_w2"] = a["L0_ffn_r_w2"]
    o["r_b1"] = a["L0_ffn_r_b1"].reshape(P, 1)
    o["r_b2"] = a["L0_ffn_r_b2"].reshape(1, 3)
    o["conv"] = by_partition(a["L1_gnn_W_conv"])
    for k in ("q", "k", "v", "o"):
        o[f"perf_w{k}"] = by_partition(a[f"L1_gnn_W{k}"])
    o["proj_t"] = swap(a["L1_gnn_proj"])
    o["peer_wq"] = by_partition(a["L1_ffn_w_q"])
    o["keys_t"] = a["L1_ffn_keys"].reshape(2, 4, KEYS, 2, 32).transpose(3, 1, 4, 0, 2).reshape(2, P, 2, KEYS)
    o["peer_down"] = by_partition(swap(a["L1_ffn_weight_down_embed"]))
    o["peer_up"] = a["L1_ffn_weight_up_embed"]
    for k in ("q", "k", "v"):
        o[f"exph_w{k}"] = by_partition(a[f"L2_gnn_W{k}"])
    o["gate_wk"] = by_partition(swap(a["L2_ffn_gate_Wk"]))
    o["eq_t"] = by_partition(swap(a["L2_ffn_expert_queries"]))
    qkv = by_partition(swap(a["L2_ffn_Wqkv"]))
    o["l2_wqk"], o["l2_wv"] = qkv[..., 0:2 * D], qkv[..., 2 * D:]
    o["l2_wo"] = by_partition(swap(a["L2_ffn_Wo"]))
    o["l2_w1"] = by_partition(swap(a["L2_ffn_W1"]))
    o["l2_w2"] = np.concatenate([swap(a["L2_ffn_W2"]), a["L2_ffn_bf2"][:, None, :]], axis=1)
    o["l2_rows"] = np.stack([a["L2_ffn_bqkv"][:, 2 * D:], a["L2_ffn_bo"], a["L2_ffn_g1"], a["L2_ffn_be1"],
                             a["L2_ffn_g2"]], axis=1)
    o["bqk"] = columns(a["L2_ffn_bqkv"][:, 0:2 * D]).reshape(P, -1)
    o["bf1"] = swap(a["L2_ffn_bf1"])
    o["be2"] = a["L2_ffn_be2"]
    for n in range(3):
        o[f"gcn_w{n + 1}"] = by_partition(a[f"L3_gnn_W{n + 1}"])
    o["gcn_b3"] = a["L3_gnn_b3"].reshape(1, D)
    o["router_w"] = by_partition(a["L3_ffn_router_w"])
    o["router_b"] = a["L3_ffn_router_b"].reshape(1, E)
    o["l3_wi"] = by_partition(a["L3_ffn_Wi"])
    o["l3_wo"] = by_partition(a["L3_ffn_Wo"])
    o["lstm_b"] = columns(a["L3_ffn_b"]).reshape(P, -1)
    o["lstm_bo"] = a["L3_ffn_bo"]
    o["cols"] = columns(np.stack([a[k] for k in (
        "L1_gnn_norm1_g", "L1_gnn_norm1_b", "L1_gnn_norm2_g", "L1_gnn_norm2_b", "L1_gnn_b_conv",
        "L2_gnn_bn_gamma", "L2_gnn_bn_beta", "L2_ffn_gate_bk", "L3_gnn_b1", "L3_gnn_b2")]))
    return {k: np.ascontiguousarray(w) for k, w in o.items()}


def kernel(**inputs):
    import concourse.bacc as bacc
    from concourse.bass_utils import run_bass_kernel_spmd

    nc = bacc.Bacc("TRN2", target_bir_lowering=False, num_devices=1)
    arrays, aps = {}, {}
    for name, a in lay_out(inputs).items():
        arrays[f"in_{name}"] = a
        aps[name] = nc.dram_tensor(f"in_{name}", a.shape, mybir.dt.from_np(a.dtype), kind="ExternalInput").ap()
    out = nc.dram_tensor("out_x", (P, D), F32, kind="ExternalOutput").ap()
    build(nc, aps, out)
    r = run_bass_kernel_spmd(nc, [arrays], core_ids=[0])
    return r.results[0]["out_x"]
```

```python
from contextlib import ExitStack

import concourse.bass as bass
from concourse import mybir

F32 = mybir.dt.float32
BF16 = mybir.dt.bfloat16
I32 = mybir.dt.int32
U32 = mybir.dt.uint32
ALU = mybir.AluOpType
ACT = mybir.ActivationFunctionType
AX = mybir.AxisListType

P = 128
D = 512
CH = D // P
H = 8
DH = D // H
EDGES_PER_PARTITION = 2176 // P
EPS = 1e-5
SUBLAYERS = 8

PERF_N = 64
PERF_M = 256
PERF_EPS = 1e-6
KEYS = 256
TOPK = 16
PICKS = TOPK * TOPK
E = 8
F2 = 64
NEG = -3.0e38
GAT_NEG = -9000000000000000.0

BV, BO, G1, BE1, G2 = range(5)
N1G, N1B, N2G, N2B, BCONV, BNG, BNB, GATEB, GCNB1, GCNB2 = range(10)

DENSE_USED = {
    "l0_W": ("gat_h_projected", 1),
    "perf_wq": ("perf_qk_projected", 1), "perf_wk": ("perf_qk_projected", 1), "perf_wv": ("perf_v_projected", 1),
    "conv": ("conv_h_projected", 1), "perf_wo": ("perf_o_projected", 1),
    "peer_wq": ("peer_q_projected", 1), "peer_tables": ("peer_up_projected", 1),
    "exph_wq": ("exph_q_projected", 1), "exph_wk": ("exph_k_projected", 1), "exph_wv": ("exph_v_projected", 1),
    "gate_wk": ("gate_keys_projected", 1),
    "gcn_w1": ("gcn_h_projected", 2), "gcn_w2": ("gcn_h_projected", 4), "gcn_w3": ("gcn_h_projected", 6),
}
DENSE = list(DENSE_USED)
SLOTS = 6


STEPS = {
    "gat_tensor_steps": [("gat_h_projected", 1), ("edges_counted", 1), ("gat_s_transposed", 1),
                         ("gat_scored", 1), ("gat_prob_transposed", 2), ("gat_attended", 1)],
    "gat_vector_steps": [("one_hot_ready", 2), ("gat_s_ready", 2), ("gat_a_used", 1), ("gat_lr_ready", 2),
                         ("counts_ready", 1), ("gat_max_ready", 2), ("gat_prob_t_ready0", 1), ("gat_out_ready", 1)],
    "gat_scalar_steps": [("gat_h_ready", 1), ("gat_leak_ready", 2), ("gat_prob_ready", 8), ("gat_prob_t_ready1", 1),
                         ("gat_exp_ready", 1), ("route_exp_ready", 1)],
    "route_tensor_steps": [("route_summed", 1), ("route_hidden_summed", 1), ("route_logits_summed", 1),
                           ("counts_transposed", 1), ("adjacency_transposed", 1)],
    "route_vector_steps": [("route_mean_ready", 1), ("route_hidden_ready", 1), ("route_logits_ready", 1),
                           ("route_selected", 1), ("gcn_deg_ready", 1), ("adjacency_ready", 2), ("mean_sd_ready", 1),
                           ("gcn_sd_ready", 1)],
    "gps_tensor_steps": [("perf_qk_projected", 1), ("perf_v_projected", 1), ("perf_u_ready", 2), ("perf_kmax_transposed", 1),
                         ("perf_diag_summed", 1), ("perf_kmax_spread", 1), ("conv_h_projected", 1),
                         ("perf_q_transposed", 1), ("conv_mixed", 1), ("perf_kv_done", 1), ("perf_attended", 1),
                         ("perf_ctx_transposed", 1), ("perf_o_projected", 1), ("gps_out_transposed", 1)],
    "gps_vector_steps": [("perf_rows_ready", 1), ("perf_t_scaled", 2), ("perf_t_ready", 1), ("perf_sq_ready", 1),
                         ("perf_kmax_ready", 1), ("perf_qmax_ready", 1), ("perf_kmax_rows_ready", 1),
                         ("perf_bias_ready0", 1), ("perf_bias_ready1", 1), ("perf_features_ready", 2),
                         ("perf_q_t_ready0", 1), ("perf_kv_ready", 2), ("perf_ctx_ready", 1), ("perf_ctx_t_ready", 1)],
    "gps_scalar_steps": [("perf_v_ready", 1), ("perf_exp_ready", 2), ("conv_h_ready", 1), ("perf_q_t_ready1", 1),
                         ("conv_t_ready", 1), ("perf_kv_ready_act", 2)],
    "exph_tensor_steps": [("exph_q_projected", 1), ("exph_k_projected", 1), ("exph_scored", 2), ("exph_v_projected", 1),
                          ("exph_attended", 1), ("exph_h_transposed", 1), ("exph_out_transposed", 1),
                          ("gate_keys_projected", 1), ("gate_scored", 1), ("gated_transposed", 1), ("be2_shared", 1)],
    "exph_vector_steps": [("exph_k_ready", 1), ("exph_clipped", 2), ("exph_weights_ready", 2), ("exph_h_ready", 1),
                          ("gate_max_ready", 1), ("gated_ready", 1), ("gated_t_ready", 1)],
    "exph_scalar_steps": [("exph_q_ready", 1), ("exph_v_ready", 1), ("exph_exp_ready", 2), ("gate_keys_ready", 1),
                          ("gate_exp_ready", 1), ("router_exp_ready", 1)],
    "router_tensor_steps": [("router_scored", 1), ("lstm_gated_transposed", 1), ("lstm_bo_shared", 1)],
    "router_vector_steps": [("lstm_hb_ready", 1), ("router_max_ready", 1), ("lstm_gated_ready", 1),
                            ("lstm_gated_t_ready", 1)],
}
STEP_BASE = {}
for _semaphore, _steps in STEPS.items():
    _n = 0
    for _step, _times in _steps:
        STEP_BASE[_step] = (_semaphore, _n)
        _n += _times


def build(nc, A, out):
    ctx = ExitStack()
    signals = {}

    def sig(name):
        name = STEP_BASE.get(name, (name, 0))[0]
        if name not in signals:
            signals[name] = ctx.enter_context(nc.semaphore(name))
        return signals[name]

    def at(name, value):
        return sig(name), STEP_BASE.get(name, (name, 0))[1] + value

    with ctx:
        def sb(name, shape, dt=F32):
            return ctx.enter_context(nc.sbuf_tensor(name, shape, dt))

        ps = ctx.enter_context(nc.psum_tensor("ps", [P, 8, 512], F32))

        dense = sb("dense", [P, SLOTS, CH * D])
        ew = sb("ew", [P, 2, 4 * CH * D])
        ew1 = sb("ew1", [P, 2, CH, F2])
        ew2 = sb("ew2", [F2 + 1, 2, D])
        erows = sb("erows", [P, 2, 5, D])
        r_w1 = erows[:, 1, 0, :].rearrange("p (c n) -> p c n", c=CH)
        r_w2 = sb("r_w2", [P, 3])
        r_b1 = sb("r_b1", [P, 1])
        r_b2 = sb("r_b2", [1, 3])
        attn_a = erows[:, 0, 0:2, :]
        cols = sb("cols", [P, 10, CH])
        proj_t = sb("proj_t", [P, PERF_M])
        keys_t = sb("keys_t", [P, 2, KEYS])
        bqk = sb("bqk", [P, E * 8])
        bf1 = sb("bf1", [F2, E])
        eq_t = sb("eq_t", [P, CH, E])
        be2 = sb("be2", [E, D])
        gcn_b3 = sb("gcn_b3", [P, D])
        router_w = sb("router_w", [P, CH, E])
        router_b = sb("router_b", [P, E])
        lstm_b = sb("lstm_b", [P, E * 16])
        lstm_hb = sb("lstm_hb", [P, E * 16])
        lstm_bo = sb("lstm_bo", [E, D])

        ident = sb("ident", [P, P])
        iota_i = sb("iota_i", [P, P], I32)
        iota_f = sb("iota_f", [P, P])
        minus_half = sb("minus_half", [P, CH])
        ones = sb("ones", [P, P])

        src_i = sb("src_i", [P, EDGES_PER_PARTITION], I32)
        dst_i = sb("dst_i", [P, EDGES_PER_PARTITION], I32)
        src_f = sb("src_f", [P, EDGES_PER_PARTITION])
        dst_f = sb("dst_f", [P, EDGES_PER_PARTITION])
        one_hot = ew[:, 1, 0:EDGES_PER_PARTITION * P].bitcast(BF16).rearrange("p (a t n) -> p a t n", a=2, n=P)
        cnt_sd = sb("cnt_sd", [P, P])
        gat_cap = sb("gat_cap", [P, P])
        mean_sd = sb("mean_sd", [P, P])
        gcn_sd = sb("gcn_sd", [P, P])
        mean_ds = sb("mean_ds", [P, P])
        gcn_ds = sb("gcn_ds", [P, P])
        mean_col = sb("mean_col", [P, 1])
        deg_col = sb("deg_col", [P, 1])
        dis_col = sb("dis_col", [P, 1])

        x = sb("x", [P, D])
        y = sb("y", [P, D])
        y_t = sb("y_t", [P, CH, P])
        z_t = sb("z_t", [P, CH, P])
        acc = sb("acc", [P, D])
        qk_t = sb("qk_t", [P, 2 * CH, P])
        v = sb("v", [P, H * (DH + 1)])
        prob_store = sb("prob_store", [P, 4 * 4 * (DH + 1)])
        prob = prob_store[:, 0:H * P].rearrange("p (h n) -> p h n", h=H)
        prob_t = sb("prob_t", [P, H, P])
        ctxv = sb("ctxv", [P, D])
        ctx_t = sb("ctx_t", [P, CH, P])
        t1 = sb("t1", [P, D])
        x1 = sb("x1", [P, D])
        x1_t = sb("x1_t", [P, CH, P])
        h1_t = sb("h1_t", [F2 + 1, P])
        h2 = sb("h2", [P, D])
        big = sb("big", [P, 2 * H * P])

        ln_st = sb("ln_st", [P, 6])
        ln_mv = sb("ln_mv", [P, 2])
        ln_var = sb("ln_var", [P, 1])
        ln_rstd = sb("ln_rstd", [P, 1])
        bn_st = sb("bn_st", [P, CH, 6])
        bn_mv = sb("bn_mv", [P, CH, 2])
        bn_var = sb("bn_var", [P, CH])
        bn_rstd = sb("bn_rstd", [P, CH])
        bn_scale = sb("bn_scale", [P, CH])
        bn_shift = sb("bn_shift", [P, CH])
        nmax = sb("nmax", [P, H])
        nmax_s = sb("nmax_s", [P, H])
        rsum = sb("rsum", [P, H])
        rinv = sb("rinv", [P, H])
        s_cat = sb("s_cat", [P, 40])
        gat_l = sb("gat_l", [40, P])
        gat_r = sb("gat_r", [40, H, P])
        r_mean = sb("r_mean", [P, CH])
        r_hcol = sb("r_hcol", [P, 1])
        r_p = sb("r_p", [1, 8])
        r_top = sb("r_top", [1, 8])
        selected = sb("selected", [1, 8], U32)
        small = sb("small", [P, 32])
        perf_r = sb("perf_r", [4, 2, PERF_N])
        perf_k2 = sb("perf_k2", [4, 2])
        topv = sb("topv", [P, 4, TOPK])
        topi = sb("topi", [P, 4, TOPK], U32)
        topif = sb("topif", [P, 4, TOPK])
        best = sb("best", [P, 4, TOPK])
        negbest = sb("negbest", [P, 4])
        picksum = sb("picksum", [P, H])
        pickinv = sb("pickinv", [P, H])
        gate8 = sb("gate8", [P, E])
        gated = sb("gated", [P, E])
        gidx = sb("gidx", [P, 8], U32)
        gidxf = sb("gidxf", [P, 8])
        gtop = sb("gtop", [P, 8])
        gated_t = sb("gated_t", [E, P])
        rg = sb("rg", [P, 1])

        def l2_wqk(u):
            return ew[:, u, 0:2 * CH * D].rearrange("p (c n) -> p c n", c=CH)

        def l2_wv(u):
            return ew[:, u, 2 * CH * D:3 * CH * D].rearrange("p (c n) -> p c n", c=CH)

        def wo_of(u):
            return ew[:, u, 3 * CH * D:4 * CH * D].rearrange("p (c n) -> p c n", c=CH)

        def l3_wi(u):
            return ew[:, u, 0:CH * D].rearrange("p (c n) -> p c n", c=CH)

        def l3_wgo(u):
            return ew[:, u, CH * D:3 * CH * D].rearrange("p (c n) -> p c n", c=CH)

        landed, so_far = {}, [0] * SLOTS
        for n, name in enumerate(DENSE):
            so_far[n % SLOTS] += 32 if name == "peer_tables" else 16
            landed[name] = so_far[n % SLOTS]

        def slot(name):
            return dense[:, DENSE.index(name) % SLOTS, :]

        def matrix(name, n=D):
            return slot(name)[:, 0:CH * n].rearrange("p (c n) -> p c n", c=CH)

        peer_down = slot("peer_tables")[:, 0:CH * PICKS].rearrange("p (c n) -> p c n", c=CH)
        peer_up = slot("peer_tables")[:, CH * PICKS:CH * PICKS + 2 * D].rearrange("p (c n) -> p c n", c=2)

        heads_v = v[:, :].rearrange("p (h e) -> p h e", h=H)
        pair_v = v[:, :].rearrange("p (g a e) -> p g a e", g=4, a=2)
        hd = ctxv[:, :].rearrange("p (g a d) -> p g a d", g=4, a=2)
        peer_work = t1[:, :].rearrange("p (b n) -> p b n", b=2)
        wide = big[:, :].rearrange("p (a n) -> p a n", a=2)
        kv_sb = prob_store[:, :].rearrange("p (b n) -> p b n", b=4)
        peer_all, peer_exp, peer_rest, peer_pick = (
            tile.rearrange("p (b n) -> p b n", b=4) for tile in (
                big[:, 0:4 * PICKS], big[:, 4 * PICKS:8 * PICKS], prob_t[:].rearrange("p h n -> p (h n)"),
                prob_store[:, 0:4 * PICKS]))
        h_t = (ctx_t, x1_t)

        def bank(b):
            return ps[:, b, :]

        def bank_heads(b):
            return ps[:, b, :].rearrange("p (h d) -> p h d", h=H)

        def bank_chunks(b):
            return ps[:, b, :].rearrange("p (c n) -> p c n", c=CH)

        block = ctx.enter_context(nc.Block())

        @block.sync
        def _(sp):
            def load_dense(name):
                n = DENSE.index(name)
                if n >= SLOTS:
                    done, value = DENSE_USED[DENSE[n - SLOTS]]
                    sp.wait_ge(*at(done, value))
                s = sig(f"dense_landed{n % SLOTS}")
                if name == "peer_tables":
                    sp.dma_start(peer_down, A["peer_down"][:, :, 0:PICKS]).then_inc(s, 16)
                    sp.dma_start(peer_up, A["peer_up"][0:PICKS, :].rearrange("(c p) n -> p c n", p=P)).then_inc(s, 16)
                else:
                    sp.dma_start(slot(name), A[name].rearrange("p c n -> p (c n)")).then_inc(s, 16)

            def load_l2(e, u):
                sp.dma_start(l2_wqk(u), A["l2_wqk"][e]).then_inc(sig(f"l2_wqk_landed{u}"), 16)
                sp.dma_start(l2_wv(u), A["l2_wv"][e]).then_inc(sig(f"l2_wv_landed{u}"), 16)
                sp.dma_start(wo_of(u), A["l2_wo"][e]).then_inc(sig(f"l2_wo_landed{u}"), 16)

                sp.dma_start(ew1[:, u], A["l2_w1"][e]).then_inc(sig(f"l2_small_landed{u}"), 16)
                sp.dma_start(ew2[:, u], A["l2_w2"][e]).then_inc(sig(f"l2_small_landed{u}"), 16)

            def load_l2_rows(e, u):
                sp.dma_start(erows[:, u], A["l2_rows"][e].rearrange("(a r) n -> a r n", a=1)
                             .broadcast_to([P, 5, D])).then_inc(sig(f"l2_rows_landed{u}"), 16)

            def load_l3(e, u):
                sp.dma_start(l3_wi(u), A["l3_wi"][e][:, :, 0:D]).then_inc(sig(f"l3_wi_landed{u}"), 16)
                sp.dma_start(l3_wgo(u), A["l3_wi"][e][:, :, 2 * D:4 * D]).then_inc(sig(f"l3_wgo_landed{u}"), 16)
                sp.dma_start(wo_of(u), A["l3_wo"][e]).then_inc(sig(f"l3_wo_landed{u}"), 16)

            sp.dma_start(x[:], A["x"]).then_inc(sig("x_landed"), 16)
            sp.dma_start(attn_a, A["gat_a"].rearrange("(a r) n -> a r n", a=1).broadcast_to([P, 2, D])) \
                .then_inc(sig("gat_a_landed"), 16)
            for name in DENSE[:SLOTS]:
                load_dense(name)
            for tile, name in ((r_w1[:], "r_w1"), (r_w2[:], "r_w2"), (r_b1[:], "r_b1")):
                sp.dma_start(tile, A[name]).then_inc(sig("router_landed"), 16)
            sp.dma_start(r_b2[:], A["r_b2"]).then_inc(sig("router_landed"), 16)
            sp.dma_start(cols[:], A["cols"]).then_inc(sig("params_landed"), 16)
            sp.dma_start(proj_t[0:DH], A["proj_t"]).then_inc(sig("params_landed"), 16)
            sp.dma_start(proj_t[DH:P], A["proj_t"]).then_inc(sig("params_landed"), 16)
            for tile, name in ((keys_t[:], "keys_t"), (bqk[:], "bqk"), (bf1[:], "bf1"), (eq_t[:], "eq_t"),
                               (be2[:], "be2"), (router_w[:], "router_w"), (lstm_b[:], "lstm_b"),
                               (lstm_bo[:], "lstm_bo")):
                sp.dma_start(tile, A[name][0] if name == "keys_t" else A[name]).then_inc(sig("late_params_landed"), 16)
            sp.dma_start(gcn_b3[:], A["gcn_b3"].broadcast_to([P, D])).then_inc(sig("late_params_landed"), 16)
            sp.dma_start(router_b[:], A["router_b"].broadcast_to([P, E])).then_inc(sig("late_params_landed"), 16)
            sp.wait_ge(*at("edges_counted", 1))
            load_l2(1, 1)
            sp.wait_ge(*at("gat_a_used", 1))
            load_l2_rows(0, 0)
            load_dense(DENSE[SLOTS])
            sp.wait_ge(*at("route_selected", 1))
            variant = sp.value_load(selected[0:1, 0:1], min_val=0, max_val=2)
            for k, name in enumerate(("wq", "wk", "wv", "wo")):
                sp.dma_start(ew[:, 0, k * CH * D:(k + 1) * CH * D], A[f"gqa_{name}"][variant]) \
                    .then_inc(sig(f"gqa_{name}_landed"), 16)
            load_l2_rows(1, 1)
            sp.wait_ge(*at("gqa_o_projected", 1))
            load_l2(0, 0)
            for name in DENSE[SLOTS + 1:]:
                load_dense(name)
            with sp.Fori(1, E // 2) as i:
                for u in range(2):
                    n = i * 2 + u
                    sp.wait_ge(*at("l2_qk_projected", n * 2 - 2))
                    sp.dma_start(l2_wqk(u), A["l2_wqk"][n]).then_inc(sig(f"l2_wqk_landed{u}"), 16)
                    sp.wait_ge(*at("l2_v_projected", n - 1))
                    sp.dma_start(l2_wv(u), A["l2_wv"][n]).then_inc(sig(f"l2_wv_landed{u}"), 16)
                    sp.wait_ge(*at("l2_o_projected", n - 1))
                    sp.dma_start(wo_of(u), A["l2_wo"][n]).then_inc(sig(f"l2_wo_landed{u}"), 16)
                    sp.wait_ge(*at("l2_h2_projected", n - 1))
                    sp.dma_start(ew1[:, u], A["l2_w1"][n]).then_inc(sig(f"l2_small_landed{u}"), 16)
                    sp.dma_start(ew2[:, u], A["l2_w2"][n]).then_inc(sig(f"l2_small_landed{u}"), 16)
                    sp.wait_ge(*at("l2_expert_added", n - 1))
                    sp.dma_start(erows[:, u], A["l2_rows"][n].rearrange("(a r) n -> a r n", a=1)
                                 .broadcast_to([P, 5, D])).then_inc(sig(f"l2_rows_landed{u}"), 16)
            for u in range(2):
                sp.wait_ge(*at("l2_qk_projected", 2 * (E - 1 + u)))
                sp.wait_ge(*at("l2_v_projected", E - 1 + u))
                sp.wait_ge(*at("l2_o_projected", E - 1 + u))
                load_l3(u, u)
            with sp.Fori(1, E // 2) as i:
                for u in range(2):
                    n = i * 2 + u
                    sp.wait_ge(*at("l3_gates_projected", n * 3 - 3))
                    sp.dma_start(l3_wi(u), A["l3_wi"][n][:, :, 0:D]).then_inc(sig(f"l3_wi_landed{u}"), 16)
                    sp.dma_start(l3_wgo(u), A["l3_wi"][n][:, :, 2 * D:4 * D]).then_inc(sig(f"l3_wgo_landed{u}"), 16)
                    sp.wait_ge(*at("l3_o_projected", n - 1))
                    sp.dma_start(wo_of(u), A["l3_wo"][n]).then_inc(sig(f"l3_wo_landed{u}"), 16)
            for s, value in (("router_landed", 64), ("params_landed", 48), ("late_params_landed", 160)):
                sp.wait_ge(*at(s, value))
            sp.wait_ge(*at("x_updated", SUBLAYERS))
            sp.dma_start(out, x[:]).then_inc(sig("out_written"), 16)
            sp.wait_ge(*at("out_written", 16))

        @block.gpsimd
        def _(pool):
            pool.memset(ident[:], 0.0).then_inc(sig("pool_cleared"), 1)
            pool.memset(gat_r[:], 0.0).then_inc(sig("pool_cleared"), 1)
            pool.memset(minus_half[:], -0.5).then_inc(sig("const_ready"), 1)
            pool.memset(ones[:], 1.0).then_inc(sig("const_ready"), 1)
            pool.iota(iota_i[:], pattern=[[1, P]], base=0, channel_multiplier=0).then_inc(sig("iota_ready"), 1)
            pool.wait_ge(*at("pool_cleared", 2))
            pool.affine_select(out=ident[:], in_=ident[:], compare_op=ALU.not_equal, fill=1.0, base=0,
                               pattern=[[-1, P]], channel_multiplier=1).then_inc(sig("const_ready"), 1)
            pool.wait_ge(*at("const_ready", 3))
            for p0 in (0, 32):
                if p0:
                    pool.wait_ge(*at("gat_r_ready", 1))
                pool.affine_select(out=gat_r[p0:p0 + H], in_=gat_r[p0:p0 + H], compare_op=ALU.not_equal,
                                   fill=1.0, base=0, pattern=[[-1, H], [0, P]], channel_multiplier=1) \
                    .then_inc(sig("gat_r_ready"), 1)
            pool.wait_ge(*at("gat_r_ready", 2))

            def layer_norm_rstd(k):
                pool.wait_ge(*at("ln_var_ready", k + 1))
                pool.tensor_tensor(ln_rstd[:], ln_var[:], minus_half[:, 0:1], ALU.pow).then_inc(sig("ln_rstd_ready"), 1)

            def batch_norm_rstd(k):
                pool.wait_ge(*at("bn_var_ready", k + 1))
                pool.tensor_tensor(bn_rstd[:], bn_var[:], minus_half[:], ALU.pow).then_inc(sig("bn_rstd_ready"), 1)

            layer_norm_rstd(0)
            layer_norm_rstd(1)
            pool.wait_ge(*at("gcn_deg_ready", 1))
            pool.tensor_tensor(dis_col[:], deg_col[:], minus_half[:, 0:1], ALU.pow).then_inc(sig("gcn_dis_ready"), 1)
            layer_norm_rstd(2)
            batch_norm_rstd(0)
            batch_norm_rstd(1)
            layer_norm_rstd(3)
            def pair_sums(k):
                for b in (2 * k % 4, 2 * k % 4 + 1):
                    if b % 2 == 0:
                        pool.wait_ge(*at("peer_top_ready", k + 1))
                    else:
                        pool.wait_ge(*at("peer_sum_ready", k + 1))
                    pool.tensor_tensor(peer_all[:, b, :].rearrange("p (i j) -> p i j", i=TOPK),
                                       topv[:, b, :].unsqueeze(2).broadcast_to([P, TOPK, TOPK]),
                                       topif[:, b, :].unsqueeze(1).broadcast_to([P, TOPK, TOPK]), ALU.add) \
                        .then_inc(sig("peer_all_ready" if b % 2 else "peer_sum_ready"), 1)

            def diagonals(k):
                for h in (2 * k, 2 * k + 1):
                    if h % 2 == 0:
                        pool.wait_ge(*at("peer_inv_ready", k + 1))
                    else:
                        pool.wait_ge(*at("peer_diag_ready", h))
                    if h >= 2:
                        pool.wait_ge(*at("peer_head_added", h - 1))
                    pool.tensor_scalar(x1_t[:, h % 2, :], ident[:], pickinv[:, h:h + 1], None, ALU.mult) \
                        .then_inc(sig("peer_diag_ready"), 1)

            pair_sums(0)
            for k in range(1, H // 2):
                pair_sums(k)
                diagonals(k - 1)
            diagonals(H // 2 - 1)
            layer_norm_rstd(4)
            batch_norm_rstd(2)
            layer_norm_rstd(5)

            def residual_rows(n, rows_value, u):
                pool.wait_ge(*at(f"l2_rows_landed{u}", rows_value))
                pool.tensor_tensor(erows[:, u, BO, :], erows[:, u, BO, :], y[:], ALU.add) \
                    .then_inc(sig("l2_residual_ready"), 1)

            def inner_norms(n, first):
                pool.wait_ge(*at("l2_var_ready", n * 2 + first))
                pool.tensor_tensor(ln_rstd[:], ln_var[:], minus_half[:, 0:1], ALU.pow).then_inc(sig("l2_rstd_ready"), 1)

            pool.wait_ge(*at("y_ready", 6))
            residual_rows(0, 16, 0)
            with pool.Fori(0, E // 2 - 1) as i:
                for u in range(2):
                    inner_norms(i * 2 + u, 1)
                    residual_rows(i * 2 + u + 1, i * 16 + 16 * (u + 1), 1 - u)
                    inner_norms(i * 2 + u, 2)
            inner_norms(E - 2, 1)
            residual_rows(E - 1, 16 * (E // 2), 1)
            inner_norms(E - 2, 2)
            inner_norms(E - 1, 1)
            inner_norms(E - 1, 2)
            layer_norm_rstd(6)
            layer_norm_rstd(7)

        @block.scalar
        def _(act):
            for tile, name in ((src_i[:], "src"), (dst_i[:], "dst")):
                act.dma_start(tile, A[name]).then_inc(sig("edges_landed"), 16)
            act.preload_act_table(ACT.Exp)

            def layer_norm_t(k):
                act.wait_ge(*at("y_transposed", k + 1))
                nc.scalar.copy(y_t[:].rearrange("p c n -> p (c n)"), bank(7)).then_inc(sig("y_t_ready"), 1)

            def exps(scores_max, done, n, scale):
                for a in range(2):
                    act.wait_ge(*at(scores_max, n * 2 + (a + 1)))
                    for g in range(4):
                        s = 4 * a + g
                        last = nc.scalar.activation(prob[:, s, :], ps[:, 3 + a, g * P:(g + 1) * P], ACT.Exp,
                                                    bias=nmax_s[:, s:s + 1], scale=scale, accum_out=rsum[:, s:s + 1])
                    last.then_inc(sig(done), 1)

            layer_norm_t(0)
            act.wait_ge(*at("gat_h_projected", 1))
            act.wait_ge(*at("gat_s_ready", 1))
            nc.scalar.copy(v[:, 0:D], bank(0)).then_inc(sig("gat_h_ready"), 1)
            act.wait_ge(*at("gat_scored", 1))
            for a in range(2):
                nc.scalar.mul(wide[:, a, 0:512], bank(3 + a), 0.2).then_inc(sig("gat_leak_ready"), 1)
            for h in range(H):
                if h % 4 == 0:
                    act.wait_ge(*at("gat_max_ready", h // 4 + 1))
                nc.scalar.activation(prob[:, h, :], prob[:, h, :], ACT.Exp, bias=nmax[:, h:h + 1],
                                     accum_out=rsum[:, h:h + 1]).then_inc(sig("gat_prob_ready"), 1)
            act.wait_ge(*at("gat_prob_transposed", 2))
            nc.scalar.copy(prob_t[:, 4:8, :].rearrange("p h n -> p (h n)"), bank(6)).then_inc(sig("gat_prob_t_ready1"), 1)
            act.wait_ge(*at("gat_out_ready", 1))
            nc.scalar.activation(t1[:], ctxv[:], ACT.Exp, bias=small[:, 0:1], accum_out=small[:, 1:2]) \
                .then_inc(sig("gat_exp_ready"), 1)

            layer_norm_t(1)
            act.wait_ge(*at("route_logits_ready", 1))
            nc.scalar.activation(r_p[0:1, 0:3], r_p[0:1, 0:3], ACT.Exp, bias=small[0:1, 0:1], accum_out=small[0:1, 1:2]) \
                .then_inc(sig("route_exp_ready"), 1)
            act.wait_ge(*at("gqa_q_projected", 1))
            nc.scalar.copy(qk_t[:, 0:CH, :].rearrange("p c n -> p (c n)"), bank(0)).then_inc(sig("gqa_q_ready"), 1)
            exps("gqa_max_ready", "gqa_exps_ready", 0, DH ** -0.5)
            act.wait_ge(*at("gqa_prob_transposed", 2))
            nc.scalar.copy(prob_t[:, 4:8, :].rearrange("p h n -> p (h n)"), bank(7)).then_inc(sig("gqa_prob_t_ready1"), 1)
            act.wait_ge(*at("gqa_attended", 1))
            nc.scalar.copy(ctx_t[:].rearrange("p c n -> p (c n)"), bank(4)).then_inc(sig("gqa_ctx_t_ready"), 1)

            layer_norm_t(2)
            act.wait_ge(*at("perf_v_projected", 1))
            act.wait_ge(*at("v_cleared", 1))
            for a in range(2):
                r = slice(DH * a, DH * a + DH)
                last = nc.scalar.copy(pair_v[r, :, a, 0:DH],
                                      ps[r, 1, :].rearrange("p (g a d) -> p g a d", g=4, a=2)[:, :, a, :])
            last.then_inc(sig("perf_v_ready"), 1)
            for w in range(2):
                act.wait_ge(*at(f"perf_bias_ready{w}", 1))
                for g in range(4):
                    last = nc.scalar.activation(wide[:, w, g * PERF_M:(g + 1) * PERF_M],
                                                ps[:, 4 + 2 * w + g // 2, (g % 2) * PERF_M:(g % 2 + 1) * PERF_M],
                                                ACT.Exp, bias=small[:, 16 + 4 * w + g:17 + 4 * w + g])
                last.then_inc(sig("perf_exp_ready"), 1)
            act.wait_ge(*at("conv_h_projected", 1))
            nc.scalar.copy(ctxv[:], bank(3)).then_inc(sig("conv_h_ready"), 1)
            act.wait_ge(*at("perf_q_transposed", 1))
            nc.scalar.copy(prob_t[:, 4:8, :].rearrange("p h n -> p (h n)"), bank(5)).then_inc(sig("perf_q_t_ready1"), 1)
            act.wait_ge(*at("conv_mixed", 1))
            for c in range(CH):
                last = nc.scalar.activation(ctx_t[:, c, :], ps[:, 3, c * P:(c + 1) * P], ACT.Relu,
                                            bias=cols[:, BCONV, c:c + 1])
            last.then_inc(sig("conv_t_ready"), 1)
            act.wait_ge(*at("perf_kv_done", 1))
            for b in (1, 3):
                nc.scalar.copy(kv_sb[:, b, :], ps[:, b, 0:4 * (DH + 1)]).then_inc(sig("perf_kv_ready_act"), 1)

            layer_norm_t(3)
            act.preload_act_table(ACT.Gelu_apprx_tanh)
            act.wait_ge(*at("peer_down_projected", 1))
            nc.scalar.activation(x1_t[:, 2:4, :].rearrange("p c n -> p (c n)"), ps[:, 5, 0:2 * P],
                                 ACT.Gelu_apprx_tanh).then_inc(sig("peer_gelu_ready"), 1)
            act.preload_act_table(ACT.Exp)
            for h in range(H):
                act.wait_ge(*at("peer_best_ready", h // 2 + 1))
                nc.scalar.activation(peer_exp[:, h % 4, :], peer_all[:, h % 4, :], ACT.Exp,
                                     bias=negbest[:, h % 4:h % 4 + 1]).then_inc(sig("peer_exp_ready"), 1)

            layer_norm_t(4)
            act.wait_ge(*at("exph_q_projected", 1))
            nc.scalar.copy(qk_t[:, 0:CH, :].rearrange("p c n -> p (c n)"), bank(0)).then_inc(sig("exph_q_ready"), 1)
            act.wait_ge(*at("exph_v_projected", 1))
            nc.scalar.copy(heads_v[:, :, 0:DH], bank_heads(2)).then_inc(sig("exph_v_ready"), 1)
            for a in range(2):
                act.wait_ge(*at("exph_clipped", a + 1))
                nc.scalar.activation(prob[:, 4 * a:4 * a + 4, :], prob[:, 4 * a:4 * a + 4, :], ACT.Exp,
                                     scale=DH ** -0.5).then_inc(sig("exph_exp_ready"), 1)

            layer_norm_t(5)
            def q_bias(n):
                act.wait_ge(*at("l2_qk_projected", n * 2 + 1))
                for c in range(CH):
                    last = nc.scalar.activation(qk_t[:, c, :], ps[:, 0, c * P:(c + 1) * P], ACT.Identity,
                                                bias=bqk[:, bass.ds(n * 8 + c, 1)])
                last.then_inc(sig("l2_q_ready"), 1)

            def expert_act(n, has_next):
                exps("l2_max_ready", "l2_exps_ready", n, DH ** -0.5)
                act.wait_ge(*at("l2_prob_transposed", n * 2 + 2))
                nc.scalar.copy(prob_t[:, 4:8, :].rearrange("p h n -> p (h n)"), bank(6)).then_inc(sig("l2_prob_t_ready1"), 1)
                act.wait_ge(*at("l2_attended", n + 1))
                nc.scalar.copy(ctx_t[:].rearrange("p c n -> p (c n)"), bank(7)).then_inc(sig("l2_ctx_t_ready"), 1)
                if has_next:
                    q_bias(n + 1)
                act.wait_ge(*at("l2_x1_transposed", n + 1))
                nc.scalar.copy(x1_t[:].rearrange("p c n -> p (c n)"), bank(5)).then_inc(sig("l2_x1_t_ready"), 1)
                act.preload_act_table(ACT.Gelu)
                act.wait_ge(*at("l2_h1_projected", n + 1))
                nc.scalar.activation(h1_t[0:F2, :], ps[0:F2, 6, 0:P], ACT.Gelu, bias=bf1[:, bass.ds(n, 1)]) \
                    .then_inc(sig("l2_h1_ready"), 1)
                act.wait_ge(*at("l2_h2_projected", n + 1))
                nc.scalar.activation(h2[:], bank(7), ACT.Gelu).then_inc(sig("l2_h2_ready"), 1)

            q_bias(0)
            act.wait_ge(*at("gate_keys_projected", 1))
            for c in range(CH):
                last = nc.scalar.activation(z_t[:, c, :], ps[:, 2, c * P:(c + 1) * P], ACT.Identity,
                                            bias=cols[:, GATEB, c:c + 1])
            last.then_inc(sig("gate_keys_ready"), 1)
            act.wait_ge(*at("gate_max_ready", 1))
            nc.scalar.activation(gate8[:], ps[:, 5, 0:E], ACT.Exp, bias=small[:, 0:1], scale=D ** -0.5,
                                 accum_out=small[:, 1:2]).then_inc(sig("gate_exp_ready"), 1)
            with act.Fori(0, E // 2 - 1) as i:
                for u in range(2):
                    expert_act(i * 2 + u, True)
            expert_act(E - 2, True)
            expert_act(E - 1, False)

            layer_norm_t(6)
            for k in range(3):
                act.wait_ge(*at("gcn_h_projected", 2 * k + 1))
                nc.scalar.copy(ctxv[:, 0:D // 2], ps[:, 0, 0:D // 2]).then_inc(sig("gcn_h_ready0"), 1)
                if k < 2:
                    act.wait_ge(*at("gcn_mixed", 2 * k + 1))
                    for c in range(2):
                        last = nc.scalar.activation(z_t[:, c, :], ps[:, 1, c * P:(c + 1) * P], ACT.Relu,
                                                    bias=cols[:, GCNB1 + k, c:c + 1])
                    last.then_inc(sig("gcn_z_ready0"), 1)

            layer_norm_t(7)
            act.wait_ge(*at("router_max_ready", 1))
            nc.scalar.activation(gate8[:], gated[:], ACT.Exp, bias=small[:, 0:1]).then_inc(sig("router_exp_ready"), 1)

            def lstm_act(n):
                for j, (tile, bias, scale, first) in enumerate((
                        (prob[:, 0:4, :], lstm_hb, 0.5, 0), (prob[:, 4:8, :], lstm_b, 1.0, 8),
                        (prob_t[:, 0:4, :], lstm_hb, 0.5, 12))):
                    act.wait_ge(*at("l3_gates_projected", n * 3 + (j + 1)))
                    if j == 2:
                        act.wait_ge(*at("l3_h_ready", n + 1))
                    for c in range(CH):
                        last = nc.scalar.activation(tile[:, c, :], ps[:, j, c * P:(c + 1) * P], ACT.Tanh,
                                                    bias=bias[:, bass.ds(n * 16 + (first + c), 1)], scale=scale)
                    last.then_inc(sig("l3_gate_ready"), 1)
                act.wait_ge(*at("l3_cell_ready", n + 1))
                nc.scalar.activation(prob_t[:, 4:8, :].rearrange("p c n -> p (c n)"), t1[:], ACT.Tanh, scale=0.5) \
                    .then_inc(sig("l3_cell_tanh_ready"), 1)

            with act.Fori(0, E) as n:
                lstm_act(n)

        @block.tensor
        def _(pe):
            def weights(name):
                pe.wait_ge(*at(f"dense_landed{DENSE.index(name) % SLOTS}", landed[name]))

            def layer_norm_transpose(k):
                pe.wait_ge(*at("y_ready", k + 1))
                if k == 1:
                    for c in range(CH):
                        last = pe.matmul(ps[:, 2, c:c + 1], y[:, c * P:(c + 1) * P], ones[:, 0:1], start=True, stop=True)
                    last.then_inc(sig("route_summed"), 1)
                for c in range(CH):
                    last = pe.transpose(ps[:, 7, c * P:(c + 1) * P], y[:, c * P:(c + 1) * P], ident[:])
                last.then_inc(sig("y_transposed"), 1)
                pe.wait_ge(*at("y_t_ready", k + 1))

            def project(b, in_t, w, n=D):
                for c in range(CH):
                    last = pe.matmul(ps[:, b, 0:n], in_t[:, c, :], w[:, c, 0:n], start=(c == 0), stop=(c == CH - 1))
                return last

            def project_t(b, in_t, w, chunks=CH, first=0, n=P):
                for m in range(chunks):
                    for c in range(CH):
                        last = pe.matmul(ps[:, b, m * n:(m + 1) * n], w[:, c, (first + m) * P:(first + m + 1) * P],
                                         in_t[:, c, 0:n], start=(c == 0), stop=(c == CH - 1))
                return last

            def scores(done):
                for g in range(4):
                    for a in range(2):
                        r = slice(DH * a, DH * a + DH)
                        last = pe.matmul(ps[:, 3 + a, g * P:(g + 1) * P], qk_t[r, g, :], qk_t[r, CH + g, :],
                                         start=True, stop=True)
                        if g == 3:
                            last.then_inc(sig(done), 1)

            def transpose_half(ready, done, n, a, b):
                pe.wait_ge(*at(ready, n * 2 + (a + 1)))
                for g in range(4):
                    last = pe.transpose(ps[:, b, g * P:(g + 1) * P], prob[:, 4 * a + g, :], ident[:])
                last.then_inc(sig(done), 1)

            def attend(b, ready0, ready1, n):
                for a in range(2):
                    pe.wait_ge(*at((ready0, ready1)[a], n + 1))
                    for g in range(4):
                        h = 2 * g + a
                        last = pe.matmul(ps[DH * a:DH * a + DH, b, g * P:(g + 1) * P], v[:, h * DH:(h + 1) * DH],
                                         prob_t[:, 4 * a + g, :], start=True, stop=True)
                return last

            def transpose_rows(b, rows):
                for c in range(CH):
                    last = pe.transpose(ps[:, b, c * P:(c + 1) * P], rows[:, c * P:(c + 1) * P], ident[:])
                return last

            pe.wait_ge(*at("const_ready", 3))
            layer_norm_transpose(0)
            weights("l0_W")
            last = project(0, y_t, matrix("l0_W"))
            last.then_inc(sig("gat_h_projected"), 1)
            pe.wait_ge(*at("one_hot_ready", 2))
            for t in range(EDGES_PER_PARTITION):
                last = pe.matmul(ps[:, 5, 0:P], one_hot[:, 0, t, :], one_hot[:, 1, t, :],
                                 start=(t == 0), stop=(t == EDGES_PER_PARTITION - 1))
            last.then_inc(sig("edges_counted"), 1)
            pe.wait_ge(*at("gat_s_ready", 2))
            pe.transpose(ps[0:40, 1, 0:P], s_cat[:], ident[:]).then_inc(sig("gat_s_transposed"), 1)
            pe.wait_ge(*at("gat_lr_ready", 2))
            for a in range(2):
                last = pe.matmul(ps[:, 3 + a, :], gat_l[:], gat_r[:, 4 * a:4 * a + 4, :], start=True, stop=True)
            last.then_inc(sig("gat_scored"), 1)
            pe.wait_ge(*at("gat_prob_ready", 4))
            for h in range(H):
                if h >= 4:
                    pe.wait_ge(*at("gat_prob_ready", h + 1))
                last = pe.transpose(ps[:, 5 + h // 4, h % 4 * P:(h % 4 + 1) * P], prob[:, h, :], ident[:])
                if h % 4 == 3:
                    last.then_inc(sig("gat_prob_transposed"), 1)
            pe.wait_ge(*at("gat_h_ready", 1))
            for h in range(H):
                if h % 4 == 0:
                    pe.wait_ge(*at(f"gat_prob_t_ready{h // 4}", 1))
                last = pe.matmul(ps[:, 0, h * DH:(h + 1) * DH], prob_t[:, h, :], v[:, h * DH:(h + 1) * DH],
                                 start=True, stop=True)
            last.then_inc(sig("gat_attended"), 1)

            layer_norm_transpose(1)
            pe.wait_ge(*at("route_mean_ready", 1))
            pe.wait_ge(*at("router_landed", 64))
            for c in range(CH):
                last = pe.matmul(ps[:, 2, 8:9], r_w1[:, c, :], r_mean[:, c:c + 1], start=(c == 0), stop=(c == CH - 1))
            last.then_inc(sig("route_hidden_summed"), 1)
            pe.wait_ge(*at("route_hidden_ready", 1))
            pe.matmul(ps[0:1, 2, 16:19], r_hcol[:], r_w2[:], start=True, stop=True).then_inc(sig("route_logits_summed"), 1)
            pe.wait_ge(*at("counts_ready", 1))
            pe.transpose(ps[:, 5, 0:P], cnt_sd[:], ident[:]).then_inc(sig("counts_transposed"), 1)
            pe.wait_ge(*at("adjacency_ready", 2))
            pe.transpose(ps[:, 6, 0:P], mean_ds[:], ident[:])
            pe.transpose(ps[:, 6, P:2 * P], gcn_ds[:], ident[:]).then_inc(sig("adjacency_transposed"), 1)

            def selected_weights(name):
                pe.wait_ge(*at(f"gqa_{name}_landed", 16))
                k = ("wq", "wk", "wv", "wo").index(name)
                return ew[:, 0, k * CH * D:(k + 1) * CH * D].rearrange("p (c n) -> p c n", c=CH)

            project_t(0, y_t, selected_weights("wq")).then_inc(sig("gqa_q_projected"), 1)
            project_t(1, y_t, selected_weights("wk")).then_inc(sig("gqa_k_projected"), 1)
            pe.wait_ge(*at("gqa_q_ready", 1))
            pe.wait_ge(*at("gqa_k_ready", 1))
            scores("gqa_scored")
            project(2, y_t, selected_weights("wv")).then_inc(sig("gqa_v_projected"), 1)
            for a in range(2):
                transpose_half("gqa_prob_ready", "gqa_prob_transposed", 0, a, 5 + 2 * a)
            pe.wait_ge(*at("gqa_v_ready", 1))
            attend(4, "gqa_prob_t_ready0", "gqa_prob_t_ready1", 0).then_inc(sig("gqa_attended"), 1)
            pe.wait_ge(*at("gqa_ctx_t_ready", 1))
            project(6, ctx_t, selected_weights("wo")).then_inc(sig("gqa_o_projected"), 1)

            layer_norm_transpose(2)
            weights("perf_wq")
            project_t(0, y_t, matrix("perf_wq"))
            weights("perf_wk")
            project_t(3, y_t, matrix("perf_wk")).then_inc(sig("perf_qk_projected"), 1)
            pe.wait_ge(*at("perf_rows_ready", 1))
            weights("perf_wv")
            project(1, x1_t, matrix("perf_wv")).then_inc(sig("perf_v_projected"), 1)
            pe.wait_ge(*at("perf_t_ready", 1))
            pe.wait_ge(*at("params_landed", 48))
            for w in (1, 0):
                for g in range(4):
                    last = pe.matmul(ps[:, 4 + 2 * w + g // 2, (g % 2) * PERF_M:(g % 2 + 1) * PERF_M],
                                     qk_t[:, 4 * w + g, :], proj_t[:], start=True, stop=True)
                last.then_inc(sig("perf_u_ready"), 1)
            pe.wait_ge(*at("perf_kmax_ready", 1))
            pe.transpose(ps[0:4, 2, P:2 * P], small[:, 4:8], ident[:]).then_inc(sig("perf_kmax_transposed"), 1)
            pe.wait_ge(*at("perf_sq_ready", 1))
            for s in range(8):
                last = pe.matmul(ps[:, 0, s:s + 1], prob[:, s, :], ones[:, 0:1], start=True, stop=True)
            last.then_inc(sig("perf_diag_summed"), 1)
            pe.wait_ge(*at("perf_kmax_rows_ready", 1))
            pe.matmul(ps[:, 2, 2 * P:2 * P + 4], perf_r[:].rearrange("g a n -> g (a n)"), ident[0:4, 0:4],
                      start=True, stop=True).then_inc(sig("perf_kmax_spread"), 1)
            pe.wait_ge(*at("bn_out_ready", 1))
            weights("conv")
            project(3, z_t, matrix("conv")).then_inc(sig("conv_h_projected"), 1)
            pe.wait_ge(*at("perf_features_ready", 1))
            for g in range(4):
                for m in range(2):
                    s = 2 * g + m
                    last = pe.transpose(ps[:, 4 + s // 4, s % 4 * P:(s % 4 + 1) * P],
                                        wide[:, 0, g * PERF_M + m * P:g * PERF_M + (m + 1) * P], ident[:])
            last.then_inc(sig("perf_q_transposed"), 1)
            pe.wait_ge(*at("conv_h_ready", 1))
            pe.wait_ge(*at("mean_sd_ready", 1))
            for c in range(CH):
                last = pe.matmul(ps[:, 3, c * P:(c + 1) * P], ctxv[:, c * P:(c + 1) * P], mean_sd[:],
                                 start=True, stop=True)
            last.then_inc(sig("conv_mixed"), 1)
            pe.wait_ge(*at("perf_features_ready", 2))
            pe.wait_ge(*at("perf_v_ready", 1))
            pair = 2 * (DH + 1)
            for m in range(2):
                for g in range(4):
                    if m + g == 0:
                        pe.wait_ge(*at("conv_t_ready", 1))
                    last = pe.matmul(ps[:, 2 * m + g // 2, g % 2 * pair:(g % 2 + 1) * pair],
                                     wide[:, 1, g * PERF_M + m * P:g * PERF_M + (m + 1) * P], pair_v[:, g],
                                     start=True, stop=True)
            last.then_inc(sig("perf_kv_done"), 1)
            pe.wait_ge(*at("perf_kv_ready", 2))
            pe.wait_ge(*at("perf_kv_ready_act", 2))
            pe.wait_ge(*at("perf_q_t_ready0", 1))
            pe.wait_ge(*at("perf_q_t_ready1", 1))
            for g in range(4):
                for m in range(2):
                    last = pe.matmul(ps[:, 6 + g // 2, g % 2 * pair:(g % 2 + 1) * pair], prob_t[:, 2 * g + m, :],
                                     kv_sb[:, 2 * m + g // 2, g % 2 * pair:(g % 2 + 1) * pair],
                                     start=(m == 0), stop=(m == 1))
            last.then_inc(sig("perf_attended"), 1)
            pe.wait_ge(*at("perf_ctx_ready", 1))
            for a in range(2):
                r = slice(DH * a, DH * a + DH)
                for g in range(4):
                    last = pe.matmul(ps[r, a, g * PERF_N:(g + 1) * PERF_N], ctxv[r, g * DH:(g + 1) * DH], ident[r, r],
                                     start=True, stop=True)
            last.then_inc(sig("perf_ctx_transposed"), 1)
            pe.wait_ge(*at("perf_ctx_t_ready", 1))
            weights("perf_wo")
            project_t(3, x1_t, matrix("perf_wo")).then_inc(sig("perf_o_projected"), 1)
            pe.wait_ge(*at("bn_out_ready", 2))
            for c in range(CH):
                last = pe.transpose(ps[:, 2, c * P:(c + 1) * P], z_t[:, c, :], ident[:])
            last.then_inc(sig("gps_out_transposed"), 1)

            layer_norm_transpose(3)
            weights("peer_wq")
            project_t(0, y_t, matrix("peer_wq")).then_inc(sig("peer_q_projected"), 1)
            pe.wait_ge(*at("peer_q_ready", 1))
            pe.wait_ge(*at("late_params_landed", 160))
            for r in range(4):
                rows = slice(32 * r, 32 * r + 32)
                for q in range(2):
                    last = pe.matmul(ps[:, 1 + r, q * KEYS:(q + 1) * KEYS], qk_t[rows, q, :], keys_t[rows, q, :],
                                     start=True, stop=True, tile_position=(32 * r, 0))
                last.then_inc(sig("peer_sim_ready"), 1)
            weights("peer_tables")
            for m in range(2):
                for c in range(CH):
                    last = pe.matmul(ps[:, 5, m * P:(m + 1) * P], peer_down[:, c, m * P:(m + 1) * P], qk_t[:, c, :],
                                     start=(c == 0), stop=(c == CH - 1))
            last.then_inc(sig("peer_down_projected"), 1)
            for h in range(H):
                pe.wait_ge(*at("peer_masked", h + 1))
                pe.wait_ge(*at("peer_diag_ready", h + 1))
                for m in range(2):
                    last = pe.matmul(ps[:, 6 + m, 0:P], peer_pick[:, h % 4, m * P:(m + 1) * P], x1_t[:, h % 2, :],
                                     start=(h == 0), stop=(h == H - 1))
                last.then_inc(sig("peer_head_added"), 1)
            pe.wait_ge(*at("peer_weights_ready", 1))
            for m in range(2):
                last = pe.matmul(bank(0), z_t[:, m, :], peer_up[:, m, :], start=(m == 0), stop=(m == 1))
            last.then_inc(sig("peer_up_projected"), 1)

            layer_norm_transpose(4)
            weights("exph_wq")
            project_t(0, y_t, matrix("exph_wq")).then_inc(sig("exph_q_projected"), 1)
            weights("exph_wk")
            project_t(1, y_t, matrix("exph_wk")).then_inc(sig("exph_k_projected"), 1)
            pe.wait_ge(*at("exph_q_ready", 1))
            pe.wait_ge(*at("exph_k_ready", 1))
            for a in range(2):
                r = slice(DH * a, DH * a + DH)
                for g in range(4):
                    last = pe.matmul(ps[:, 3 + a, g * P:(g + 1) * P], qk_t[r, CH + g, :], qk_t[r, g, :],
                                     start=True, stop=True)
                last.then_inc(sig("exph_scored"), 1)
            weights("exph_wv")
            project(2, y_t, matrix("exph_wv")).then_inc(sig("exph_v_projected"), 1)
            pe.wait_ge(*at("exph_v_ready", 1))
            for a in range(2):
                pe.wait_ge(*at("exph_weights_ready", a + 1))
                for g in range(4):
                    last = pe.matmul(ps[:, 5 + a, g * (DH + 1):(g + 1) * (DH + 1)], prob_t[:, 4 * a + g, :],
                                     heads_v[:, 2 * g + a, :], start=True, stop=True)
            last.then_inc(sig("exph_attended"), 1)
            pe.wait_ge(*at("exph_h_ready", 1))
            transpose_rows(0, ctxv).then_inc(sig("exph_h_transposed"), 1)
            pe.wait_ge(*at("bn_out_ready", 3))
            for c in range(CH):
                last = pe.transpose(ps[:, 1, c * P:(c + 1) * P], z_t[:, c, :], ident[:])
            last.then_inc(sig("exph_out_transposed"), 1)

            layer_norm_transpose(5)

            def expert_q(n, u, it):
                pe.wait_ge(*at(f"l2_wqk_landed{u}", it * 16 + 16))
                project_t(0, y_t, l2_wqk(u)).then_inc(sig("l2_qk_projected"), 1)

            def expert_k(u, parts):
                for m in parts:
                    for c in range(CH):
                        last = pe.matmul(ps[:, 1, m * P:(m + 1) * P], l2_wqk(u)[:, c, (CH + m) * P:(CH + m + 1) * P],
                                         y_t[:, c, :], start=(c == 0), stop=(c == CH - 1))
                if m == CH - 1:
                    last.then_inc(sig("l2_qk_projected"), 1)

            def expert_v(u, parts):
                for c in parts:
                    last = pe.matmul(bank(2), y_t[:, c, :], l2_wv(u)[:, c, :], start=(c == 0), stop=(c == CH - 1))
                if c == CH - 1:
                    last.then_inc(sig("l2_v_projected"), 1)

            def expert_scores(n):
                pe.wait_ge(*at("l2_q_ready", n + 1))
                pe.wait_ge(*at("l2_k_ready", n + 1))
                scores("l2_scored")

            def expert_pe(n, u, it, next_it, has_next):
                if has_next:
                    expert_q(n + 1, 1 - u, next_it)
                for a in range(2):
                    if has_next:
                        expert_k(1 - u, (a,))
                    transpose_half("l2_prob_ready", "l2_prob_transposed", n, a, 5 + a)
                if has_next:
                    expert_k(1 - u, (2,))
                pe.wait_ge(*at("l2_v_ready", n + 1))
                pe.wait_ge(*at("l2_h2_ready", n + 1))
                attend(7, "l2_prob_t_ready0", "l2_prob_t_ready1", n).then_inc(sig("l2_attended"), 1)
                if has_next:
                    expert_k(1 - u, (3,))
                pe.wait_ge(*at("l2_ctx_t_ready", n + 1))
                pe.wait_ge(*at(f"l2_wo_landed{u}", it * 16 + 16))
                project(4, ctx_t, wo_of(u)).then_inc(sig("l2_o_projected"), 1)
                if has_next:
                    pe.wait_ge(*at(f"l2_wv_landed{1 - u}", next_it * 16 + 16))
                    expert_v(1 - u, range(CH - 1))
                for c in range(CH):
                    if c % 2 == 0:
                        pe.wait_ge(*at("l2_x1_ready", n * 2 + (c // 2 + 1)))
                    last = pe.transpose(ps[:, 5, c * P:(c + 1) * P], x1[:, c * P:(c + 1) * P], ident[:])
                last.then_inc(sig("l2_x1_transposed"), 1)
                if has_next:
                    expert_v(1 - u, (CH - 1,))
                pe.wait_ge(*at("l2_x1_t_ready", n + 1))
                pe.wait_ge(*at(f"l2_small_landed{u}", it * 32 + 32))
                for c in range(CH):
                    last = pe.matmul(ps[0:F2, 6, 0:P], ew1[:, u, c, :], x1_t[:, c, :], start=(c == 0), stop=(c == CH - 1))
                last.then_inc(sig("l2_h1_projected"), 1)
                if has_next:
                    expert_scores(n + 1)
                pe.wait_ge(*at("l2_h1_ready", n + 1))
                pe.matmul(bank(7), h1_t[:], ew2[:, u, :], start=True, stop=True).then_inc(sig("l2_h2_projected"), 1)

            expert_q(0, 0, 0)
            weights("gate_wk")
            project_t(2, y_t, matrix("gate_wk")).then_inc(sig("gate_keys_projected"), 1)
            expert_k(0, range(CH))
            pe.wait_ge(*at("gate_keys_ready", 1))
            for c in range(CH):
                last = pe.matmul(ps[:, 5, 0:E], z_t[:, c, :], eq_t[:, c, :], start=(c == 0), stop=(c == CH - 1))
            last.then_inc(sig("gate_scored"), 1)
            expert_scores(0)
            pe.wait_ge(*at("l2_wv_landed0", 16))
            expert_v(0, range(CH))
            pe.wait_ge(*at("gated_ready", 1))
            pe.transpose(ps[0:E, 7, 0:P], gated[:], ident[:]).then_inc(sig("gated_transposed"), 1)
            pe.wait_ge(*at("gated_t_ready", 1))
            pe.matmul(bank(7), gated_t[:], be2[:], start=True, stop=True).then_inc(sig("be2_shared"), 1)
            with pe.Fori(0, E // 2 - 1) as i:
                for u in range(2):
                    expert_pe(i * 2 + u, u, i, i + u, True)
            expert_pe(E - 2, 0, E // 2 - 1, E // 2 - 1, True)
            expert_pe(E - 1, 1, E // 2 - 1, None, False)

            layer_norm_transpose(6)
            pe.wait_ge(*at("gcn_sd_ready", 1))
            for k in range(3):
                weights(f"gcn_w{k + 1}")
                for half in range(2):
                    for c in range(CH):
                        if k and half == 0 and c % 2 == 0:
                            pe.wait_ge(*at(f"gcn_z_ready{c // 2}", k))
                        last = pe.matmul(ps[:, 2 * half, 0:D // 2], (z_t if k else y_t)[:, c, :],
                                         matrix(f"gcn_w{k + 1}")[:, c, half * D // 2:(half + 1) * D // 2],
                                         start=(c == 0), stop=(c == CH - 1))
                    last.then_inc(sig("gcn_h_projected"), 1)
                for half in range(2):
                    pe.wait_ge(*at(f"gcn_h_ready{half}", k + 1))
                    if k < 2:
                        for c in range(2):
                            last = pe.matmul(ps[:, 1 + 2 * half, c * P:(c + 1) * P],
                                             ctxv[:, (2 * half + c) * P:(2 * half + c + 1) * P], gcn_sd[:],
                                             start=True, stop=True)
                    else:
                        last = pe.matmul(ps[:, 1 + 2 * half, 0:D // 2], gcn_sd[:], ctxv[:, half * D // 2:(half + 1) * D // 2],
                                         start=True, stop=True)
                    last.then_inc(sig("gcn_mixed"), 1)

            layer_norm_transpose(7)
            def lstm_gates(n, u, it, gates=range(3)):
                for j in gates:
                    w, first, landed_by = ((l3_wi(u), 0, "l3_wi_landed"), (l3_wgo(u), 0, "l3_wgo_landed"),
                                           (l3_wgo(u), CH, "l3_wgo_landed"))[j]
                    if j < 2:
                        pe.wait_ge(*at(f"{landed_by}{u}", it * 16 + 16))
                    if not isinstance(n, int) or n > 0:
                        pe.wait_ge(*at("l3_gate_ready", n * 3 + (j - 2)))
                    project_t(j, y_t, w, first=first).then_inc(sig("l3_gates_projected"), 1)

            def lstm_out(n, u, it):
                pe.wait_ge(*at("l3_h_ready", n + 2))
                pe.wait_ge(*at(f"l3_wo_landed{u}", it * 16 + 16))
                if not isinstance(n, int) or n > 0:
                    pe.wait_ge(*at("l3_expert_added", n))
                project(3 + u, h_t[u], wo_of(u)).then_inc(sig("l3_o_projected"), 1)

            lstm_gates(0, 0, 0, (0,))
            for c in range(CH):
                last = pe.matmul(ps[:, 6, 0:E], y_t[:, c, :], router_w[:, c, :], start=(c == 0), stop=(c == CH - 1))
            last.then_inc(sig("router_scored"), 1)
            lstm_gates(0, 0, 0, (1,))
            pe.wait_ge(*at("lstm_gated_ready", 1))
            pe.transpose(ps[0:E, 5, 0:P], gated[:], ident[:]).then_inc(sig("lstm_gated_transposed"), 1)
            lstm_gates(0, 0, 0, (2,))
            pe.wait_ge(*at("lstm_gated_t_ready", 1))
            pe.matmul(bank(7), gated_t[:], lstm_bo[:], start=True, stop=True).then_inc(sig("lstm_bo_shared"), 1)
            lstm_gates(1, 1, 0)
            lstm_out(0, 0, 0)
            with pe.Fori(1, E // 2) as i:
                for u in range(2):
                    lstm_gates(i * 2 + u, u, i)
                    lstm_out(i * 2 + (u - 1), 1 - u, i + (u - 1))
            lstm_out(E - 1, 1, E // 2 - 1)

        @block.vector
        def _(dve):
            settle = dve.drain

            def layer_norm(k):
                settle()
                dve.bn_stats(ln_st[:], x[:])
                settle()
                dve.bn_aggr(ln_mv[:], ln_st[:])
                settle()
                dve.tensor_scalar_add(ln_var[:], ln_mv[:, 1:2], EPS).then_inc(sig("ln_var_ready"), 1)
                dve.wait_ge(*at("ln_rstd_ready", k + 1))
                dve.tensor_scalar(y[:], x[:], ln_mv[:, 0:1], ln_rstd[:], ALU.subtract, ALU.mult).then_inc(sig("y_ready"), 1)

            def batch_norm(k, in_t, gamma, beta):
                settle()
                for c in range(CH):
                    dve.bn_stats(bn_st[:, c, :], in_t[:, c, :])
                settle()
                for c in range(CH):
                    dve.bn_aggr(bn_mv[:, c, :], bn_st[:, c, :])
                settle()
                dve.tensor_scalar_add(bn_var[:], bn_mv[:, :, 1], EPS).then_inc(sig("bn_var_ready"), 1)
                dve.tensor_tensor(bn_shift[:], bn_mv[:, :, 0], cols[:, gamma, :], ALU.mult)
                settle()
                dve.wait_ge(*at("bn_rstd_ready", k + 1))
                dve.tensor_tensor(bn_scale[:], bn_rstd[:], cols[:, gamma, :], ALU.mult)
                dve.tensor_tensor(bn_shift[:], bn_rstd[:], bn_shift[:], ALU.mult)
                settle()
                dve.tensor_tensor(bn_shift[:], cols[:, beta, :], bn_shift[:], ALU.subtract)
                settle()
                for c in range(CH):
                    last = dve.tensor_scalar(z_t[:, c, :], in_t[:, c, :], bn_scale[:, c:c + 1], bn_shift[:, c:c + 1],
                                             ALU.mult, ALU.add)
                last.then_inc(sig("bn_out_ready"), 1)

            def maxima(scored, done, n, scale):
                for a in range(2):
                    s = slice(4 * a, 4 * a + 4)
                    dve.wait_ge(*at(scored, n * 2 + (a + 1)))
                    dve.tensor_reduce(nmax[:, s], bank_chunks(3 + a), AX.X, ALU.max, negate=True)
                    settle()
                    dve.tensor_scalar(nmax_s[:, s], nmax[:, s], scale, None, ALU.mult).then_inc(sig(done), 1)

            def normalise(exps_done, done, n):
                for a in range(2):
                    s = slice(4 * a, 4 * a + 4)
                    dve.wait_ge(*at(exps_done, n * 2 + (a + 1)))
                    dve.reciprocal(rinv[:, s], rsum[:, s])
                    settle()
                    dve.tensor_tensor(prob[:, s, :], prob[:, s, :], rinv[:, s].unsqueeze(2).broadcast_to([P, 4, P]),
                                      ALU.mult).then_inc(sig(done), 1)

            dve.memset(s_cat[:], 0.0)
            dve.memset(gat_l[:], 0.0)
            dve.memset(h1_t[:], 1.0)
            settle()
            dve.memset(gat_l[32:40], 1.0)
            dve.wait_ge(*at("x_landed", 16))
            layer_norm(0)
            dve.wait_ge(*at("edges_landed", 32))
            dve.wait_ge(*at("iota_ready", 1))
            dve.tensor_copy(src_f[:], src_i[:])
            dve.tensor_copy(dst_f[:], dst_i[:])
            dve.tensor_copy(iota_f[:], iota_i[:])
            settle()
            for k, ends in enumerate((src_f, dst_f)):
                dve.tensor_tensor(one_hot[:, k, :, :],
                                  iota_f[:].unsqueeze(1).broadcast_to([P, EDGES_PER_PARTITION, P]),
                                  ends[:].unsqueeze(2).broadcast_to([P, EDGES_PER_PARTITION, P]),
                                  ALU.is_equal).then_inc(sig("one_hot_ready"), 1)
            dve.wait_ge(*at("gat_h_projected", 1))
            dve.wait_ge(*at("gat_a_landed", 16))
            for k in range(2):
                dve.tensor_tensor(wide[:, k, 0:D], bank(0), attn_a[:, k, :], ALU.mult)
            settle()
            for k in range(2):
                dve.tensor_reduce(s_cat[:, 32 * k:32 * k + H], wide[:, k, 0:D].rearrange("p (h d) -> p h d", h=H),
                                  AX.X, ALU.add).then_inc(sig("gat_s_ready"), 1)
            settle()
            dve.memset(small[:, 2:3], 0.0).then_inc(sig("gat_a_used"), 1)
            dve.wait_ge(*at("gat_s_transposed", 1))
            dve.tensor_copy(gat_l[0:H], ps[0:H, 1, 0:P]).then_inc(sig("gat_lr_ready"), 1)
            dve.wait_ge(*at("gat_r_ready", 2))
            dve.tensor_tensor(gat_r[32:32 + H], gat_r[32:32 + H],
                              ps[32:32 + H, 1, 0:P].unsqueeze(1).broadcast_to([H, H, P]), ALU.mult) \
                .then_inc(sig("gat_lr_ready"), 1)
            dve.wait_ge(*at("edges_counted", 1))
            dve.wait_ge(*at("const_ready", 3))
            dve.tensor_copy(cnt_sd[:], ps[:, 5, 0:P]).then_inc(sig("counts_ready"), 1)
            dve.tensor_tensor(gat_cap[:], ps[:, 5, 0:P], ident[:], ALU.add)
            settle()
            dve.tensor_scalar(gat_cap[:], gat_cap[:], 1.0, -2.0 * GAT_NEG, ALU.min, ALU.mult)
            settle()
            dve.tensor_scalar(gat_cap[:], gat_cap[:], GAT_NEG, None, ALU.add)
            settle()
            for a in range(2):
                s = slice(4 * a, 4 * a + 4)
                dve.wait_ge(*at("gat_leak_ready", a + 1))
                dve.tensor_tensor(prob[:, s, :].rearrange("p h n -> p (h n)"), bank(3 + a), wide[:, a, 0:512], ALU.max)
                settle()
                dve.tensor_tensor(prob[:, s, :], prob[:, s, :], gat_cap[:].unsqueeze(1).broadcast_to([P, 4, P]), ALU.min)
                settle()
                dve.tensor_reduce(nmax[:, s], prob[:, s, :], AX.X, ALU.max, negate=True).then_inc(sig("gat_max_ready"), 1)
            dve.wait_ge(*at("gat_prob_transposed", 1))
            dve.tensor_copy(prob_t[:, 0:4, :].rearrange("p h n -> p (h n)"), bank(5)).then_inc(sig("gat_prob_t_ready0"), 1)
            dve.wait_ge(*at("gat_prob_ready", 8))
            dve.reciprocal(rinv[:], rsum[:])
            settle()
            dve.wait_ge(*at("gat_attended", 1))
            dve.tensor_tensor(ctxv[:].rearrange("p (h d) -> p h d", h=H), bank_heads(0),
                              rinv[:].unsqueeze(2).broadcast_to([P, H, DH]), ALU.mult)
            settle()
            dve.tensor_reduce(small[:, 0:1], ctxv[:], AX.X, ALU.max, negate=True).then_inc(sig("gat_out_ready"), 1)
            dve.wait_ge(*at("gat_exp_ready", 1))
            dve.reciprocal(small[:, 2:3], small[:, 1:2])
            settle()
            dve.scalar_tensor_tensor(x[:], t1[:], small[:, 2:3], x[:], ALU.mult, ALU.add).then_inc(sig("x_updated"), 1)

            layer_norm(1)
            dve.memset(r_p[0:1, 3:8], -1.0)
            dve.wait_ge(*at("route_summed", 1))
            dve.tensor_scalar(r_mean[:], ps[:, 2, 0:CH], 1.0 / P, None, ALU.mult).then_inc(sig("route_mean_ready"), 1)
            dve.wait_ge(*at("router_landed", 64))
            dve.wait_ge(*at("route_hidden_summed", 1))
            dve.tensor_scalar(r_hcol[:], ps[:, 2, 8:9], r_b1[:], 0.0, ALU.add, ALU.max).then_inc(sig("route_hidden_ready"), 1)
            dve.wait_ge(*at("route_logits_summed", 1))
            dve.tensor_tensor(r_p[0:1, 0:3], ps[0:1, 2, 16:19], r_b2[:], ALU.add)
            settle()
            dve.tensor_reduce(small[0:1, 0:1], r_p[0:1, 0:3], AX.X, ALU.max, negate=True) \
                .then_inc(sig("route_logits_ready"), 1)
            dve.wait_ge(*at("route_exp_ready", 1))
            dve.reciprocal(small[0:1, 2:3], small[0:1, 1:2])
            settle()
            dve.tensor_scalar(r_p[0:1, 0:3], r_p[0:1, 0:3], small[0:1, 2:3], None, ALU.mult)
            settle()
            dve.max(r_top[:], r_p[0:1, :])
            settle()
            dve.max_index(selected[:], r_top[:], r_p[0:1, :]).then_inc(sig("route_selected"), 1)
            dve.wait_ge(*at("counts_transposed", 1))
            dve.tensor_reduce(deg_col[:], ps[:, 5, 0:P], AX.X, ALU.add)
            dve.tensor_tensor(gcn_ds[:], ps[:, 5, 0:P], ident[:], ALU.add)
            settle()
            dve.tensor_scalar(mean_col[:], deg_col[:], 1.0, None, ALU.max)
            dve.tensor_scalar(deg_col[:], deg_col[:], 1.0, None, ALU.add).then_inc(sig("gcn_deg_ready"), 1)
            settle()
            dve.reciprocal(mean_col[:], mean_col[:])
            settle()
            dve.tensor_scalar(mean_ds[:], ps[:, 5, 0:P], mean_col[:], None, ALU.mult).then_inc(sig("adjacency_ready"), 1)
            dve.wait_ge(*at("gcn_dis_ready", 1))
            dve.tensor_scalar(gcn_ds[:], gcn_ds[:], dis_col[:], None, ALU.mult).then_inc(sig("adjacency_ready"), 1)
            dve.wait_ge(*at("adjacency_transposed", 1))
            dve.tensor_copy(mean_sd[:], ps[:, 6, 0:P]).then_inc(sig("mean_sd_ready"), 1)
            dve.tensor_scalar(gcn_sd[:], ps[:, 6, P:2 * P], dis_col[:], None, ALU.mult).then_inc(sig("gcn_sd_ready"), 1)
            dve.wait_ge(*at("gqa_k_projected", 1))
            dve.tensor_copy(qk_t[:, CH:, :].rearrange("p c n -> p (c n)"), bank(1)).then_inc(sig("gqa_k_ready"), 1)
            maxima("gqa_scored", "gqa_max_ready", 0, DH ** -0.5)
            normalise("gqa_exps_ready", "gqa_prob_ready", 0)
            dve.wait_ge(*at("gqa_v_projected", 1))
            dve.tensor_copy(v[:, 0:D], bank(2)).then_inc(sig("gqa_v_ready"), 1)
            dve.wait_ge(*at("gqa_prob_transposed", 1))
            dve.tensor_copy(prob_t[:, 0:4, :].rearrange("p h n -> p (h n)"), bank(5)).then_inc(sig("gqa_prob_t_ready0"), 1)
            dve.wait_ge(*at("gqa_attended", 1))
            dve.memset(v[:], 0.0)
            settle()
            for a in range(2):
                last = dve.memset(pair_v[DH * a:DH * a + DH, :, a, DH:DH + 1], 1.0)
            last.then_inc(sig("v_cleared"), 1)
            dve.wait_ge(*at("gqa_o_projected", 1))
            dve.tensor_tensor(x[:], x[:], bank(6), ALU.add).then_inc(sig("x_updated"), 1)

            layer_norm(2)
            dve.memset(qk_t[:], 0.0)
            dve.wait_ge(*at("y_t_ready", 3))
            dve.tensor_copy(x1_t[:].rearrange("p c (a n) -> p c a n", a=2),
                            y_t[:, :, 0:PERF_N].unsqueeze(2).broadcast_to([P, CH, 2, PERF_N])).then_inc(sig("perf_rows_ready"), 1)
            dve.wait_ge(*at("params_landed", 48))
            batch_norm(0, y_t, N1G, N1B)
            dve.wait_ge(*at("perf_qk_projected", 1))
            for a in range(2):
                r = slice(DH * a, DH * a + DH)
                for w in range(2):
                    last = dve.tensor_scalar(qk_t[r, CH * w:CH * w + CH, PERF_N * a:PERF_N * (a + 1)],
                                             ps[r, 3 * w, :].rearrange("p (s n) -> p s n", s=CH)[:, :, 0:PERF_N],
                                             DH ** -0.25, None, ALU.mult)
                last.then_inc(sig("perf_t_scaled"), 1)
            settle()
            dve.memset(small[:, 3:4], 0.0).then_inc(sig("perf_t_ready"), 1)
            dve.tensor_tensor(prob[:], qk_t[:], qk_t[:], ALU.mult).then_inc(sig("perf_sq_ready"), 1)
            for w in (1, 0):
                dve.wait_ge(*at("perf_u_ready", 2 - w))
                dve.tensor_reduce(small[:, 4:8] if w else small[:, 8:12],
                                  ps[:, 4 + 2 * w:6 + 2 * w, :].rearrange("p b (g m) -> p (b g) m", m=PERF_M),
                                  AX.X, ALU.max).then_inc(sig("perf_kmax_ready" if w else "perf_qmax_ready"), 1)
            dve.wait_ge(*at("perf_kmax_transposed", 1))
            dve.tensor_reduce(perf_k2[:], ps[0:4, 2, P:2 * P].rearrange("g (a n) -> g a n", a=2), AX.X, ALU.max)
            settle()
            dve.tensor_copy(perf_r[:], perf_k2[:].unsqueeze(2).broadcast_to([4, 2, PERF_N])) \
                .then_inc(sig("perf_kmax_rows_ready"), 1)
            dve.wait_ge(*at("perf_diag_summed", 1))
            dve.scalar_tensor_tensor(small[:, 16:20], ps[:, 0, 0:4], -0.5, small[:, 8:12], ALU.mult, ALU.subtract) \
                .then_inc(sig("perf_bias_ready0"), 1)
            dve.wait_ge(*at("perf_kmax_spread", 1))
            dve.tensor_copy(small[:, 12:16], ps[:, 2, 2 * P:2 * P + 4])
            settle()
            dve.scalar_tensor_tensor(small[:, 20:24], ps[:, 0, 4:8], -0.5, small[:, 12:16], ALU.mult, ALU.subtract) \
                .then_inc(sig("perf_bias_ready1"), 1)
            for w in range(2):
                dve.wait_ge(*at("perf_exp_ready", w + 1))
                dve.tensor_scalar(wide[:, w, :], wide[:, w, :], PERF_M ** -0.5, PERF_EPS, ALU.mult, ALU.add) \
                    .then_inc(sig("perf_features_ready"), 1)
            dve.wait_ge(*at("perf_q_transposed", 1))
            dve.tensor_copy(prob_t[:, 0:4, :].rearrange("p h n -> p (h n)"), bank(4)).then_inc(sig("perf_q_t_ready0"), 1)
            dve.wait_ge(*at("conv_t_ready", 1))
            dve.tensor_tensor(ctx_t[:], ctx_t[:], y_t[:], ALU.add)
            dve.wait_ge(*at("perf_kv_done", 1))
            for b in (0, 2):
                dve.tensor_copy(kv_sb[:, b, :], ps[:, b, 0:4 * (DH + 1)]).then_inc(sig("perf_kv_ready"), 1)
            dve.wait_ge(*at("perf_attended", 1))
            halves = [slice(DH * a, DH * a + DH) for a in range(2)]
            num = [ps[r, 6:8, 0:4 * (DH + 1)].rearrange("p b (g a e) -> p b g a e", g=2, a=2)[:, :, :, a, :]
                   for a, r in enumerate(halves)]
            for a, r in enumerate(halves):
                dve.tensor_scalar(small[r, 24:28].rearrange("p (b g) -> p b g", b=2), num[a][:, :, :, DH], PERF_EPS, None,
                                  ALU.add)
            settle()
            dve.reciprocal(small[:, 24:28], small[:, 24:28])
            settle()
            for a, r in enumerate(halves):
                last = dve.tensor_tensor(
                    ctxv[r, 0:4 * DH].rearrange("p (b g d) -> p b g d", b=2, g=2), num[a][:, :, :, 0:DH],
                    small[r, 24:28].rearrange("p (b g) -> p b g", b=2).unsqueeze(3).broadcast_to([DH, 2, 2, DH]), ALU.mult)
            last.then_inc(sig("perf_ctx_ready"), 1)
            dve.wait_ge(*at("perf_ctx_transposed", 1))
            for a, r in enumerate(halves):
                pt = ps[r, a, 0:CH * PERF_N].rearrange("p (c n) -> p c n", c=CH)
                dve.tensor_copy(x1_t[r, :, 0:PERF_N], pt)
                last = dve.tensor_copy(x1_t[r, :, PERF_N:P], pt[:, :, PERF_N - 1:PERF_N].broadcast_to([DH, CH, P - PERF_N]))
            last.then_inc(sig("perf_ctx_t_ready"), 1)
            dve.wait_ge(*at("perf_o_projected", 1))
            dve.tensor_tensor(ctx_t[:].rearrange("p c n -> p (c n)"), ctx_t[:].rearrange("p c n -> p (c n)"), bank(3), ALU.add)
            batch_norm(1, ctx_t, N2G, N2B)
            dve.wait_ge(*at("gps_out_transposed", 1))
            dve.tensor_tensor(x[:], x[:], bank(2), ALU.add).then_inc(sig("x_updated"), 1)

            layer_norm(3)
            dve.wait_ge(*at("peer_q_projected", 1))
            dve.tensor_scalar(qk_t[:, 0:CH, :].rearrange("p c n -> p (c n)"), bank(0), (1.0 + EPS) ** -0.5, None, ALU.mult) \
                .then_inc(sig("peer_q_ready"), 1)

            def top_keys(k):
                dve.wait_ge(*at("peer_sim_ready", k + 1))
                pair = [((2 * k + j) % 4, peer_work[:, j, :], ps[:, 1 + k, j * KEYS:(j + 1) * KEYS]) for j in range(2)]
                for b, work, sim in pair:
                    dve.max(topv[:, b, 0:8], sim)
                settle()
                for b, work, sim in pair:
                    dve.match_replace(work, topv[:, b, 0:8], sim, NEG)
                    dve.max_index(topi[:, b, 0:8], topv[:, b, 0:8], sim)
                settle()
                for b, work, sim in pair:
                    dve.max(topv[:, b, 8:16], work)
                settle()
                for b, work, sim in pair:
                    dve.max_index(topi[:, b, 8:16], topv[:, b, 8:16], work)
                settle()
                two = slice(2 * k % 4, 2 * k % 4 + 2)
                dve.tensor_copy(topif[:, two, :], topi[:, two, :]).then_inc(sig("peer_top_ready"), 1)

            def pick(k):
                two = slice(2 * k % 4, 2 * k % 4 + 2)
                pair = [((2 * k + j) % 4, peer_work[:, j, :], 2 * k + j) for j in range(2)]
                dve.wait_ge(*at("peer_all_ready", k + 1))
                for b, work, h in pair:
                    dve.max(best[:, b, 0:8], peer_all[:, b, :])
                settle()
                dve.tensor_scalar(negbest[:, two], best[:, two, 0], -1.0, None, ALU.mult).then_inc(sig("peer_best_ready"), 1)
                for b, work, h in pair:
                    dve.match_replace(work, best[:, b, 0:8], peer_all[:, b, :], NEG)
                settle()
                for b, work, h in pair:
                    dve.max(best[:, b, 8:16], work)
                settle()
                for b, work, h in pair:
                    dve.match_replace(peer_rest[:, b, :], best[:, b, 8:16], work, NEG)
                settle()
                for b, work, h in pair:
                    dve.wait_ge(*at("peer_exp_ready", h + 1))
                    if h >= 4:
                        dve.wait_ge(*at("peer_head_added", h - 3))
                    dve.scalar_tensor_tensor(peer_pick[:, b, :], peer_rest[:, b, :], NEG, peer_exp[:, b, :], ALU.is_equal,
                                             ALU.mult, accum_out=picksum[:, h:h + 1]).then_inc(sig("peer_masked"), 1)
                settle()
                dve.reciprocal(pickinv[:, 2 * k:2 * k + 2], picksum[:, 2 * k:2 * k + 2]).then_inc(sig("peer_inv_ready"), 1)

            top_keys(0)
            for k in range(1, H // 2):
                top_keys(k)
                pick(k - 1)
            pick(H // 2 - 1)
            dve.wait_ge(*at("peer_head_added", H))
            dve.wait_ge(*at("peer_gelu_ready", 1))
            for m in range(2):
                last = dve.tensor_tensor(z_t[:, m, :], ps[:, 6 + m, 0:P], x1_t[:, 2 + m, :], ALU.mult)
            last.then_inc(sig("peer_weights_ready"), 1)
            dve.wait_ge(*at("peer_up_projected", 1))
            dve.tensor_tensor(x[:], x[:], bank(0), ALU.add).then_inc(sig("x_updated"), 1)

            layer_norm(4)
            dve.memset(heads_v[:, :, DH:DH + 1], 1.0)
            dve.wait_ge(*at("exph_k_projected", 1))
            dve.tensor_copy(qk_t[:, CH:, :].rearrange("p c n -> p (c n)"), bank(1)).then_inc(sig("exph_k_ready"), 1)
            clip = 5.0 * DH ** 0.5
            for a in range(2):
                dve.wait_ge(*at("exph_scored", a + 1))
                dve.tensor_scalar(prob[:, 4 * a:4 * a + 4, :].rearrange("p h n -> p (h n)"), bank(3 + a), -clip, clip,
                                  ALU.max, ALU.min).then_inc(sig("exph_clipped"), 1)
            for a in range(2):
                s = slice(4 * a, 4 * a + 4)
                dve.wait_ge(*at("exph_exp_ready", a + 1))
                dve.tensor_tensor(prob_t[:, s, :], prob[:, s, :], cnt_sd[:].unsqueeze(1).broadcast_to([P, 4, P]), ALU.mult) \
                    .then_inc(sig("exph_weights_ready"), 1)
            dve.wait_ge(*at("exph_attended", 1))
            for a in range(2):
                num = ps[:, 5 + a, 0:4 * (DH + 1)].rearrange("p (g e) -> p g e", g=4)
                zz = small[:, 24 + 4 * a:28 + 4 * a]
                dve.tensor_scalar(zz, num[:, :, DH], 1e-6, None, ALU.add)
                settle()
                dve.reciprocal(zz, zz)
                settle()
                dve.tensor_tensor(hd[:, :, a, :], num[:, :, 0:DH], zz.unsqueeze(2).broadcast_to([P, 4, DH]), ALU.mult)
            settle()
            dve.tensor_tensor(ctxv[:], ctxv[:], y[:], ALU.add).then_inc(sig("exph_h_ready"), 1)
            dve.wait_ge(*at("exph_h_transposed", 1))
            dve.tensor_copy(ctx_t[:].rearrange("p c n -> p (c n)"), bank(0))
            batch_norm(2, ctx_t, BNG, BNB)
            dve.wait_ge(*at("exph_out_transposed", 1))
            dve.tensor_tensor(x[:], x[:], bank(1), ALU.add).then_inc(sig("x_updated"), 1)

            layer_norm(5)

            def top2():
                dve.max(gtop[:], gate8[:])
                settle()
                dve.max_index(gidx[:], gtop[:], gate8[:])
                settle()
                dve.tensor_copy(gidxf[:], gidx[:])
                settle()

            def k_bias(n):
                dve.wait_ge(*at("l2_qk_projected", n * 2 + 2))
                for c in range(CH):
                    last = dve.tensor_scalar(qk_t[:, CH + c, :], ps[:, 1, c * P:(c + 1) * P],
                                             bqk[:, bass.ds(n * 8 + (CH + c), 1)], None, ALU.add)
                last.then_inc(sig("l2_k_ready"), 1)

            def v_bias(n, u, it):
                dve.wait_ge(*at(f"l2_rows_landed{u}", it * 16 + 16))
                dve.wait_ge(*at("l2_v_projected", n + 1))
                dve.tensor_tensor(v[:, 0:D], bank(2), erows[:, u, BV, :], ALU.add).then_inc(sig("l2_v_ready"), 1)

            def statistics(rows):
                settle()
                dve.bn_stats(ln_st[:], rows[:])
                settle()
                dve.bn_aggr(ln_mv[:], ln_st[:])
                settle()
                dve.tensor_scalar_add(ln_var[:], ln_mv[:, 1:2], EPS).then_inc(sig("l2_var_ready"), 1)

            def probabilities(n):
                normalise("l2_exps_ready", "l2_prob_ready", n)
                dve.wait_ge(*at("l2_prob_transposed", n * 2 + 1))
                dve.tensor_copy(prob_t[:, 0:4, :].rearrange("p h n -> p (h n)"), bank(5)).then_inc(sig("l2_prob_t_ready0"), 1)

            def expert_dve(n, u, next_it, has_next):
                if has_next:
                    k_bias(n + 1)
                settle()
                dve.wait_ge(*at("l2_residual_ready", n + 1))
                dve.wait_ge(*at("l2_o_projected", n + 1))
                dve.tensor_tensor(t1[:], bank(4), erows[:, u, BO, :], ALU.add)
                statistics(t1)
                dve.scalar_tensor_tensor(x1[:], t1[:], ln_mv[:, 0:1], erows[:, u, G1, :], ALU.subtract, ALU.mult)
                settle()
                dve.wait_ge(*at("l2_rstd_ready", n * 2 + 1))
                for half in (slice(0, D // 2), slice(D // 2, D)):
                    dve.scalar_tensor_tensor(x1[:, half], x1[:, half], ln_rstd[:], erows[:, u, BE1, half], ALU.mult,
                                             ALU.add).then_inc(sig("l2_x1_ready"), 1)
                if has_next:
                    v_bias(n + 1, 1 - u, next_it)
                    maxima("l2_scored", "l2_max_ready", n + 1, DH ** -0.5)
                dve.wait_ge(*at("l2_h2_ready", n + 2))
                dve.tensor_tensor(t1[:], x1[:], h2[:], ALU.add)
                statistics(t1)
                if has_next:
                    probabilities(n + 1)
                dve.scalar_tensor_tensor(t1[:], t1[:], ln_mv[:, 0:1], erows[:, u, G2, :], ALU.subtract, ALU.mult)
                dve.wait_ge(*at("l2_rstd_ready", n * 2 + 2))
                dve.tensor_tensor(rg[:], ln_rstd[:], gated[:, bass.ds(n, 1)], ALU.mult)
                settle()
                dve.scalar_tensor_tensor(acc[:], t1[:], rg[:], acc[:], ALU.mult, ALU.add).then_inc(sig("l2_expert_added"), 1)

            k_bias(0)
            dve.wait_ge(*at("gate_scored", 1))
            dve.tensor_reduce(small[:, 2:3], ps[:, 5, 0:E], AX.X, ALU.max, negate=True)
            settle()
            dve.tensor_scalar(small[:, 0:1], small[:, 2:3], D ** -0.5, None, ALU.mult).then_inc(sig("gate_max_ready"), 1)
            maxima("l2_scored", "l2_max_ready", 0, DH ** -0.5)
            dve.wait_ge(*at("gate_exp_ready", 1))
            dve.reciprocal(small[:, 2:3], small[:, 1:2])
            settle()
            dve.tensor_scalar(gate8[:], gate8[:], small[:, 2:3], None, ALU.mult)
            settle()
            top2()
            dve.tensor_scalar(gated[:], iota_f[:, 0:E], gidxf[:, 0:1], gtop[:, 0:1], ALU.is_equal, ALU.mult)
            dve.tensor_scalar(small[:, 8:16], iota_f[:, 0:E], gidxf[:, 1:2], gtop[:, 1:2], ALU.is_equal, ALU.mult)
            dve.tensor_tensor(small[:, 4:5], gtop[:, 0:1], gtop[:, 1:2], ALU.add)
            settle()
            dve.tensor_scalar(small[:, 4:5], small[:, 4:5], 1e-9, None, ALU.add)
            dve.tensor_tensor(gated[:], gated[:], small[:, 8:16], ALU.add)
            settle()
            dve.reciprocal(small[:, 4:5], small[:, 4:5])
            settle()
            dve.tensor_scalar(gated[:], gated[:], small[:, 4:5], None, ALU.mult).then_inc(sig("gated_ready"), 1)
            dve.wait_ge(*at("gated_transposed", 1))
            dve.tensor_copy(gated_t[:], ps[0:E, 7, 0:P]).then_inc(sig("gated_t_ready"), 1)
            dve.wait_ge(*at("be2_shared", 1))
            dve.tensor_copy(acc[:], bank(7)).then_inc(sig("l2_h2_ready"), 1)
            v_bias(0, 0, 0)
            probabilities(0)
            with dve.Fori(0, E // 2 - 1) as i:
                for u in range(2):
                    expert_dve(i * 2 + u, u, i + u, True)
            expert_dve(E - 2, 0, E // 2 - 1, True)
            expert_dve(E - 1, 1, None, False)
            settle()
            dve.tensor_tensor(x[:], x[:], acc[:], ALU.add).then_inc(sig("x_updated"), 1)

            layer_norm(6)
            dve.tensor_tensor(x[:], x[:], gcn_b3[:], ALU.add)
            for k in range(3):
                dve.wait_ge(*at("gcn_h_projected", 2 * k + 2))
                dve.tensor_copy(ctxv[:, D // 2:], ps[:, 2, 0:D // 2]).then_inc(sig("gcn_h_ready1"), 1)
                if k < 2:
                    dve.wait_ge(*at("gcn_mixed", 2 * k + 2))
                    for c in range(2):
                        last = dve.tensor_scalar(z_t[:, 2 + c, :], ps[:, 3, c * P:(c + 1) * P],
                                                 cols[:, GCNB1 + k, 2 + c:3 + c], 0.0, ALU.add, ALU.max)
                    last.then_inc(sig("gcn_z_ready1"), 1)
            for half in range(2):
                r = slice(half * D // 2, (half + 1) * D // 2)
                dve.wait_ge(*at("gcn_mixed", 5 + half))
                last = dve.tensor_tensor(x[:, r], x[:, r], ps[:, 1 + 2 * half, 0:D // 2], ALU.add)
            last.then_inc(sig("x_updated"), 1)

            layer_norm(7)
            dve.tensor_scalar(lstm_hb[:], lstm_b[:], 0.5, None, ALU.mult).then_inc(sig("lstm_hb_ready"), 1)
            dve.wait_ge(*at("router_scored", 1))
            dve.tensor_tensor(gate8[:], ps[:, 6, 0:E], router_b[:], ALU.add)
            settle()
            top2()
            dve.tensor_scalar(small[:, 0:1], gtop[:, 0:1], -1.0, None, ALU.mult)
            dve.tensor_copy(gated[:], gtop[:]).then_inc(sig("router_max_ready"), 1)
            dve.wait_ge(*at("router_exp_ready", 1))
            dve.tensor_tensor(small[:, 4:5], gate8[:, 0:1], gate8[:, 1:2], ALU.add)
            dve.tensor_scalar(gated[:], iota_f[:, 0:E], gidxf[:, 0:1], gate8[:, 0:1], ALU.is_equal, ALU.mult)
            dve.tensor_scalar(small[:, 8:16], iota_f[:, 0:E], gidxf[:, 1:2], gate8[:, 1:2], ALU.is_equal, ALU.mult)
            settle()
            dve.reciprocal(small[:, 4:5], small[:, 4:5])
            dve.tensor_tensor(gated[:], gated[:], small[:, 8:16], ALU.add)
            settle()
            dve.tensor_scalar(gated[:], gated[:], small[:, 4:5], None, ALU.mult).then_inc(sig("lstm_gated_ready"), 1)
            settle()
            dve.tensor_scalar(gate8[:], gated[:], 0.5, None, ALU.mult)

            def lstm_cell(n, u):
                dve.wait_ge(*at("l3_gate_ready", n * 3 + 2))
                dve.scalar_tensor_tensor(t1[:], prob[:, 0:4, :].rearrange("p c n -> p (c n)"), 1.0,
                                         prob[:, 4:8, :].rearrange("p c n -> p (c n)"), ALU.add, ALU.mult) \
                    .then_inc(sig("l3_cell_ready"), 1)
                dve.wait_ge(*at("l3_cell_tanh_ready", n + 1))
                dve.scalar_tensor_tensor(h_t[u][:].rearrange("p c n -> p (c n)"),
                                         prob_t[:, 0:4, :].rearrange("p c n -> p (c n)"), 1.0,
                                         prob_t[:, 4:8, :].rearrange("p c n -> p (c n)"), ALU.add, ALU.mult) \
                    .then_inc(sig("l3_h_ready"), 1)

            def lstm_add(n, u):
                settle()
                dve.wait_ge(*at("l3_o_projected", n + 1))
                dve.scalar_tensor_tensor(acc[:], bank(3 + u), gate8[:, bass.ds(n, 1)], acc[:], ALU.mult, ALU.add) \
                    .then_inc(sig("l3_expert_added"), 1)

            dve.sem_inc(sig("l3_h_ready"), 1)
            dve.sem_inc(sig("l3_expert_added"), 1)
            dve.wait_ge(*at("lstm_gated_transposed", 1))
            dve.tensor_copy(gated_t[:], ps[0:E, 5, 0:P]).then_inc(sig("lstm_gated_t_ready"), 1)
            lstm_cell(0, 0)
            dve.wait_ge(*at("lstm_bo_shared", 1))
            dve.tensor_tensor(acc[:], x[:], bank(7), ALU.add)
            settle()
            lstm_cell(1, 1)
            lstm_add(0, 0)
            with dve.Fori(1, E // 2) as i:
                for u in range(2):
                    lstm_cell(i * 2 + u, u)
                    lstm_add(i * 2 + (u - 1), 1 - u)
            lstm_add(E - 1, 1)
            settle()
            dve.tensor_copy(x[:], acc[:]).then_inc(sig("x_updated"), 1)


def lay_out(inputs):
    import numpy as np

    a = {k: np.asarray(v) for k, v in inputs.items()}

    def by_partition(w):
        s = w.shape
        w = w.reshape(*s[:-2], s[-2] // P, P, s[-1])
        return np.moveaxis(w, -3, -2)

    def columns(w):
        return np.moveaxis(w.reshape(*w.shape[:-1], -1, P), -1, 0)

    swap = lambda w: np.swapaxes(w, -1, -2)
    o = {"x": a["x"], "src": a["src"].reshape(P, -1), "dst": a["dst"].reshape(P, -1)}
    o["l0_W"] = by_partition(a["L0_gnn_W"].transpose(1, 0, 2).reshape(D, D))
    o["gat_a"] = a["L0_gnn_a"].reshape(H, 2, DH).transpose(1, 0, 2).reshape(2, D)
    for k in ("wq", "wk", "wv", "wo"):
        stack = np.stack([np.repeat(w.reshape(D, -1, DH), D // w.shape[1], axis=1).reshape(D, D)
                          for w in (a[f"L0_ffn_{k}{n}"] for n in range(3))])
        o[f"gqa_{k}"] = by_partition(stack).reshape(3, P, CH * D)
    o["r_w1"] = by_partition(a["L0_ffn_r_w1"])
    o["r_w2"] = a["L0_ffn_r_w2"]
    o["r_b1"] = a["L0_ffn_r_b1"].reshape(P, 1)
    o["r_b2"] = a["L0_ffn_r_b2"].reshape(1, 3)
    o["conv"] = by_partition(a["L1_gnn_W_conv"])
    for k in ("q", "k", "v", "o"):
        o[f"perf_w{k}"] = by_partition(a[f"L1_gnn_W{k}"])
    o["proj_t"] = swap(a["L1_gnn_proj"])
    o["peer_wq"] = by_partition(a["L1_ffn_w_q"])
    o["keys_t"] = a["L1_ffn_keys"].reshape(2, 4, KEYS, 2, 32).transpose(3, 1, 4, 0, 2).reshape(2, P, 2, KEYS)
    o["peer_down"] = by_partition(swap(a["L1_ffn_weight_down_embed"]))
    o["peer_up"] = a["L1_ffn_weight_up_embed"]
    for k in ("q", "k", "v"):
        o[f"exph_w{k}"] = by_partition(a[f"L2_gnn_W{k}"])
    o["gate_wk"] = by_partition(swap(a["L2_ffn_gate_Wk"]))
    o["eq_t"] = by_partition(swap(a["L2_ffn_expert_queries"]))
    qkv = by_partition(swap(a["L2_ffn_Wqkv"]))
    o["l2_wqk"], o["l2_wv"] = qkv[..., 0:2 * D], qkv[..., 2 * D:]
    o["l2_wo"] = by_partition(swap(a["L2_ffn_Wo"]))
    o["l2_w1"] = by_partition(swap(a["L2_ffn_W1"]))
    o["l2_w2"] = np.concatenate([swap(a["L2_ffn_W2"]), a["L2_ffn_bf2"][:, None, :]], axis=1)
    o["l2_rows"] = np.stack([a["L2_ffn_bqkv"][:, 2 * D:], a["L2_ffn_bo"], a["L2_ffn_g1"], a["L2_ffn_be1"],
                             a["L2_ffn_g2"]], axis=1)
    o["bqk"] = columns(a["L2_ffn_bqkv"][:, 0:2 * D]).reshape(P, -1)
    o["bf1"] = swap(a["L2_ffn_bf1"])
    o["be2"] = a["L2_ffn_be2"]
    for n in range(3):
        o[f"gcn_w{n + 1}"] = by_partition(a[f"L3_gnn_W{n + 1}"])
    o["gcn_b3"] = a["L3_gnn_b3"].reshape(1, D)
    o["router_w"] = by_partition(a["L3_ffn_router_w"])
    o["router_b"] = a["L3_ffn_router_b"].reshape(1, E)
    o["l3_wi"] = by_partition(a["L3_ffn_Wi"])
    o["l3_wo"] = by_partition(a["L3_ffn_Wo"])
    o["lstm_b"] = columns(a["L3_ffn_b"]).reshape(P, -1)
    o["lstm_bo"] = a["L3_ffn_bo"]
    o["cols"] = columns(np.stack([a[k] for k in (
        "L1_gnn_norm1_g", "L1_gnn_norm1_b", "L1_gnn_norm2_g", "L1_gnn_norm2_b", "L1_gnn_b_conv",
        "L2_gnn_bn_gamma", "L2_gnn_bn_beta", "L2_ffn_gate_bk", "L3_gnn_b1", "L3_gnn_b2")]))
    return {k: np.ascontiguousarray(w) for k, w in o.items()}


def kernel(**inputs):
    import concourse.bacc as bacc
    from concourse.bass_utils import run_bass_kernel_spmd

    nc = bacc.Bacc("TRN2", target_bir_lowering=False, num_devices=1)
    arrays, aps = {}, {}
    for name, a in lay_out(inputs).items():
        arrays[f"in_{name}"] = a
        aps[name] = nc.dram_tensor(f"in_{name}", a.shape, mybir.dt.from_np(a.dtype), kind="ExternalInput").ap()
    out = nc.dram_tensor("out_x", (P, D), F32, kind="ExternalOutput").ap()
    build(nc, aps, out)
    r = run_bass_kernel_spmd(nc, [arrays], core_ids=[0])
    return r.results[0]["out_x"]
```

```python
from contextlib import ExitStack

import concourse.bass as bass
from concourse import mybir

F32 = mybir.dt.float32
BF16 = mybir.dt.bfloat16
I32 = mybir.dt.int32
U32 = mybir.dt.uint32
ALU = mybir.AluOpType
ACT = mybir.ActivationFunctionType
AX = mybir.AxisListType

P = 128
D = 512
CH = D // P
H = 8
DH = D // H
EDGES_PER_PARTITION = 2176 // P
EPS = 1e-5
SUBLAYERS = 8

PERF_N = 64
PERF_M = 256
PERF_EPS = 1e-6
KV_BANKS = (0, 1, 2, 6)
KEYS = 256
TOPK = 16
PICKS = TOPK * TOPK
E = 8
F2 = 64
NEG = -3.0e38
GAT_NEG = -9000000000000000.0

BV, BO, G1, BE1, G2 = range(5)
N1G, N1B, N2G, N2B, BCONV, BNG, BNB, GATEB, GCNB1, GCNB2 = range(10)

DENSE_USED = {
    "l0_W": ("gat_h_projected", 1),
    "perf_wq": ("perf_qk_projected", 1), "perf_wk": ("perf_qk_projected", 1), "perf_wv": ("perf_v_projected", 1),
    "conv": ("conv_h_projected", 1), "perf_wo": ("perf_o_projected", 2),
    "peer_wq": ("peer_q_projected", 2), "peer_tables": ("peer_up_projected", 1),
    "exph_wq": ("exph_q_projected", 1), "exph_wk": ("exph_k_projected", 1), "exph_wv": ("exph_v_projected", 1),
    "gate_wk": ("gate_keys_projected", 1),
    "gcn_w1": ("gcn_h_projected", 2), "gcn_w2": ("gcn_h_projected", 4), "gcn_w3": ("gcn_h_projected", 6),
}
DENSE = list(DENSE_USED)
SLOTS = 6


STEPS = {
    "gat_tensor_steps": [("gat_h_projected", 1), ("edges_counted", 1), ("gat_s_transposed", 1),
                         ("gat_scored", 1), ("gat_prob_transposed", 2), ("gat_attended", 1)],
    "gat_vector_steps": [("one_hot_ready", 2), ("gat_s_ready", 2), ("gat_a_used", 1), ("gat_lr_ready", 2),
                         ("counts_ready", 1), ("gat_max_ready", 2), ("gat_prob_t_ready0", 1), ("gat_out_ready", 1)],
    "gat_scalar_steps": [("gat_h_ready", 1), ("gat_leak_ready", 2), ("gat_prob_ready", 8), ("gat_prob_t_ready1", 1),
                         ("gat_exp_ready", 1), ("route_exp_ready", 1)],
    "route_tensor_steps": [("route_summed", 1), ("route_hidden_summed", 1), ("route_logits_summed", 1),
                           ("counts_transposed", 1), ("adjacency_transposed", 1)],
    "route_vector_steps": [("route_mean_ready", 1), ("route_hidden_ready", 1), ("route_logits_ready", 1),
                           ("route_selected", 1), ("gcn_deg_ready", 1), ("adjacency_ready", 2), ("mean_sd_ready", 1),
                           ("gcn_sd_ready", 1)],
    "gps_tensor_steps": [("perf_qk_projected", 1), ("perf_v_projected", 1), ("perf_k_products", 1), ("perf_diag_summed", 1),
                         ("perf_kmax_transposed", 1), ("perf_q_products", 1), ("perf_kmax_spread", 1), ("conv_h_projected", 1),
                         ("perf_kv_done", 1), ("perf_q_transposed", 1), ("conv_mixed", 1), ("perf_attended", 1),
                         ("perf_ctx_transposed", 1), ("perf_o_projected", 2), ("gps_out_transposed", 1)],
    "gps_vector_steps": [("perf_rows_ready", 1), ("perf_t_scaled", 2), ("perf_t_ready", 1), ("perf_sq_ready", 1),
                         ("perf_kmax_ready", 1), ("perf_kmax_rows_ready", 1), ("perf_bias_ready1", 1),
                         ("perf_qmax_ready", 1), ("perf_bias_ready0", 1), ("perf_features_ready", 2),
                         ("perf_kv_ready", 2), ("perf_q_t_ready0", 1), ("perf_ctx_ready", 1), ("perf_ctx_t_ready0", 1)],
    "gps_scalar_steps": [("perf_v_ready", 1), ("perf_exp_ready", 2), ("conv_h_ready", 1), ("perf_kv_ready_act", 2),
                         ("perf_q_t_ready1", 1), ("conv_t_ready", 1), ("perf_ctx_t_ready1", 1)],
    "exph_tensor_steps": [("exph_q_projected", 1), ("exph_k_projected", 1), ("exph_scored", 2), ("exph_v_projected", 1),
                          ("exph_attended", 1), ("exph_h_transposed", 1), ("exph_out_transposed", 1),
                          ("gate_keys_projected", 1), ("gate_scored", 1), ("gated_transposed", 1), ("be2_shared", 1)],
    "exph_vector_steps": [("exph_k_ready", 1), ("exph_clipped", 2), ("exph_weights_ready", 2), ("exph_h_ready", 1),
                          ("gate_max_ready", 1), ("gated_ready", 1), ("gated_t_ready", 1)],
    "exph_scalar_steps": [("exph_q_ready", 1), ("exph_exp_ready", 2), ("exph_v_ready", 1), ("gate_keys_ready", 1),
                          ("gate_exp_ready", 1), ("router_exp_ready", 1)],
    "router_tensor_steps": [("router_scored", 1), ("lstm_gated_transposed", 1), ("lstm_bo_shared", 1)],
    "router_vector_steps": [("lstm_hb_ready", 1), ("router_max_ready", 1), ("lstm_gated_ready", 1),
                            ("lstm_gated_t_ready", 1)],
}
STEP_BASE = {}
for _semaphore, _steps in STEPS.items():
    _n = 0
    for _step, _times in _steps:
        STEP_BASE[_step] = (_semaphore, _n)
        _n += _times


def build(nc, A, out):
    ctx = ExitStack()
    signals = {}

    def sig(name):
        name = STEP_BASE.get(name, (name, 0))[0]
        if name not in signals:
            signals[name] = ctx.enter_context(nc.semaphore(name))
        return signals[name]

    def at(name, value):
        return sig(name), STEP_BASE.get(name, (name, 0))[1] + value

    with ctx:
        def sb(name, shape, dt=F32):
            return ctx.enter_context(nc.sbuf_tensor(name, shape, dt))

        ps = ctx.enter_context(nc.psum_tensor("ps", [P, 8, 512], F32))

        dense = sb("dense", [P, SLOTS, CH * D])
        ew = sb("ew", [P, 2, 4 * CH * D])
        ew1 = sb("ew1", [P, 2, CH, F2])
        ew2 = sb("ew2", [F2 + 1, 2, D])
        erows = sb("erows", [P, 2, 5, D])
        r_w1 = erows[:, 1, 0, :].rearrange("p (c n) -> p c n", c=CH)
        r_w2 = sb("r_w2", [P, 3])
        r_b1 = sb("r_b1", [P, 1])
        r_b2 = sb("r_b2", [1, 3])
        attn_a = erows[:, 0, 0:2, :]
        cols = sb("cols", [P, 10, CH])
        proj_t = sb("proj_t", [P, PERF_M])
        keys_t = sb("keys_t", [P, 2, KEYS])
        bqk = sb("bqk", [P, E * 8])
        bf1 = sb("bf1", [F2, E])
        eq_t = sb("eq_t", [P, CH, E])
        be2 = sb("be2", [E, D])
        gcn_b3 = sb("gcn_b3", [P, D])
        router_w = sb("router_w", [P, CH, E])
        router_b = sb("router_b", [P, E])
        lstm_b = sb("lstm_b", [P, E * 16])
        lstm_hb = sb("lstm_hb", [P, E * 16])
        lstm_bo = sb("lstm_bo", [E, D])

        ident = sb("ident", [P, P])
        iota_i = sb("iota_i", [P, P], I32)
        iota_f = sb("iota_f", [P, P])
        minus_half = sb("minus_half", [P, CH])
        ones = sb("ones", [P, P])

        src_i = sb("src_i", [P, EDGES_PER_PARTITION], I32)
        dst_i = sb("dst_i", [P, EDGES_PER_PARTITION], I32)
        src_f = sb("src_f", [P, EDGES_PER_PARTITION])
        dst_f = sb("dst_f", [P, EDGES_PER_PARTITION])
        one_hot = ew[:, 1, 0:EDGES_PER_PARTITION * P].bitcast(BF16).rearrange("p (a t n) -> p a t n", a=2, n=P)
        cnt_sd = sb("cnt_sd", [P, P])
        gat_cap = sb("gat_cap", [P, P])
        mean_sd = sb("mean_sd", [P, P])
        gcn_sd = sb("gcn_sd", [P, P])
        mean_ds = sb("mean_ds", [P, P])
        gcn_ds = sb("gcn_ds", [P, P])
        mean_col = sb("mean_col", [P, 1])
        deg_col = sb("deg_col", [P, 1])
        dis_col = sb("dis_col", [P, 1])

        x = sb("x", [P, D])
        y = sb("y", [P, D])
        y_t = sb("y_t", [P, CH, P])
        z_t = sb("z_t", [P, CH, P])
        acc = sb("acc", [P, D])
        qk_t = sb("qk_t", [P, 2 * CH, P])
        v = sb("v", [P, H * (DH + 1)])
        prob_store = sb("prob_store", [P, 4 * 4 * (DH + 1)])
        prob = prob_store[:, 0:H * P].rearrange("p (h n) -> p h n", h=H)
        prob_t = sb("prob_t", [P, H, P])
        ctxv = sb("ctxv", [P, D])
        ctx_t = sb("ctx_t", [P, CH, P])
        t1 = sb("t1", [P, D])
        x1 = sb("x1", [P, D])
        x1_t = sb("x1_t", [P, CH, P])
        h1_t = sb("h1_t", [F2 + 1, P])
        h2 = sb("h2", [P, D])
        big = sb("big", [P, 2 * H * P])

        ln_st = sb("ln_st", [P, 6])
        half_st = sb("half_st", [P, 2, 6])
        ln_mv = sb("ln_mv", [P, 2])
        ln_var = sb("ln_var", [P, 1])
        ln_rstd = sb("ln_rstd", [P, 1])
        bn_st = sb("bn_st", [P, CH, 6])
        bn_mv = sb("bn_mv", [P, CH, 2])
        bn_var = sb("bn_var", [P, CH])
        bn_rstd = sb("bn_rstd", [P, CH])
        bn_scale = sb("bn_scale", [P, CH])
        bn_shift = sb("bn_shift", [P, CH])
        nmax = sb("nmax", [P, H])
        nmax_s = sb("nmax_s", [P, H])
        rsum = sb("rsum", [P, H])
        rinv = sb("rinv", [P, H])
        s_cat = sb("s_cat", [P, 40])
        gat_l = sb("gat_l", [40, P])
        gat_r = sb("gat_r", [40, H, P])
        r_mean = sb("r_mean", [P, CH])
        r_hcol = sb("r_hcol", [P, 1])
        r_p = sb("r_p", [1, 8])
        r_top = sb("r_top", [1, 8])
        selected = sb("selected", [1, 8], U32)
        small = sb("small", [P, 32])
        perf_r = sb("perf_r", [4, 2, PERF_N])
        perf_k2 = sb("perf_k2", [4, 2])
        topv = sb("topv", [P, 4, TOPK])
        topi = sb("topi", [P, 4, TOPK], U32)
        topif = sb("topif", [P, 4, TOPK])
        best = sb("best", [P, 4, TOPK])
        negbest = sb("negbest", [P, 4])
        picksum = sb("picksum", [P, H])
        pickinv = sb("pickinv", [P, H])
        gate8 = sb("gate8", [P, E])
        gated = sb("gated", [P, E])
        gidx = sb("gidx", [P, 8], U32)
        gidxf = sb("gidxf", [P, 8])
        gtop = sb("gtop", [P, 8])
        gated_t = sb("gated_t", [E, P])
        rg = sb("rg", [P, 1])

        def l2_wqk(u):
            return ew[:, u, 0:2 * CH * D].rearrange("p (c n) -> p c n", c=CH)

        def l2_wv(u):
            return ew[:, u, 2 * CH * D:3 * CH * D].rearrange("p (c n) -> p c n", c=CH)

        def wo_of(u):
            return ew[:, u, 3 * CH * D:4 * CH * D].rearrange("p (c n) -> p c n", c=CH)

        def l3_wi(u):
            return ew[:, u, 0:CH * D].rearrange("p (c n) -> p c n", c=CH)

        def l3_wgo(u):
            return ew[:, u, CH * D:3 * CH * D].rearrange("p (c n) -> p c n", c=CH)

        landed, so_far = {}, [0] * SLOTS
        for n, name in enumerate(DENSE):
            so_far[n % SLOTS] += 32 if name == "peer_tables" else 16
            landed[name] = so_far[n % SLOTS]

        def slot(name):
            return dense[:, DENSE.index(name) % SLOTS, :]

        def matrix(name, n=D):
            return slot(name)[:, 0:CH * n].rearrange("p (c n) -> p c n", c=CH)

        peer_down = slot("peer_tables")[:, 0:CH * PICKS].rearrange("p (c n) -> p c n", c=CH)
        peer_up = slot("peer_tables")[:, CH * PICKS:CH * PICKS + 2 * D].rearrange("p (c n) -> p c n", c=2)

        heads_v = v[:, :].rearrange("p (h e) -> p h e", h=H)
        pair_v = v[:, :].rearrange("p (g a e) -> p g a e", g=4, a=2)
        hd = ctxv[:, :].rearrange("p (g a d) -> p g a d", g=4, a=2)
        peer_work, peer_work2 = (tile[:, :].rearrange("p (b n) -> p b n", b=2) for tile in (t1, h2))
        wide = big[:, :].rearrange("p (a n) -> p a n", a=2)
        kv_sb = prob_store[:, :].rearrange("p (b n) -> p b n", b=4)
        peer_all, peer_exp, peer_rest, peer_pick = (
            tile.rearrange("p (b n) -> p b n", b=4) for tile in (
                big[:, 0:4 * PICKS], big[:, 4 * PICKS:8 * PICKS], prob_t[:].rearrange("p h n -> p (h n)"),
                prob_store[:, 0:4 * PICKS]))
        h_t = (ctx_t, x1_t)

        def bank(b):
            return ps[:, b, :]

        def bank_heads(b):
            return ps[:, b, :].rearrange("p (h d) -> p h d", h=H)

        def ctx_half(copy, a):
            r = slice(DH * a, DH * a + DH)
            pt = ps[r, a, 0:CH * PERF_N].rearrange("p (c n) -> p c n", c=CH)
            copy(x1_t[r, :, 0:PERF_N], pt)
            return copy(x1_t[r, :, PERF_N:P], pt[:, :, PERF_N - 1:PERF_N].broadcast_to([DH, CH, P - PERF_N]))

        def bank_chunks(b):
            return ps[:, b, :].rearrange("p (c n) -> p c n", c=CH)

        block = ctx.enter_context(nc.Block())

        @block.sync
        def _(sp):
            def load_dense(name):
                n = DENSE.index(name)
                if n >= SLOTS:
                    done, value = DENSE_USED[DENSE[n - SLOTS]]
                    sp.wait_ge(*at(done, value))
                s = sig(f"dense_landed{n % SLOTS}")
                if name == "peer_tables":
                    sp.dma_start(peer_down, A["peer_down"][:, :, 0:PICKS]).then_inc(s, 16)
                    sp.dma_start(peer_up, A["peer_up"][0:PICKS, :].rearrange("(c p) n -> p c n", p=P)).then_inc(s, 16)
                else:
                    sp.dma_start(slot(name), A[name].rearrange("p c n -> p (c n)")).then_inc(s, 16)

            def load_l2(e, u):
                sp.dma_start(l2_wqk(u), A["l2_wqk"][e]).then_inc(sig(f"l2_wqk_landed{u}"), 16)
                sp.dma_start(l2_wv(u), A["l2_wv"][e]).then_inc(sig(f"l2_wv_landed{u}"), 16)
                sp.dma_start(wo_of(u), A["l2_wo"][e]).then_inc(sig(f"l2_wo_landed{u}"), 16)

                sp.dma_start(ew1[:, u], A["l2_w1"][e]).then_inc(sig(f"l2_small_landed{u}"), 16)
                sp.dma_start(ew2[:, u], A["l2_w2"][e]).then_inc(sig(f"l2_small_landed{u}"), 16)

            def load_l2_rows(e, u):
                sp.dma_start(erows[:, u], A["l2_rows"][e].rearrange("(a r) n -> a r n", a=1)
                             .broadcast_to([P, 5, D])).then_inc(sig(f"l2_rows_landed{u}"), 16)

            def load_l3(e, u):
                sp.dma_start(l3_wi(u), A["l3_wi"][e][:, :, 0:D]).then_inc(sig(f"l3_wi_landed{u}"), 16)
                sp.dma_start(l3_wgo(u), A["l3_wi"][e][:, :, 2 * D:4 * D]).then_inc(sig(f"l3_wgo_landed{u}"), 16)
                sp.dma_start(wo_of(u), A["l3_wo"][e]).then_inc(sig(f"l3_wo_landed{u}"), 16)

            sp.dma_start(x[:], A["x"]).then_inc(sig("x_landed"), 16)
            sp.dma_start(attn_a, A["gat_a"].rearrange("(a r) n -> a r n", a=1).broadcast_to([P, 2, D])) \
                .then_inc(sig("gat_a_landed"), 16)
            for name in DENSE[:SLOTS]:
                load_dense(name)
            for tile, name in ((r_w1[:], "r_w1"), (r_w2[:], "r_w2"), (r_b1[:], "r_b1")):
                sp.dma_start(tile, A[name]).then_inc(sig("router_landed"), 16)
            sp.dma_start(r_b2[:], A["r_b2"]).then_inc(sig("router_landed"), 16)
            sp.dma_start(cols[:], A["cols"]).then_inc(sig("params_landed"), 16)
            sp.dma_start(proj_t[0:DH], A["proj_t"]).then_inc(sig("params_landed"), 16)
            sp.dma_start(proj_t[DH:P], A["proj_t"]).then_inc(sig("params_landed"), 16)
            for tile, name in ((keys_t[:], "keys_t"), (bqk[:], "bqk"), (bf1[:], "bf1"), (eq_t[:], "eq_t"),
                               (be2[:], "be2"), (router_w[:], "router_w"), (lstm_b[:], "lstm_b"),
                               (lstm_bo[:], "lstm_bo")):
                sp.dma_start(tile, A[name][0] if name == "keys_t" else A[name]).then_inc(sig("late_params_landed"), 16)
            sp.dma_start(gcn_b3[:], A["gcn_b3"].broadcast_to([P, D])).then_inc(sig("late_params_landed"), 16)
            sp.dma_start(router_b[:], A["router_b"].broadcast_to([P, E])).then_inc(sig("late_params_landed"), 16)
            sp.wait_ge(*at("edges_counted", 1))
            load_l2(1, 1)
            sp.wait_ge(*at("gat_a_used", 1))
            load_l2_rows(0, 0)
            load_dense(DENSE[SLOTS])
            sp.wait_ge(*at("route_selected", 1))
            variant = sp.value_load(selected[0:1, 0:1], min_val=0, max_val=2)
            first = CH * P
            sp.dma_start(ew[:, 0, 0:first], A["gqa_wq"][variant][:, 0:first]).then_inc(sig("gqa_wq_first_landed"), 16)
            sp.dma_start(ew[:, 0, first:CH * D], A["gqa_wq"][variant][:, first:]).then_inc(sig("gqa_wq_landed"), 16)
            for k, name in enumerate(("wk", "wv", "wo"), 1):
                sp.dma_start(ew[:, 0, k * CH * D:(k + 1) * CH * D], A[f"gqa_{name}"][variant]) \
                    .then_inc(sig(f"gqa_{name}_landed"), 16)
            load_l2_rows(1, 1)
            sp.wait_ge(*at("gqa_o_projected", 1))
            load_l2(0, 0)
            for name in DENSE[SLOTS + 1:]:
                load_dense(name)
            with sp.Fori(1, E // 2) as i:
                for u in range(2):
                    n = i * 2 + u
                    sp.wait_ge(*at("l2_qk_projected", n * 2 - 2))
                    sp.dma_start(l2_wqk(u), A["l2_wqk"][n]).then_inc(sig(f"l2_wqk_landed{u}"), 16)
                    sp.wait_ge(*at("l2_v_projected", n - 1))
                    sp.dma_start(l2_wv(u), A["l2_wv"][n]).then_inc(sig(f"l2_wv_landed{u}"), 16)
                    sp.wait_ge(*at("l2_o_projected", n * 2 - 2))
                    sp.dma_start(wo_of(u), A["l2_wo"][n]).then_inc(sig(f"l2_wo_landed{u}"), 16)
                    sp.wait_ge(*at("l2_h2_projected", n - 1))
                    sp.dma_start(ew1[:, u], A["l2_w1"][n]).then_inc(sig(f"l2_small_landed{u}"), 16)
                    sp.dma_start(ew2[:, u], A["l2_w2"][n]).then_inc(sig(f"l2_small_landed{u}"), 16)
                    sp.wait_ge(*at("l2_expert_added", n - 1))
                    sp.dma_start(erows[:, u], A["l2_rows"][n].rearrange("(a r) n -> a r n", a=1)
                                 .broadcast_to([P, 5, D])).then_inc(sig(f"l2_rows_landed{u}"), 16)
            for u in range(2):
                sp.wait_ge(*at("l2_qk_projected", 2 * (E - 1 + u)))
                sp.wait_ge(*at("l2_v_projected", E - 1 + u))
                sp.wait_ge(*at("l2_o_projected", 2 * (E - 1 + u)))
                load_l3(u, u)
            with sp.Fori(1, E // 2) as i:
                for u in range(2):
                    n = i * 2 + u
                    sp.wait_ge(*at("l3_gates_projected", n * 3 - 3))
                    sp.dma_start(l3_wi(u), A["l3_wi"][n][:, :, 0:D]).then_inc(sig(f"l3_wi_landed{u}"), 16)
                    sp.dma_start(l3_wgo(u), A["l3_wi"][n][:, :, 2 * D:4 * D]).then_inc(sig(f"l3_wgo_landed{u}"), 16)
                    sp.wait_ge(*at("l3_o_projected", n - 1))
                    sp.dma_start(wo_of(u), A["l3_wo"][n]).then_inc(sig(f"l3_wo_landed{u}"), 16)
            for s, value in (("router_landed", 64), ("params_landed", 48), ("late_params_landed", 160)):
                sp.wait_ge(*at(s, value))
            sp.wait_ge(*at("x_updated", SUBLAYERS))
            sp.dma_start(out, acc[:]).then_inc(sig("out_written"), 16)
            sp.wait_ge(*at("out_written", 16))

        @block.gpsimd
        def _(pool):
            pool.memset(ident[:], 0.0).then_inc(sig("pool_cleared"), 1)
            pool.memset(gat_r[:], 0.0).then_inc(sig("pool_cleared"), 1)
            pool.memset(minus_half[:], -0.5).then_inc(sig("const_ready"), 1)
            pool.memset(ones[:], 1.0).then_inc(sig("const_ready"), 1)
            pool.iota(iota_i[:], pattern=[[1, P]], base=0, channel_multiplier=0).then_inc(sig("iota_ready"), 1)
            pool.wait_ge(*at("pool_cleared", 2))
            pool.affine_select(out=ident[:], in_=ident[:], compare_op=ALU.not_equal, fill=1.0, base=0,
                               pattern=[[-1, P]], channel_multiplier=1).then_inc(sig("const_ready"), 1)
            pool.wait_ge(*at("const_ready", 3))
            for p0 in (0, 32):
                if p0:
                    pool.wait_ge(*at("gat_r_ready", 1))
                pool.affine_select(out=gat_r[p0:p0 + H], in_=gat_r[p0:p0 + H], compare_op=ALU.not_equal,
                                   fill=1.0, base=0, pattern=[[-1, H], [0, P]], channel_multiplier=1) \
                    .then_inc(sig("gat_r_ready"), 1)
            pool.wait_ge(*at("gat_r_ready", 2))

            def layer_norm_rstd(k):
                pool.wait_ge(*at("ln_var_ready", k + 1))
                pool.tensor_tensor(ln_rstd[:], ln_var[:], minus_half[:, 0:1], ALU.pow).then_inc(sig("ln_rstd_ready"), 1)

            def batch_norm_rstd(k):
                pool.wait_ge(*at("bn_var_ready", k + 1))
                pool.tensor_tensor(bn_rstd[:], bn_var[:], minus_half[:], ALU.pow).then_inc(sig("bn_rstd_ready"), 1)

            layer_norm_rstd(0)
            layer_norm_rstd(1)
            pool.wait_ge(*at("gcn_deg_ready", 1))
            pool.tensor_tensor(dis_col[:], deg_col[:], minus_half[:, 0:1], ALU.pow).then_inc(sig("gcn_dis_ready"), 1)
            layer_norm_rstd(2)
            batch_norm_rstd(0)
            batch_norm_rstd(1)
            layer_norm_rstd(3)
            def pair_sums(k):
                for h in (2 * k, 2 * k + 1):
                    if h % 2 == 0:
                        pool.wait_ge(*at("peer_top_ready", k + 1))
                    else:
                        pool.wait_ge(*at("peer_sum_ready", h))
                    pool.tensor_tensor(peer_all[:, h % 4, :].rearrange("p (i j) -> p i j", i=TOPK),
                                       topv[:, h % 4, :].unsqueeze(2).broadcast_to([P, TOPK, TOPK]),
                                       topif[:, h % 4, :].unsqueeze(1).broadcast_to([P, TOPK, TOPK]), ALU.add) \
                        .then_inc(sig("peer_sum_ready"), 1)

            def diagonal(k):
                pool.wait_ge(*at("peer_inv_ready", k + 1))
                if k:
                    pool.wait_ge(*at("peer_head_added", 2 * k - 1))
                pool.tensor_scalar(x1_t[:, 0, :], ident[:], pickinv[:, 2 * k:2 * k + 1], None, ALU.mult) \
                    .then_inc(sig("peer_diag_ready0"), 1)

            for k in range(H // 2):
                pair_sums(k)
                if k >= 2:
                    diagonal(k - 2)
            diagonal(H // 2 - 2)
            diagonal(H // 2 - 1)
            layer_norm_rstd(4)
            batch_norm_rstd(2)
            layer_norm_rstd(5)

            def residual_rows(n, rows_value, u):
                pool.wait_ge(*at(f"l2_rows_landed{u}", rows_value))
                pool.tensor_tensor(erows[:, u, BO, :], erows[:, u, BO, :], y[:], ALU.add) \
                    .then_inc(sig("l2_residual_ready"), 1)

            def inner_norms(n, first):
                pool.wait_ge(*at("l2_var_ready", n * 2 + first))
                pool.tensor_tensor(ln_rstd[:], ln_var[:], minus_half[:, 0:1], ALU.pow).then_inc(sig("l2_rstd_ready"), 1)

            pool.wait_ge(*at("y_ready", 12))
            residual_rows(0, 16, 0)
            with pool.Fori(0, E // 2 - 1) as i:
                for u in range(2):
                    inner_norms(i * 2 + u, 1)
                    residual_rows(i * 2 + u + 1, i * 16 + 16 * (u + 1), 1 - u)
                    inner_norms(i * 2 + u, 2)
            inner_norms(E - 2, 1)
            residual_rows(E - 1, 16 * (E // 2), 1)
            inner_norms(E - 2, 2)
            inner_norms(E - 1, 1)
            inner_norms(E - 1, 2)
            layer_norm_rstd(6)
            layer_norm_rstd(7)

        @block.scalar
        def _(act):
            for tile, name in ((src_i[:], "src"), (dst_i[:], "dst")):
                act.dma_start(tile, A[name]).then_inc(sig("edges_landed"), 16)
            act.preload_act_table(ACT.Exp)

            def layer_norm_t(k):
                for half in range(2):
                    act.wait_ge(*at("y_transposed", 2 * k + half + 1))
                    last = nc.scalar.copy(y_t[:, 2 * half:2 * half + 2, :].rearrange("p c n -> p (c n)"),
                                          ps[:, 7 - half, 0:2 * P])
                last.then_inc(sig("y_t_ready"), 1)

            def exps(scores_max, done, n, scale):
                for a in range(2):
                    act.wait_ge(*at(scores_max, n * 2 + (a + 1)))
                    for g in range(4):
                        s = 4 * a + g
                        last = nc.scalar.activation(prob[:, s, :], ps[:, 3 + a, g * P:(g + 1) * P], ACT.Exp,
                                                    bias=nmax_s[:, s:s + 1], scale=scale, accum_out=rsum[:, s:s + 1])
                    last.then_inc(sig(done), 1)

            layer_norm_t(0)
            act.wait_ge(*at("gat_h_projected", 1))
            act.wait_ge(*at("gat_s_ready", 1))
            nc.scalar.copy(v[:, 0:D], bank(0)).then_inc(sig("gat_h_ready"), 1)
            act.wait_ge(*at("gat_scored", 1))
            for a in range(2):
                nc.scalar.mul(wide[:, a, 0:512], bank(3 + a), 0.2).then_inc(sig("gat_leak_ready"), 1)
            for h in range(H):
                if h % 4 == 0:
                    act.wait_ge(*at("gat_max_ready", h // 4 + 1))
                nc.scalar.activation(prob[:, h, :], prob[:, h, :], ACT.Exp, bias=nmax[:, h:h + 1],
                                     accum_out=rsum[:, h:h + 1]).then_inc(sig("gat_prob_ready"), 1)
            act.wait_ge(*at("gat_prob_transposed", 2))
            nc.scalar.copy(prob_t[:, 4:8, :].rearrange("p h n -> p (h n)"), bank(6)).then_inc(sig("gat_prob_t_ready1"), 1)
            act.wait_ge(*at("gat_out_ready", 1))
            nc.scalar.activation(t1[:], ctxv[:], ACT.Exp, bias=small[:, 0:1], accum_out=small[:, 1:2]) \
                .then_inc(sig("gat_exp_ready"), 1)

            layer_norm_t(1)
            act.wait_ge(*at("route_logits_ready", 1))
            nc.scalar.activation(r_p[0:1, 0:3], r_p[0:1, 0:3], ACT.Exp, bias=small[0:1, 0:1], accum_out=small[0:1, 1:2]) \
                .then_inc(sig("route_exp_ready"), 1)
            act.wait_ge(*at("gqa_q_projected", 1))
            nc.scalar.copy(qk_t[:, 0:CH, :].rearrange("p c n -> p (c n)"), bank(0)).then_inc(sig("gqa_q_ready"), 1)
            exps("gqa_max_ready", "gqa_exps_ready", 0, DH ** -0.5)
            act.wait_ge(*at("gqa_prob_transposed", 2))
            nc.scalar.copy(prob_t[:, 4:8, :].rearrange("p h n -> p (h n)"), bank(7)).then_inc(sig("gqa_prob_t_ready1"), 1)
            act.wait_ge(*at("gqa_attended", 1))
            nc.scalar.copy(ctx_t[:].rearrange("p c n -> p (c n)"), bank(4)).then_inc(sig("gqa_ctx_t_ready"), 1)

            layer_norm_t(2)
            act.wait_ge(*at("perf_v_projected", 1))
            act.wait_ge(*at("v_cleared", 1))
            for a in range(2):
                r = slice(DH * a, DH * a + DH)
                last = nc.scalar.copy(pair_v[r, :, a, 0:DH],
                                      ps[r, 1, :].rearrange("p (g a d) -> p g a d", g=4, a=2)[:, :, a, :])
            last.then_inc(sig("perf_v_ready"), 1)
            for w in (1, 0):
                act.wait_ge(*at(f"perf_bias_ready{w}", 1))
                for g in range(4):
                    last = nc.scalar.activation(wide[:, w, g * PERF_M:(g + 1) * PERF_M],
                                                ps[:, 4 + 2 * w + g // 2, (g % 2) * PERF_M:(g % 2 + 1) * PERF_M],
                                                ACT.Exp, bias=small[:, 16 + 4 * w + g:17 + 4 * w + g])
                last.then_inc(sig("perf_exp_ready"), 1)
            act.wait_ge(*at("conv_h_projected", 1))
            nc.scalar.copy(ctxv[:], bank(3)).then_inc(sig("conv_h_ready"), 1)
            act.wait_ge(*at("perf_kv_done", 1))
            for k in (1, 3):
                nc.scalar.copy(kv_sb[:, k, :], ps[:, KV_BANKS[k], 0:4 * (DH + 1)]).then_inc(sig("perf_kv_ready_act"), 1)
            act.wait_ge(*at("perf_q_transposed", 1))
            nc.scalar.copy(prob_t[:, 4:8, :].rearrange("p h n -> p (h n)"), bank(5)).then_inc(sig("perf_q_t_ready1"), 1)
            act.wait_ge(*at("conv_mixed", 1))
            for c in range(CH):
                last = nc.scalar.activation(ctx_t[:, c, :], ps[:, 3, c * P:(c + 1) * P], ACT.Relu,
                                            bias=cols[:, BCONV, c:c + 1])
            last.then_inc(sig("conv_t_ready"), 1)
            act.wait_ge(*at("perf_ctx_transposed", 1))
            ctx_half(nc.scalar.copy, 1).then_inc(sig("perf_ctx_t_ready1"), 1)

            layer_norm_t(3)
            act.wait_ge(*at("peer_q_projected", 2))
            nc.scalar.mul(qk_t[:, 2:4, :].rearrange("p c n -> p (c n)"), ps[:, 5, 0:2 * P], (1.0 + EPS) ** -0.5) \
                .then_inc(sig("peer_q_rest_ready"), 1)
            act.preload_act_table(ACT.Gelu_apprx_tanh)
            act.wait_ge(*at("peer_down_projected", 1))
            nc.scalar.activation(x1_t[:, 2:4, :].rearrange("p c n -> p (c n)"), ps[:, 5, 0:2 * P],
                                 ACT.Gelu_apprx_tanh).then_inc(sig("peer_gelu_ready"), 1)
            act.preload_act_table(ACT.Exp)
            def diagonal(k):
                act.wait_ge(*at("peer_inv_ready", k + 1))
                if k:
                    act.wait_ge(*at("peer_head_added", 2 * k))
                nc.scalar.mul(x1_t[:, 1, :], ident[:], pickinv[:, 2 * k + 1:2 * k + 2]).then_inc(sig("peer_diag_ready1"), 1)

            for k in range(H // 2):
                for h in (2 * k, 2 * k + 1):
                    act.wait_ge(*at("peer_best_ready", h + 1))
                    nc.scalar.activation(peer_exp[:, h % 4, :], peer_all[:, h % 4, :], ACT.Exp,
                                         bias=negbest[:, h % 4:h % 4 + 1]).then_inc(sig("peer_exp_ready"), 1)
                if k:
                    diagonal(k - 1)
            diagonal(H // 2 - 1)

            layer_norm_t(4)
            act.wait_ge(*at("exph_q_projected", 1))
            nc.scalar.copy(qk_t[:, 0:CH, :].rearrange("p c n -> p (c n)"), bank(0)).then_inc(sig("exph_q_ready"), 1)
            for a in range(2):
                act.wait_ge(*at("exph_clipped", a + 1))
                nc.scalar.activation(prob[:, 4 * a:4 * a + 4, :], prob[:, 4 * a:4 * a + 4, :], ACT.Exp,
                                     scale=DH ** -0.5).then_inc(sig("exph_exp_ready"), 1)
            act.wait_ge(*at("exph_v_projected", 1))
            nc.scalar.copy(heads_v[:, :, 0:DH], bank_heads(2)).then_inc(sig("exph_v_ready"), 1)

            layer_norm_t(5)
            def q_bias(n):
                act.wait_ge(*at("l2_qk_projected", n * 2 + 1))
                for c in range(CH):
                    last = nc.scalar.activation(qk_t[:, c, :], ps[:, 0, c * P:(c + 1) * P], ACT.Identity,
                                                bias=bqk[:, bass.ds(n * 8 + c, 1)])
                last.then_inc(sig("l2_q_ready"), 1)

            def expert_act(n, has_next):
                exps("l2_max_ready", "l2_exps_ready", n, DH ** -0.5)
                act.preload_act_table(ACT.Gelu)
                act.wait_ge(*at("l2_prob_transposed", n * 2 + 2))
                nc.scalar.copy(prob_t[:, 4:8, :].rearrange("p h n -> p (h n)"), bank(6)).then_inc(sig("l2_prob_t_ready1"), 1)
                act.wait_ge(*at("l2_attended", n + 1))
                nc.scalar.copy(ctx_t[:].rearrange("p c n -> p (c n)"), bank(7)).then_inc(sig("l2_ctx_t_ready"), 1)
                if has_next:
                    q_bias(n + 1)
                act.wait_ge(*at("l2_x1_transposed", n + 1))
                nc.scalar.copy(x1_t[:].rearrange("p c n -> p (c n)"), bank(5)).then_inc(sig("l2_x1_t_ready"), 1)
                act.wait_ge(*at("l2_h1_projected", n + 1))
                nc.scalar.activation(h1_t[0:F2, :], ps[0:F2, 6, 0:P], ACT.Gelu, bias=bf1[:, bass.ds(n, 1)]) \
                    .then_inc(sig("l2_h1_ready"), 1)
                act.wait_ge(*at("l2_h2_projected", n + 1))
                nc.scalar.activation(h2[:], bank(7), ACT.Gelu).then_inc(sig("l2_h2_ready"), 1)
                if has_next:
                    act.preload_act_table(ACT.Exp)

            q_bias(0)
            act.wait_ge(*at("gate_keys_projected", 1))
            for c in range(CH):
                last = nc.scalar.activation(z_t[:, c, :], ps[:, 2, c * P:(c + 1) * P], ACT.Identity,
                                            bias=cols[:, GATEB, c:c + 1])
            last.then_inc(sig("gate_keys_ready"), 1)
            act.wait_ge(*at("gate_max_ready", 1))
            nc.scalar.activation(gate8[:], ps[:, 5, 0:E], ACT.Exp, bias=small[:, 0:1], scale=D ** -0.5,
                                 accum_out=small[:, 1:2]).then_inc(sig("gate_exp_ready"), 1)
            with act.Fori(0, E // 2 - 1) as i:
                for u in range(2):
                    expert_act(i * 2 + u, True)
            expert_act(E - 2, True)
            expert_act(E - 1, False)

            layer_norm_t(6)
            for k in range(3):
                act.wait_ge(*at("gcn_h_projected", 2 * k + 1))
                nc.scalar.copy(ctxv[:, 0:D // 2], ps[:, 0, 0:D // 2]).then_inc(sig("gcn_h_ready0"), 1)
                if k < 2:
                    act.wait_ge(*at("gcn_mixed", 2 * k + 1))
                    for c in range(2):
                        last = nc.scalar.activation(z_t[:, c, :], ps[:, 1, c * P:(c + 1) * P], ACT.Relu,
                                                    bias=cols[:, GCNB1 + k, c:c + 1])
                    last.then_inc(sig("gcn_z_ready0"), 1)

            layer_norm_t(7)
            act.wait_ge(*at("router_max_ready", 1))
            nc.scalar.activation(gate8[:], gated[:], ACT.Exp, bias=small[:, 0:1]).then_inc(sig("router_exp_ready"), 1)

            def lstm_act(n):
                for j, (tile, bias, scale, first) in enumerate((
                        (prob[:, 0:4, :], lstm_hb, 0.5, 0), (prob[:, 4:8, :], lstm_b, 1.0, 8),
                        (prob_t[:, 0:4, :], lstm_hb, 0.5, 12))):
                    act.wait_ge(*at("l3_gates_projected", n * 3 + (j + 1)))
                    if j == 2:
                        act.wait_ge(*at("l3_h_ready", n + 1))
                    for c in range(CH):
                        last = nc.scalar.activation(tile[:, c, :], ps[:, j, c * P:(c + 1) * P], ACT.Tanh,
                                                    bias=bias[:, bass.ds(n * 16 + (first + c), 1)], scale=scale)
                    last.then_inc(sig("l3_gate_ready"), 1)
                act.wait_ge(*at("l3_cell_ready", n + 1))
                nc.scalar.activation(prob_t[:, 4:8, :].rearrange("p c n -> p (c n)"), t1[:], ACT.Tanh, scale=0.5) \
                    .then_inc(sig("l3_cell_tanh_ready"), 1)

            with act.Fori(0, E) as n:
                lstm_act(n)

        @block.tensor
        def _(pe):
            def weights(name):
                pe.wait_ge(*at(f"dense_landed{DENSE.index(name) % SLOTS}", landed[name]))

            def keep_clock(b, times=8):
                for _ in range(times):
                    pe.matmul(ps[:, b, 3 * P:4 * P], ident[:], ident[:], start=True, stop=True)

            def layer_norm_transpose(k):
                for half in range(2):
                    pe.wait_ge(*at("y_ready", 2 * k + half + 1))
                    for c in range(2):
                        f = (2 * half + c) * P
                        last = pe.transpose(ps[:, 7 - half, c * P:(c + 1) * P], y[:, f:f + P], ident[:])
                    last.then_inc(sig("y_transposed"), 1)

            def project_term(b, in_t, w, c):
                return pe.matmul(bank(b), in_t[:, c, :], w[:, c, :], start=(c == 0), stop=(c == CH - 1))

            def project(b, in_t, w):
                for c in range(CH):
                    last = project_term(b, in_t, w, c)
                return last

            def project_t(b, in_t, w, chunks=CH, first=0, n=P):
                for m in range(chunks):
                    for c in range(CH):
                        last = pe.matmul(ps[:, b, m * n:(m + 1) * n], w[:, c, (first + m) * P:(first + m + 1) * P],
                                         in_t[:, c, 0:n], start=(c == 0), stop=(c == CH - 1))
                return last

            def scores(done):
                for g in range(4):
                    for a in range(2):
                        r = slice(DH * a, DH * a + DH)
                        last = pe.matmul(ps[:, 3 + a, g * P:(g + 1) * P], qk_t[r, g, :], qk_t[r, CH + g, :],
                                         start=True, stop=True)
                        if g == 3:
                            last.then_inc(sig(done), 1)

            def transpose_half(ready, done, n, a, b):
                pe.wait_ge(*at(ready, n * 2 + (a + 1)))
                for g in range(4):
                    last = pe.transpose(ps[:, b, g * P:(g + 1) * P], prob[:, 4 * a + g, :], ident[:])
                last.then_inc(sig(done), 1)

            def attend(b, ready0, ready1, n):
                for a in range(2):
                    pe.wait_ge(*at((ready0, ready1)[a], n + 1))
                    for g in range(4):
                        h = 2 * g + a
                        last = pe.matmul(ps[DH * a:DH * a + DH, b, g * P:(g + 1) * P], v[:, h * DH:(h + 1) * DH],
                                         prob_t[:, 4 * a + g, :], start=True, stop=True)
                return last

            def transpose_rows(b, rows):
                for c in range(CH):
                    last = pe.transpose(ps[:, b, c * P:(c + 1) * P], rows[:, c * P:(c + 1) * P], ident[:])
                return last

            pe.wait_ge(*at("const_ready", 3))
            keep_clock(6, times=14)
            layer_norm_transpose(0)
            pe.wait_ge(*at("y_t_ready", 1))
            weights("l0_W")
            last = project(0, y_t, matrix("l0_W"))
            last.then_inc(sig("gat_h_projected"), 1)
            pe.wait_ge(*at("one_hot_ready", 2))
            for t in range(EDGES_PER_PARTITION):
                last = pe.matmul(ps[:, 5, 0:P], one_hot[:, 0, t, :], one_hot[:, 1, t, :],
                                 start=(t == 0), stop=(t == EDGES_PER_PARTITION - 1))
            last.then_inc(sig("edges_counted"), 1)
            pe.wait_ge(*at("gat_s_ready", 2))
            pe.transpose(ps[0:40, 1, 0:P], s_cat[:], ident[:]).then_inc(sig("gat_s_transposed"), 1)
            pe.wait_ge(*at("gat_lr_ready", 2))
            for a in range(2):
                last = pe.matmul(ps[:, 3 + a, :], gat_l[:], gat_r[:, 4 * a:4 * a + 4, :], start=True, stop=True)
            last.then_inc(sig("gat_scored"), 1)
            pe.wait_ge(*at("gat_prob_ready", 4))
            for h in range(H):
                if h >= 4:
                    pe.wait_ge(*at("gat_prob_ready", h + 1))
                last = pe.transpose(ps[:, 5 + h // 4, h % 4 * P:(h % 4 + 1) * P], prob[:, h, :], ident[:])
                if h % 4 == 3:
                    last.then_inc(sig("gat_prob_transposed"), 1)
            pe.wait_ge(*at("gat_h_ready", 1))
            for h in range(H):
                if h % 4 == 0:
                    pe.wait_ge(*at(f"gat_prob_t_ready{h // 4}", 1))
                last = pe.matmul(ps[:, 0, h * DH:(h + 1) * DH], prob_t[:, h, :], v[:, h * DH:(h + 1) * DH],
                                 start=True, stop=True)
            last.then_inc(sig("gat_attended"), 1)

            for c in range(CH):
                if c % 2 == 0:
                    pe.wait_ge(*at("y_ready", 3 + c // 2))
                last = pe.matmul(ps[:, 2, c:c + 1], y[:, c * P:(c + 1) * P], ones[:, 0:1], start=True, stop=True)
            last.then_inc(sig("route_summed"), 1)
            pe.wait_ge(*at("route_mean_ready", 1))
            pe.wait_ge(*at("router_landed", 64))
            for c in range(CH):
                last = pe.matmul(ps[:, 2, 8:9], r_w1[:, c, :], r_mean[:, c:c + 1], start=(c == 0), stop=(c == CH - 1))
            last.then_inc(sig("route_hidden_summed"), 1)
            layer_norm_transpose(1)
            pe.wait_ge(*at("route_hidden_ready", 1))
            pe.matmul(ps[0:1, 2, 16:19], r_hcol[:], r_w2[:], start=True, stop=True).then_inc(sig("route_logits_summed"), 1)
            pe.wait_ge(*at("counts_ready", 1))
            pe.transpose(ps[:, 5, 0:P], cnt_sd[:], ident[:]).then_inc(sig("counts_transposed"), 1)
            pe.wait_ge(*at("adjacency_ready", 2))
            pe.transpose(ps[:, 6, 0:P], mean_ds[:], ident[:])
            pe.transpose(ps[:, 6, P:2 * P], gcn_ds[:], ident[:]).then_inc(sig("adjacency_transposed"), 1)

            def selected_weights(name):
                pe.wait_ge(*at(f"gqa_{name}_landed", 16))
                k = ("wq", "wk", "wv", "wo").index(name)
                return ew[:, 0, k * CH * D:(k + 1) * CH * D].rearrange("p (c n) -> p c n", c=CH)

            pe.wait_ge(*at("y_t_ready", 2))
            wq = ew[:, 0, 0:CH * D].rearrange("p (m c n) -> p m c n", m=CH, c=CH)
            for m in range(CH):
                if m < 2:
                    pe.wait_ge(*at("gqa_wq_landed" if m else "gqa_wq_first_landed", 16))
                for c in range(CH):
                    last = pe.matmul(ps[:, 0, m * P:(m + 1) * P], wq[:, m, c, :], y_t[:, c, :],
                                     start=(c == 0), stop=(c == CH - 1))
            last.then_inc(sig("gqa_q_projected"), 1)
            project_t(1, y_t, selected_weights("wk")).then_inc(sig("gqa_k_projected"), 1)
            wv = selected_weights("wv")
            project_term(2, y_t, wv, 0)
            pe.wait_ge(*at("gqa_q_ready", 1))
            pe.wait_ge(*at("gqa_k_ready", 1))
            scores("gqa_scored")
            for c in range(1, CH):
                last = project_term(2, y_t, wv, c)
            last.then_inc(sig("gqa_v_projected"), 1)
            for a in range(2):
                transpose_half("gqa_prob_ready", "gqa_prob_transposed", 0, a, 5 + 2 * a)
            pe.wait_ge(*at("gqa_v_ready", 1))
            attend(4, "gqa_prob_t_ready0", "gqa_prob_t_ready1", 0).then_inc(sig("gqa_attended"), 1)
            pe.wait_ge(*at("gqa_ctx_t_ready", 1))
            project(6, ctx_t, selected_weights("wo")).then_inc(sig("gqa_o_projected"), 1)

            keep_clock(7)
            layer_norm_transpose(2)
            pe.wait_ge(*at("y_t_ready", 3))
            weights("perf_wq")
            project_t(0, y_t, matrix("perf_wq"))
            weights("perf_wk")
            project_t(3, y_t, matrix("perf_wk")).then_inc(sig("perf_qk_projected"), 1)
            pe.wait_ge(*at("perf_rows_ready", 1))
            weights("perf_wv")
            project(1, x1_t, matrix("perf_wv")).then_inc(sig("perf_v_projected"), 1)
            pe.wait_ge(*at("perf_t_ready", 1))
            pe.wait_ge(*at("params_landed", 48))
            def performer_products(w):
                for g in range(4):
                    last = pe.matmul(ps[:, 4 + 2 * w + g // 2, (g % 2) * PERF_M:(g % 2 + 1) * PERF_M],
                                     qk_t[:, 4 * w + g, :], proj_t[:], start=True, stop=True)
                last.then_inc(sig("perf_k_products" if w else "perf_q_products"), 1)

            performer_products(1)
            pe.wait_ge(*at("perf_sq_ready", 1))
            for s in range(8):
                last = pe.matmul(ps[:, 0, s:s + 1], prob[:, s, :], ones[:, 0:1], start=True, stop=True)
            last.then_inc(sig("perf_diag_summed"), 1)
            pe.wait_ge(*at("perf_kmax_ready", 1))
            pe.transpose(ps[0:4, 2, P:2 * P], small[:, 4:8], ident[:]).then_inc(sig("perf_kmax_transposed"), 1)
            performer_products(0)
            pe.wait_ge(*at("perf_kmax_rows_ready", 1))
            pe.matmul(ps[:, 2, 2 * P:2 * P + 4], perf_r[:].rearrange("g a n -> g (a n)"), ident[0:4, 0:4],
                      start=True, stop=True).then_inc(sig("perf_kmax_spread"), 1)
            pe.wait_ge(*at("bn_out_ready", CH))
            weights("conv")
            project(3, z_t, matrix("conv")).then_inc(sig("conv_h_projected"), 1)
            pe.wait_ge(*at("perf_features_ready", 1))
            pe.wait_ge(*at("perf_v_ready", 1))
            pair = 2 * (DH + 1)
            for m in range(2):
                for g in range(4):
                    last = pe.matmul(ps[:, KV_BANKS[2 * m + g // 2], g % 2 * pair:(g % 2 + 1) * pair],
                                     wide[:, 1, g * PERF_M + m * P:g * PERF_M + (m + 1) * P], pair_v[:, g],
                                     start=True, stop=True)
            last.then_inc(sig("perf_kv_done"), 1)
            pe.wait_ge(*at("perf_features_ready", 2))
            for g in range(4):
                for m in range(2):
                    s = 2 * g + m
                    last = pe.transpose(ps[:, 4 + s // 4, s % 4 * P:(s % 4 + 1) * P],
                                        wide[:, 0, g * PERF_M + m * P:g * PERF_M + (m + 1) * P], ident[:])
            last.then_inc(sig("perf_q_transposed"), 1)
            pe.wait_ge(*at("conv_h_ready", 1))
            pe.wait_ge(*at("mean_sd_ready", 1))
            for c in range(CH):
                last = pe.matmul(ps[:, 3, c * P:(c + 1) * P], ctxv[:, c * P:(c + 1) * P], mean_sd[:],
                                 start=True, stop=True)
            last.then_inc(sig("conv_mixed"), 1)
            pe.wait_ge(*at("perf_kv_ready", 2))
            pe.wait_ge(*at("perf_kv_ready_act", 2))
            pe.wait_ge(*at("perf_q_t_ready0", 1))
            pe.wait_ge(*at("perf_q_t_ready1", 1))
            for g in range(4):
                for m in range(2):
                    last = pe.matmul(ps[:, 4 + 3 * (g // 2), g % 2 * pair:(g % 2 + 1) * pair], prob_t[:, 2 * g + m, :],
                                     kv_sb[:, 2 * m + g // 2, g % 2 * pair:(g % 2 + 1) * pair],
                                     start=(m == 0), stop=(m == 1))
            last.then_inc(sig("perf_attended"), 1)
            pe.wait_ge(*at("perf_ctx_ready", 1))
            for a in range(2):
                r = slice(DH * a, DH * a + DH)
                for g in range(4):
                    last = pe.matmul(ps[r, a, g * PERF_N:(g + 1) * PERF_N], ctxv[r, g * DH:(g + 1) * DH], ident[r, r],
                                     start=True, stop=True)
            last.then_inc(sig("perf_ctx_transposed"), 1)
            pe.wait_ge(*at("perf_ctx_t_ready0", 1))
            pe.wait_ge(*at("perf_ctx_t_ready1", 1))
            weights("perf_wo")
            for half in range(2):
                project_t(3 + 2 * half, x1_t, matrix("perf_wo"), chunks=2, first=2 * half) \
                    .then_inc(sig("perf_o_projected"), 1)
            for c in range(CH):
                pe.wait_ge(*at("bn_out_ready", 1 * CH + c + 1))
                last = pe.transpose(ps[:, 2, c * P:(c + 1) * P], z_t[:, c, :], ident[:])
            last.then_inc(sig("gps_out_transposed"), 1)

            keep_clock(6)
            layer_norm_transpose(3)
            pe.wait_ge(*at("y_t_ready", 4))
            weights("peer_wq")
            project_t(0, y_t, matrix("peer_wq"), chunks=2).then_inc(sig("peer_q_projected"), 1)
            project_t(5, y_t, matrix("peer_wq"), chunks=2, first=2).then_inc(sig("peer_q_projected"), 1)
            pe.wait_ge(*at("peer_q_ready", 1))
            pe.wait_ge(*at("late_params_landed", 160))
            for r in range(4):
                rows = slice(32 * r, 32 * r + 32)
                for q in range(2):
                    last = pe.matmul(ps[:, 1 + r, q * KEYS:(q + 1) * KEYS], qk_t[rows, q, :], keys_t[rows, q, :],
                                     start=True, stop=True, tile_position=(32 * r, 0))
                last.then_inc(sig("peer_sim_ready"), 1)
            weights("peer_tables")
            pe.wait_ge(*at("peer_q_rest_ready", 1))
            for m in range(2):
                for c in range(CH):
                    last = pe.matmul(ps[:, 5, m * P:(m + 1) * P], peer_down[:, c, m * P:(m + 1) * P], qk_t[:, c, :],
                                     start=(c == 0), stop=(c == CH - 1))
            last.then_inc(sig("peer_down_projected"), 1)
            for h in range(H):
                pe.wait_ge(*at("peer_masked", h + 1))
                pe.wait_ge(*at(f"peer_diag_ready{h % 2}", h // 2 + 1))
                for m in range(2):
                    last = pe.matmul(ps[:, 6 + m, 0:P], peer_pick[:, h % 4, m * P:(m + 1) * P], x1_t[:, h % 2, :],
                                     start=(h == 0), stop=(h == H - 1))
                last.then_inc(sig("peer_head_added"), 1)
            pe.wait_ge(*at("peer_weights_ready", 1))
            for m in range(2):
                last = pe.matmul(bank(0), z_t[:, m, :], peer_up[:, m, :], start=(m == 0), stop=(m == 1))
            last.then_inc(sig("peer_up_projected"), 1)

            keep_clock(7)
            layer_norm_transpose(4)
            pe.wait_ge(*at("y_t_ready", 5))
            weights("exph_wq")
            project_t(0, y_t, matrix("exph_wq")).then_inc(sig("exph_q_projected"), 1)
            weights("exph_wk")
            project_t(1, y_t, matrix("exph_wk")).then_inc(sig("exph_k_projected"), 1)
            weights("exph_wv")
            project_term(2, y_t, matrix("exph_wv"), 0)
            pe.wait_ge(*at("exph_q_ready", 1))
            pe.wait_ge(*at("exph_k_ready", 1))
            for a in range(2):
                r = slice(DH * a, DH * a + DH)
                for g in range(4):
                    last = pe.matmul(ps[:, 3 + a, g * P:(g + 1) * P], qk_t[r, CH + g, :], qk_t[r, g, :],
                                     start=True, stop=True)
                last.then_inc(sig("exph_scored"), 1)
            for c in range(1, CH):
                last = project_term(2, y_t, matrix("exph_wv"), c)
            last.then_inc(sig("exph_v_projected"), 1)
            pe.wait_ge(*at("exph_v_ready", 1))
            for a in range(2):
                pe.wait_ge(*at("exph_weights_ready", a + 1))
                for g in range(4):
                    last = pe.matmul(ps[:, 5 + a, g * (DH + 1):(g + 1) * (DH + 1)], prob_t[:, 4 * a + g, :],
                                     heads_v[:, 2 * g + a, :], start=True, stop=True)
            last.then_inc(sig("exph_attended"), 1)
            pe.wait_ge(*at("exph_h_ready", 1))
            transpose_rows(0, ctxv).then_inc(sig("exph_h_transposed"), 1)
            for c in range(CH):
                pe.wait_ge(*at("bn_out_ready", 2 * CH + c + 1))
                last = pe.transpose(ps[:, 1, c * P:(c + 1) * P], z_t[:, c, :], ident[:])
            last.then_inc(sig("exph_out_transposed"), 1)

            keep_clock(7)
            layer_norm_transpose(5)
            pe.wait_ge(*at("y_t_ready", 6))

            def expert_q(n, u, it):
                pe.wait_ge(*at(f"l2_wqk_landed{u}", it * 16 + 16))
                project_t(0, y_t, l2_wqk(u)).then_inc(sig("l2_qk_projected"), 1)

            def expert_k(u, parts):
                for m in parts:
                    for c in range(CH):
                        last = pe.matmul(ps[:, 1, m * P:(m + 1) * P], l2_wqk(u)[:, c, (CH + m) * P:(CH + m + 1) * P],
                                         y_t[:, c, :], start=(c == 0), stop=(c == CH - 1))
                if m == CH - 1:
                    last.then_inc(sig("l2_qk_projected"), 1)

            def expert_v(u, parts):
                for c in parts:
                    last = project_term(2, y_t, l2_wv(u), c)
                if c == CH - 1:
                    last.then_inc(sig("l2_v_projected"), 1)

            def expert_scores(n):
                pe.wait_ge(*at("l2_q_ready", n + 1))
                pe.wait_ge(*at("l2_k_ready", n + 1))
                scores("l2_scored")

            def expert_pe(n, u, it, next_it, has_next):
                if has_next:
                    expert_q(n + 1, 1 - u, next_it)
                for a in range(2):
                    if has_next:
                        expert_k(1 - u, (a,))
                    transpose_half("l2_prob_ready", "l2_prob_transposed", n, a, 5 + a)
                if has_next:
                    expert_k(1 - u, (2,))
                pe.wait_ge(*at("l2_v_ready", n + 1))
                pe.wait_ge(*at("l2_h2_ready", n + 1))
                attend(7, "l2_prob_t_ready0", "l2_prob_t_ready1", n).then_inc(sig("l2_attended"), 1)
                if has_next:
                    expert_k(1 - u, (3,))
                pe.wait_ge(*at("l2_ctx_t_ready", n + 1))
                pe.wait_ge(*at(f"l2_wo_landed{u}", it * 16 + 16))
                for half in range(2):
                    for c in range(CH):
                        last = pe.matmul(ps[:, 4 + half, 0:D // 2], ctx_t[:, c, :],
                                         wo_of(u)[:, c, half * D // 2:(half + 1) * D // 2],
                                         start=(c == 0), stop=(c == CH - 1))
                    last.then_inc(sig("l2_o_projected"), 1)
                if has_next:
                    pe.wait_ge(*at(f"l2_wv_landed{1 - u}", next_it * 16 + 16))
                    expert_v(1 - u, range(CH - 1))
                for c in range(CH):
                    if c % 2 == 0:
                        pe.wait_ge(*at("l2_x1_ready", n * 2 + (c // 2 + 1)))
                    last = pe.transpose(ps[:, 5, c * P:(c + 1) * P], x1[:, c * P:(c + 1) * P], ident[:])
                last.then_inc(sig("l2_x1_transposed"), 1)
                if has_next:
                    expert_v(1 - u, (CH - 1,))
                pe.wait_ge(*at("l2_x1_t_ready", n + 1))
                pe.wait_ge(*at(f"l2_small_landed{u}", it * 32 + 32))
                for c in range(CH):
                    last = pe.matmul(ps[0:F2, 6, 0:P], ew1[:, u, c, :], x1_t[:, c, :], start=(c == 0), stop=(c == CH - 1))
                last.then_inc(sig("l2_h1_projected"), 1)
                if has_next:
                    expert_scores(n + 1)
                pe.wait_ge(*at("l2_h1_ready", n + 1))
                pe.matmul(bank(7), h1_t[:], ew2[:, u, :], start=True, stop=True).then_inc(sig("l2_h2_projected"), 1)

            expert_q(0, 0, 0)
            weights("gate_wk")
            project_t(2, y_t, matrix("gate_wk")).then_inc(sig("gate_keys_projected"), 1)
            expert_k(0, range(CH))
            pe.wait_ge(*at("gate_keys_ready", 1))
            for c in range(CH):
                last = pe.matmul(ps[:, 5, 0:E], z_t[:, c, :], eq_t[:, c, :], start=(c == 0), stop=(c == CH - 1))
            last.then_inc(sig("gate_scored"), 1)
            expert_scores(0)
            pe.wait_ge(*at("l2_wv_landed0", 16))
            expert_v(0, range(CH))
            pe.wait_ge(*at("gated_ready", 1))
            pe.transpose(ps[0:E, 7, 0:P], gated[:], ident[:]).then_inc(sig("gated_transposed"), 1)
            pe.wait_ge(*at("gated_t_ready", 1))
            pe.matmul(bank(7), gated_t[:], be2[:], start=True, stop=True).then_inc(sig("be2_shared"), 1)
            with pe.Fori(0, E // 2 - 1) as i:
                for u in range(2):
                    expert_pe(i * 2 + u, u, i, i + u, True)
            expert_pe(E - 2, 0, E // 2 - 1, E // 2 - 1, True)
            expert_pe(E - 1, 1, E // 2 - 1, None, False)

            keep_clock(6)
            layer_norm_transpose(6)
            pe.wait_ge(*at("y_t_ready", 7))
            pe.wait_ge(*at("gcn_sd_ready", 1))
            for k in range(3):
                weights(f"gcn_w{k + 1}")
                for half in range(2):
                    for c in range(CH):
                        if k and half == 0 and c % 2 == 0:
                            pe.wait_ge(*at(f"gcn_z_ready{c // 2}", k))
                        last = pe.matmul(ps[:, 2 * half, 0:D // 2], (z_t if k else y_t)[:, c, :],
                                         matrix(f"gcn_w{k + 1}")[:, c, half * D // 2:(half + 1) * D // 2],
                                         start=(c == 0), stop=(c == CH - 1))
                    last.then_inc(sig("gcn_h_projected"), 1)
                for half in range(2):
                    pe.wait_ge(*at(f"gcn_h_ready{half}", k + 1))
                    if k < 2:
                        for c in range(2):
                            last = pe.matmul(ps[:, 1 + 2 * half, c * P:(c + 1) * P],
                                             ctxv[:, (2 * half + c) * P:(2 * half + c + 1) * P], gcn_sd[:],
                                             start=True, stop=True)
                    else:
                        last = pe.matmul(ps[:, 1 + 2 * half, 0:D // 2], gcn_sd[:], ctxv[:, half * D // 2:(half + 1) * D // 2],
                                         start=True, stop=True)
                    last.then_inc(sig("gcn_mixed"), 1)

            keep_clock(7)
            layer_norm_transpose(7)
            pe.wait_ge(*at("y_t_ready", 8))
            def lstm_gates(n, u, it, gates=range(3)):
                for j in gates:
                    w, first, landed_by = ((l3_wi(u), 0, "l3_wi_landed"), (l3_wgo(u), 0, "l3_wgo_landed"),
                                           (l3_wgo(u), CH, "l3_wgo_landed"))[j]
                    if j < 2:
                        pe.wait_ge(*at(f"{landed_by}{u}", it * 16 + 16))
                    if not isinstance(n, int) or n > 0:
                        pe.wait_ge(*at("l3_gate_ready", n * 3 + (j - 2)))
                    project_t(j, y_t, w, first=first).then_inc(sig("l3_gates_projected"), 1)

            def lstm_out(n, u, it):
                pe.wait_ge(*at("l3_h_ready", n + 2))
                pe.wait_ge(*at(f"l3_wo_landed{u}", it * 16 + 16))
                if not isinstance(n, int) or n > 0:
                    pe.wait_ge(*at("l3_expert_added", n))
                project(3 + u, h_t[u], wo_of(u)).then_inc(sig("l3_o_projected"), 1)

            lstm_gates(0, 0, 0, (0,))
            for c in range(CH):
                last = pe.matmul(ps[:, 6, 0:E], y_t[:, c, :], router_w[:, c, :], start=(c == 0), stop=(c == CH - 1))
            last.then_inc(sig("router_scored"), 1)
            lstm_gates(0, 0, 0, (1,))
            pe.wait_ge(*at("lstm_gated_ready", 1))
            pe.transpose(ps[0:E, 5, 0:P], gated[:], ident[:]).then_inc(sig("lstm_gated_transposed"), 1)
            lstm_gates(0, 0, 0, (2,))
            pe.wait_ge(*at("lstm_gated_t_ready", 1))
            pe.matmul(bank(7), gated_t[:], lstm_bo[:], start=True, stop=True).then_inc(sig("lstm_bo_shared"), 1)
            lstm_gates(1, 1, 0)
            lstm_out(0, 0, 0)
            with pe.Fori(1, E // 2) as i:
                for u in range(2):
                    lstm_gates(i * 2 + u, u, i)
                    lstm_out(i * 2 + (u - 1), 1 - u, i + (u - 1))
            lstm_out(E - 1, 1, E // 2 - 1)

        @block.vector
        def _(dve):
            settle = dve.drain

            def layer_norm(k):
                settle()
                dve.bn_stats(ln_st[:], x[:])
                settle()
                dve.bn_aggr(ln_mv[:], ln_st[:])
                settle()
                dve.tensor_scalar_add(ln_var[:], ln_mv[:, 1:2], EPS).then_inc(sig("ln_var_ready"), 1)
                dve.wait_ge(*at("ln_rstd_ready", k + 1))
                for half in (slice(0, D // 2), slice(D // 2, D)):
                    dve.tensor_scalar(y[:, half], x[:, half], ln_mv[:, 0:1], ln_rstd[:], ALU.subtract, ALU.mult) \
                        .then_inc(sig("y_ready"), 1)

            def node_statistics(in_t, chunks=range(CH)):
                settle()
                for c in chunks:
                    dve.bn_stats(bn_st[:, c, :], in_t[:, c, :])

            def batch_norm(k, in_t, gamma, beta):
                settle()
                for c in range(CH):
                    dve.bn_aggr(bn_mv[:, c, :], bn_st[:, c, :])
                settle()
                dve.tensor_scalar_add(bn_var[:], bn_mv[:, :, 1], EPS).then_inc(sig("bn_var_ready"), 1)
                dve.tensor_tensor(bn_shift[:], bn_mv[:, :, 0], cols[:, gamma, :], ALU.mult)
                settle()
                dve.wait_ge(*at("bn_rstd_ready", k + 1))
                dve.tensor_tensor(bn_scale[:], bn_rstd[:], cols[:, gamma, :], ALU.mult)
                dve.tensor_tensor(bn_shift[:], bn_rstd[:], bn_shift[:], ALU.mult)
                settle()
                dve.tensor_tensor(bn_shift[:], cols[:, beta, :], bn_shift[:], ALU.subtract)
                settle()
                for c in range(CH):
                    dve.tensor_scalar(z_t[:, c, :], in_t[:, c, :], bn_scale[:, c:c + 1], bn_shift[:, c:c + 1],
                                      ALU.mult, ALU.add).then_inc(sig("bn_out_ready"), 1)

            def maxima(scored, done, n, scale):
                for a in range(2):
                    s = slice(4 * a, 4 * a + 4)
                    dve.wait_ge(*at(scored, n * 2 + (a + 1)))
                    dve.tensor_reduce(nmax[:, s], bank_chunks(3 + a), AX.X, ALU.max, negate=True)
                    settle()
                    dve.tensor_scalar(nmax_s[:, s], nmax[:, s], scale, None, ALU.mult).then_inc(sig(done), 1)

            def normalise(exps_done, done, n):
                for a in range(2):
                    s = slice(4 * a, 4 * a + 4)
                    dve.wait_ge(*at(exps_done, n * 2 + (a + 1)))
                    dve.reciprocal(rinv[:, s], rsum[:, s])
                    settle()
                    dve.tensor_tensor(prob[:, s, :], prob[:, s, :], rinv[:, s].unsqueeze(2).broadcast_to([P, 4, P]),
                                      ALU.mult).then_inc(sig(done), 1)

            dve.memset(s_cat[:], 0.0)
            dve.memset(gat_l[:], 0.0)
            dve.memset(h1_t[:], 1.0)
            settle()
            dve.memset(gat_l[32:40], 1.0)
            dve.wait_ge(*at("x_landed", 16))
            layer_norm(0)
            dve.wait_ge(*at("edges_landed", 32))
            dve.wait_ge(*at("iota_ready", 1))
            dve.tensor_copy(src_f[:], src_i[:])
            dve.tensor_copy(dst_f[:], dst_i[:])
            dve.tensor_copy(iota_f[:], iota_i[:])
            settle()
            for k, ends in enumerate((src_f, dst_f)):
                dve.tensor_tensor(one_hot[:, k, :, :],
                                  iota_f[:].unsqueeze(1).broadcast_to([P, EDGES_PER_PARTITION, P]),
                                  ends[:].unsqueeze(2).broadcast_to([P, EDGES_PER_PARTITION, P]),
                                  ALU.is_equal).then_inc(sig("one_hot_ready"), 1)
            dve.wait_ge(*at("gat_h_projected", 1))
            dve.wait_ge(*at("gat_a_landed", 16))
            for k in range(2):
                dve.tensor_tensor(wide[:, k, 0:D], bank(0), attn_a[:, k, :], ALU.mult)
            settle()
            for k in range(2):
                dve.tensor_reduce(s_cat[:, 32 * k:32 * k + H], wide[:, k, 0:D].rearrange("p (h d) -> p h d", h=H),
                                  AX.X, ALU.add).then_inc(sig("gat_s_ready"), 1)
            settle()
            dve.memset(small[:, 2:3], 0.0).then_inc(sig("gat_a_used"), 1)
            dve.wait_ge(*at("gat_s_transposed", 1))
            dve.tensor_copy(gat_l[0:H], ps[0:H, 1, 0:P]).then_inc(sig("gat_lr_ready"), 1)
            dve.wait_ge(*at("gat_r_ready", 2))
            dve.tensor_tensor(gat_r[32:32 + H], gat_r[32:32 + H],
                              ps[32:32 + H, 1, 0:P].unsqueeze(1).broadcast_to([H, H, P]), ALU.mult) \
                .then_inc(sig("gat_lr_ready"), 1)
            dve.wait_ge(*at("edges_counted", 1))
            dve.wait_ge(*at("const_ready", 3))
            dve.tensor_copy(cnt_sd[:], ps[:, 5, 0:P]).then_inc(sig("counts_ready"), 1)
            dve.tensor_tensor(gat_cap[:], ps[:, 5, 0:P], ident[:], ALU.add)
            settle()
            dve.tensor_scalar(gat_cap[:], gat_cap[:], 1.0, -2.0 * GAT_NEG, ALU.min, ALU.mult)
            settle()
            dve.tensor_scalar(gat_cap[:], gat_cap[:], GAT_NEG, None, ALU.add)
            settle()
            for a in range(2):
                s = slice(4 * a, 4 * a + 4)
                dve.wait_ge(*at("gat_leak_ready", a + 1))
                dve.tensor_tensor(prob[:, s, :].rearrange("p h n -> p (h n)"), bank(3 + a), wide[:, a, 0:512], ALU.max)
                settle()
                dve.tensor_tensor(prob[:, s, :], prob[:, s, :], gat_cap[:].unsqueeze(1).broadcast_to([P, 4, P]), ALU.min)
                settle()
                dve.tensor_reduce(nmax[:, s], prob[:, s, :], AX.X, ALU.max, negate=True).then_inc(sig("gat_max_ready"), 1)
            dve.wait_ge(*at("gat_prob_transposed", 1))
            dve.tensor_copy(prob_t[:, 0:4, :].rearrange("p h n -> p (h n)"), bank(5)).then_inc(sig("gat_prob_t_ready0"), 1)
            dve.wait_ge(*at("gat_prob_ready", 8))
            dve.reciprocal(rinv[:], rsum[:])
            settle()
            dve.wait_ge(*at("gat_attended", 1))
            dve.tensor_tensor(ctxv[:].rearrange("p (h d) -> p h d", h=H), bank_heads(0),
                              rinv[:].unsqueeze(2).broadcast_to([P, H, DH]), ALU.mult)
            settle()
            dve.tensor_reduce(small[:, 0:1], ctxv[:], AX.X, ALU.max, negate=True).then_inc(sig("gat_out_ready"), 1)
            dve.wait_ge(*at("gat_exp_ready", 1))
            dve.reciprocal(small[:, 2:3], small[:, 1:2])
            settle()
            dve.scalar_tensor_tensor(x[:], t1[:], small[:, 2:3], x[:], ALU.mult, ALU.add).then_inc(sig("x_updated"), 1)

            layer_norm(1)
            dve.memset(r_p[0:1, 3:8], -1.0)
            dve.wait_ge(*at("route_summed", 1))
            dve.tensor_scalar(r_mean[:], ps[:, 2, 0:CH], 1.0 / P, None, ALU.mult).then_inc(sig("route_mean_ready"), 1)
            dve.wait_ge(*at("router_landed", 64))
            dve.wait_ge(*at("route_hidden_summed", 1))
            dve.tensor_scalar(r_hcol[:], ps[:, 2, 8:9], r_b1[:], 0.0, ALU.add, ALU.max).then_inc(sig("route_hidden_ready"), 1)
            dve.wait_ge(*at("route_logits_summed", 1))
            dve.tensor_tensor(r_p[0:1, 0:3], ps[0:1, 2, 16:19], r_b2[:], ALU.add)
            settle()
            dve.tensor_reduce(small[0:1, 0:1], r_p[0:1, 0:3], AX.X, ALU.max, negate=True) \
                .then_inc(sig("route_logits_ready"), 1)
            dve.wait_ge(*at("route_exp_ready", 1))
            dve.reciprocal(small[0:1, 2:3], small[0:1, 1:2])
            settle()
            dve.tensor_scalar(r_p[0:1, 0:3], r_p[0:1, 0:3], small[0:1, 2:3], None, ALU.mult)
            settle()
            dve.max(r_top[:], r_p[0:1, :])
            settle()
            dve.max_index(selected[:], r_top[:], r_p[0:1, :]).then_inc(sig("route_selected"), 1)
            dve.wait_ge(*at("counts_transposed", 1))
            dve.tensor_reduce(deg_col[:], ps[:, 5, 0:P], AX.X, ALU.add)
            dve.tensor_tensor(gcn_ds[:], ps[:, 5, 0:P], ident[:], ALU.add)
            settle()
            dve.tensor_scalar(mean_col[:], deg_col[:], 1.0, None, ALU.max)
            dve.tensor_scalar(deg_col[:], deg_col[:], 1.0, None, ALU.add).then_inc(sig("gcn_deg_ready"), 1)
            settle()
            dve.reciprocal(mean_col[:], mean_col[:])
            settle()
            dve.tensor_scalar(mean_ds[:], ps[:, 5, 0:P], mean_col[:], None, ALU.mult).then_inc(sig("adjacency_ready"), 1)
            dve.wait_ge(*at("gcn_dis_ready", 1))
            dve.tensor_scalar(gcn_ds[:], gcn_ds[:], dis_col[:], None, ALU.mult).then_inc(sig("adjacency_ready"), 1)
            dve.wait_ge(*at("adjacency_transposed", 1))
            dve.tensor_copy(mean_sd[:], ps[:, 6, 0:P]).then_inc(sig("mean_sd_ready"), 1)
            dve.tensor_scalar(gcn_sd[:], ps[:, 6, P:2 * P], dis_col[:], None, ALU.mult).then_inc(sig("gcn_sd_ready"), 1)
            dve.wait_ge(*at("gqa_k_projected", 1))
            dve.tensor_copy(qk_t[:, CH:, :].rearrange("p c n -> p (c n)"), bank(1)).then_inc(sig("gqa_k_ready"), 1)
            maxima("gqa_scored", "gqa_max_ready", 0, DH ** -0.5)
            normalise("gqa_exps_ready", "gqa_prob_ready", 0)
            dve.wait_ge(*at("gqa_v_projected", 1))
            dve.tensor_copy(v[:, 0:D], bank(2)).then_inc(sig("gqa_v_ready"), 1)
            dve.wait_ge(*at("gqa_prob_transposed", 1))
            dve.tensor_copy(prob_t[:, 0:4, :].rearrange("p h n -> p (h n)"), bank(5)).then_inc(sig("gqa_prob_t_ready0"), 1)
            dve.wait_ge(*at("gqa_attended", 1))
            dve.memset(v[:], 0.0)
            settle()
            for a in range(2):
                last = dve.memset(pair_v[DH * a:DH * a + DH, :, a, DH:DH + 1], 1.0)
            last.then_inc(sig("v_cleared"), 1)
            dve.wait_ge(*at("gqa_o_projected", 1))
            dve.tensor_tensor(x[:], x[:], bank(6), ALU.add).then_inc(sig("x_updated"), 1)

            layer_norm(2)
            dve.memset(qk_t[:], 0.0)
            dve.wait_ge(*at("y_t_ready", 3))
            dve.tensor_copy(x1_t[:].rearrange("p c (a n) -> p c a n", a=2),
                            y_t[:, :, 0:PERF_N].unsqueeze(2).broadcast_to([P, CH, 2, PERF_N])).then_inc(sig("perf_rows_ready"), 1)
            dve.wait_ge(*at("params_landed", 48))
            node_statistics(y_t)
            batch_norm(0, y_t, N1G, N1B)
            dve.wait_ge(*at("perf_qk_projected", 1))
            for a in range(2):
                r = slice(DH * a, DH * a + DH)
                for w in range(2):
                    last = dve.tensor_scalar(qk_t[r, CH * w:CH * w + CH, PERF_N * a:PERF_N * (a + 1)],
                                             ps[r, 3 * w, :].rearrange("p (s n) -> p s n", s=CH)[:, :, 0:PERF_N],
                                             DH ** -0.25, None, ALU.mult)
                last.then_inc(sig("perf_t_scaled"), 1)
            settle()
            dve.memset(small[:, 3:4], 0.0).then_inc(sig("perf_t_ready"), 1)
            dve.tensor_tensor(prob[:], qk_t[:], qk_t[:], ALU.mult).then_inc(sig("perf_sq_ready"), 1)
            def row_maxima(out, w):
                dve.tensor_reduce(out, ps[:, 4 + 2 * w:6 + 2 * w, :].rearrange("p b (g m) -> p (b g) m", m=PERF_M),
                                  AX.X, ALU.max).then_inc(sig("perf_kmax_ready" if w else "perf_qmax_ready"), 1)

            dve.wait_ge(*at("perf_k_products", 1))
            row_maxima(small[:, 4:8], 1)
            dve.wait_ge(*at("perf_kmax_transposed", 1))
            dve.tensor_reduce(perf_k2[:], ps[0:4, 2, P:2 * P].rearrange("g (a n) -> g a n", a=2), AX.X, ALU.max)
            settle()
            dve.tensor_copy(perf_r[:], perf_k2[:].unsqueeze(2).broadcast_to([4, 2, PERF_N])) \
                .then_inc(sig("perf_kmax_rows_ready"), 1)
            dve.wait_ge(*at("perf_kmax_spread", 1))
            dve.tensor_copy(small[:, 12:16], ps[:, 2, 2 * P:2 * P + 4])
            settle()
            dve.scalar_tensor_tensor(small[:, 20:24], ps[:, 0, 4:8], -0.5, small[:, 12:16], ALU.mult, ALU.subtract) \
                .then_inc(sig("perf_bias_ready1"), 1)
            dve.wait_ge(*at("perf_q_products", 1))
            row_maxima(small[:, 8:12], 0)
            settle()
            dve.scalar_tensor_tensor(small[:, 16:20], ps[:, 0, 0:4], -0.5, small[:, 8:12], ALU.mult, ALU.subtract) \
                .then_inc(sig("perf_bias_ready0"), 1)
            for w in (1, 0):
                dve.wait_ge(*at("perf_exp_ready", 2 - w))
                dve.tensor_scalar(wide[:, w, :], wide[:, w, :], PERF_M ** -0.5, PERF_EPS, ALU.mult, ALU.add) \
                    .then_inc(sig("perf_features_ready"), 1)
            dve.wait_ge(*at("perf_kv_done", 1))
            for k in (0, 2):
                dve.tensor_copy(kv_sb[:, k, :], ps[:, KV_BANKS[k], 0:4 * (DH + 1)]).then_inc(sig("perf_kv_ready"), 1)
            dve.wait_ge(*at("perf_q_transposed", 1))
            dve.tensor_copy(prob_t[:, 0:4, :].rearrange("p h n -> p (h n)"), bank(4)).then_inc(sig("perf_q_t_ready0"), 1)
            dve.wait_ge(*at("conv_t_ready", 1))
            dve.tensor_tensor(ctx_t[:], ctx_t[:], y_t[:], ALU.add)
            dve.wait_ge(*at("perf_attended", 1))
            halves = [slice(DH * a, DH * a + DH) for a in range(2)]
            num = [ps[r, 4:8:3, 0:4 * (DH + 1)].rearrange("p b (g a e) -> p b g a e", g=2, a=2)[:, :, :, a, :]
                   for a, r in enumerate(halves)]
            for a, r in enumerate(halves):
                dve.tensor_scalar(small[r, 24:28].rearrange("p (b g) -> p b g", b=2), num[a][:, :, :, DH], PERF_EPS, None,
                                  ALU.add)
            settle()
            dve.reciprocal(small[:, 24:28], small[:, 24:28])
            settle()
            for a, r in enumerate(halves):
                last = dve.tensor_tensor(
                    ctxv[r, 0:4 * DH].rearrange("p (b g d) -> p b g d", b=2, g=2), num[a][:, :, :, 0:DH],
                    small[r, 24:28].rearrange("p (b g) -> p b g", b=2).unsqueeze(3).broadcast_to([DH, 2, 2, DH]), ALU.mult)
            last.then_inc(sig("perf_ctx_ready"), 1)
            dve.wait_ge(*at("perf_ctx_transposed", 1))
            ctx_half(dve.tensor_copy, 0).then_inc(sig("perf_ctx_t_ready0"), 1)
            for half in range(2):
                dve.wait_ge(*at("perf_o_projected", half + 1))
                dve.tensor_tensor(ctx_t[:, 2 * half:2 * half + 2, :], ctx_t[:, 2 * half:2 * half + 2, :],
                                  ps[:, 3 + 2 * half, 0:2 * P].rearrange("p (c n) -> p c n", c=2), ALU.add)
                node_statistics(ctx_t, (2 * half, 2 * half + 1))
            batch_norm(1, ctx_t, N2G, N2B)
            dve.wait_ge(*at("gps_out_transposed", 1))
            dve.tensor_tensor(x[:], x[:], bank(2), ALU.add).then_inc(sig("x_updated"), 1)

            layer_norm(3)
            dve.wait_ge(*at("peer_q_projected", 1))
            dve.tensor_scalar(qk_t[:, 0:2, :].rearrange("p c n -> p (c n)"), ps[:, 0, 0:2 * P], (1.0 + EPS) ** -0.5, None,
                              ALU.mult).then_inc(sig("peer_q_ready"), 1)

            def search(k):
                tops, picks = [], []
                if k < H // 2:
                    tops = [((2 * k + j) % 4, peer_work[:, j, :], ps[:, 1 + k, j * KEYS:(j + 1) * KEYS]) for j in range(2)]
                if k > 0:
                    picks = [(h % 4, peer_work2[:, h % 2, :], h) for h in (2 * k - 2, 2 * k - 1)]
                if tops:
                    dve.wait_ge(*at("peer_sim_ready", k + 1))
                for b, work, sim in tops:
                    dve.max(topv[:, b, 0:8], sim)
                for b, work, h in picks:
                    dve.wait_ge(*at("peer_sum_ready", h + 1))
                    dve.max(best[:, b, 0:8], peer_all[:, b, :])
                settle()
                if k > 1:
                    weight_sums(k - 2)
                for b, work, h in picks:
                    dve.tensor_scalar(negbest[:, b:b + 1], best[:, b, 0:1], -1.0, None, ALU.mult) \
                        .then_inc(sig("peer_best_ready"), 1)
                for b, work, sim in tops:
                    dve.match_replace(work, topv[:, b, 0:8], sim, NEG)
                    dve.max_index(topi[:, b, 0:8], topv[:, b, 0:8], sim)
                for b, work, h in picks:
                    dve.match_replace(work, best[:, b, 0:8], peer_all[:, b, :], NEG)
                settle()
                for b, work, sim in tops:
                    dve.max(topv[:, b, 8:16], work)
                for b, work, h in picks:
                    dve.max(best[:, b, 8:16], work)
                settle()
                for b, work, sim in tops:
                    dve.max_index(topi[:, b, 8:16], topv[:, b, 8:16], work)
                for b, work, h in picks:
                    dve.match_replace(peer_rest[:, b, :], best[:, b, 8:16], work, NEG)
                settle()
                if tops:
                    two = slice(2 * k % 4, 2 * k % 4 + 2)
                    dve.tensor_copy(topif[:, two, :], topi[:, two, :]).then_inc(sig("peer_top_ready"), 1)
                for b, work, h in picks:
                    dve.wait_ge(*at("peer_exp_ready", h + 1))
                    if h >= 4:
                        dve.wait_ge(*at("peer_head_added", h - 3))
                    dve.scalar_tensor_tensor(peer_pick[:, b, :], peer_rest[:, b, :], NEG, peer_exp[:, b, :], ALU.is_equal,
                                             ALU.mult, accum_out=picksum[:, h:h + 1]).then_inc(sig("peer_masked"), 1)

            def weight_sums(k):
                dve.reciprocal(pickinv[:, 2 * k:2 * k + 2], picksum[:, 2 * k:2 * k + 2]).then_inc(sig("peer_inv_ready"), 1)

            for k in range(H // 2 + 1):
                search(k)
            settle()
            weight_sums(H // 2 - 1)
            dve.wait_ge(*at("peer_head_added", H))
            dve.wait_ge(*at("peer_gelu_ready", 1))
            for m in range(2):
                last = dve.tensor_tensor(z_t[:, m, :], ps[:, 6 + m, 0:P], x1_t[:, 2 + m, :], ALU.mult)
            last.then_inc(sig("peer_weights_ready"), 1)
            dve.wait_ge(*at("peer_up_projected", 1))
            dve.tensor_tensor(x[:], x[:], bank(0), ALU.add).then_inc(sig("x_updated"), 1)

            layer_norm(4)
            dve.memset(heads_v[:, :, DH:DH + 1], 1.0)
            dve.wait_ge(*at("exph_k_projected", 1))
            dve.tensor_copy(qk_t[:, CH:, :].rearrange("p c n -> p (c n)"), bank(1)).then_inc(sig("exph_k_ready"), 1)
            clip = 5.0 * DH ** 0.5
            for a in range(2):
                dve.wait_ge(*at("exph_scored", a + 1))
                dve.tensor_scalar(prob[:, 4 * a:4 * a + 4, :].rearrange("p h n -> p (h n)"), bank(3 + a), -clip, clip,
                                  ALU.max, ALU.min).then_inc(sig("exph_clipped"), 1)
            for a in range(2):
                s = slice(4 * a, 4 * a + 4)
                dve.wait_ge(*at("exph_exp_ready", a + 1))
                dve.tensor_tensor(prob_t[:, s, :], prob[:, s, :], cnt_sd[:].unsqueeze(1).broadcast_to([P, 4, P]), ALU.mult) \
                    .then_inc(sig("exph_weights_ready"), 1)
            dve.wait_ge(*at("exph_attended", 1))
            num = ps[:, 5:7, 0:4 * (DH + 1)].rearrange("p a (g e) -> p a g e", g=4)
            zz = small[:, 24:32].rearrange("p (a g) -> p a g", a=2)
            dve.tensor_scalar(zz, num[:, :, :, DH], 1e-6, None, ALU.add)
            settle()
            dve.reciprocal(zz, zz)
            settle()
            for a in range(2):
                last = dve.tensor_tensor(hd[:, :, a, :], num[:, a, :, 0:DH], zz[:, a, :].unsqueeze(2).broadcast_to([P, 4, DH]),
                                         ALU.mult)
            last.then_inc(sig("exph_h_ready"), 1)
            dve.wait_ge(*at("exph_h_transposed", 1))
            dve.tensor_tensor(ctx_t[:], y_t[:], bank_chunks(0), ALU.add)
            node_statistics(ctx_t)
            batch_norm(2, ctx_t, BNG, BNB)
            dve.wait_ge(*at("exph_out_transposed", 1))
            dve.tensor_tensor(x[:], x[:], bank(1), ALU.add).then_inc(sig("x_updated"), 1)

            layer_norm(5)

            def top2():
                dve.max(gtop[:], gate8[:])
                settle()
                dve.max_index(gidx[:], gtop[:], gate8[:])
                settle()
                dve.tensor_copy(gidxf[:], gidx[:])
                settle()

            def k_bias(n):
                dve.wait_ge(*at("l2_qk_projected", n * 2 + 2))
                for c in range(CH):
                    last = dve.tensor_scalar(qk_t[:, CH + c, :], ps[:, 1, c * P:(c + 1) * P],
                                             bqk[:, bass.ds(n * 8 + (CH + c), 1)], None, ALU.add)
                last.then_inc(sig("l2_k_ready"), 1)

            def v_bias(n, u, it):
                dve.wait_ge(*at(f"l2_rows_landed{u}", it * 16 + 16))
                dve.wait_ge(*at("l2_v_projected", n + 1))
                dve.tensor_tensor(v[:, 0:D], bank(2), erows[:, u, BV, :], ALU.add).then_inc(sig("l2_v_ready"), 1)

            def statistics(rows):
                settle()
                dve.bn_stats(ln_st[:], rows[:])
                aggregate(ln_st[:])

            def aggregate(stats):
                settle()
                dve.bn_aggr(ln_mv[:], stats)
                settle()
                dve.tensor_scalar_add(ln_var[:], ln_mv[:, 1:2], EPS).then_inc(sig("l2_var_ready"), 1)

            def probabilities(n):
                normalise("l2_exps_ready", "l2_prob_ready", n)
                dve.wait_ge(*at("l2_prob_transposed", n * 2 + 1))
                dve.tensor_copy(prob_t[:, 0:4, :].rearrange("p h n -> p (h n)"), bank(5)).then_inc(sig("l2_prob_t_ready0"), 1)

            def expert_dve(n, u, next_it, has_next):
                if has_next:
                    k_bias(n + 1)
                settle()
                dve.wait_ge(*at("l2_residual_ready", n + 1))
                for half in range(2):
                    r = slice(half * D // 2, (half + 1) * D // 2)
                    dve.wait_ge(*at("l2_o_projected", n * 2 + (half + 1)))
                    dve.tensor_tensor(t1[:, r], ps[:, 4 + half, 0:D // 2], erows[:, u, BO, r], ALU.add)
                    settle()
                    dve.bn_stats(half_st[:, half, :], t1[:, r])
                aggregate(half_st[:])
                dve.scalar_tensor_tensor(x1[:], t1[:], ln_mv[:, 0:1], erows[:, u, G1, :], ALU.subtract, ALU.mult)
                settle()
                dve.wait_ge(*at("l2_rstd_ready", n * 2 + 1))
                for half in (slice(0, D // 2), slice(D // 2, D)):
                    dve.scalar_tensor_tensor(x1[:, half], x1[:, half], ln_rstd[:], erows[:, u, BE1, half], ALU.mult,
                                             ALU.add).then_inc(sig("l2_x1_ready"), 1)
                if has_next:
                    v_bias(n + 1, 1 - u, next_it)
                    maxima("l2_scored", "l2_max_ready", n + 1, DH ** -0.5)
                dve.wait_ge(*at("l2_h2_ready", n + 2))
                dve.tensor_tensor(t1[:], x1[:], h2[:], ALU.add)
                statistics(t1)
                if has_next:
                    probabilities(n + 1)
                dve.scalar_tensor_tensor(t1[:], t1[:], ln_mv[:, 0:1], erows[:, u, G2, :], ALU.subtract, ALU.mult)
                dve.wait_ge(*at("l2_rstd_ready", n * 2 + 2))
                dve.tensor_tensor(rg[:], ln_rstd[:], gated[:, bass.ds(n, 1)], ALU.mult)
                settle()
                dve.scalar_tensor_tensor(acc[:] if has_next else x[:], t1[:], rg[:], acc[:], ALU.mult, ALU.add) \
                    .then_inc(sig("l2_expert_added" if has_next else "x_updated"), 1)

            k_bias(0)
            dve.wait_ge(*at("gate_scored", 1))
            dve.tensor_reduce(small[:, 2:3], ps[:, 5, 0:E], AX.X, ALU.max, negate=True)
            settle()
            dve.tensor_scalar(small[:, 0:1], small[:, 2:3], D ** -0.5, None, ALU.mult).then_inc(sig("gate_max_ready"), 1)
            maxima("l2_scored", "l2_max_ready", 0, DH ** -0.5)
            dve.wait_ge(*at("gate_exp_ready", 1))
            dve.reciprocal(small[:, 2:3], small[:, 1:2])
            settle()
            dve.tensor_scalar(gate8[:], gate8[:], small[:, 2:3], None, ALU.mult)
            settle()
            top2()
            dve.tensor_scalar(gated[:], iota_f[:, 0:E], gidxf[:, 0:1], gtop[:, 0:1], ALU.is_equal, ALU.mult)
            dve.tensor_scalar(small[:, 8:16], iota_f[:, 0:E], gidxf[:, 1:2], gtop[:, 1:2], ALU.is_equal, ALU.mult)
            dve.tensor_tensor(small[:, 4:5], gtop[:, 0:1], gtop[:, 1:2], ALU.add)
            settle()
            dve.tensor_scalar(small[:, 4:5], small[:, 4:5], 1e-9, None, ALU.add)
            dve.tensor_tensor(gated[:], gated[:], small[:, 8:16], ALU.add)
            settle()
            dve.reciprocal(small[:, 4:5], small[:, 4:5])
            settle()
            dve.tensor_scalar(gated[:], gated[:], small[:, 4:5], None, ALU.mult).then_inc(sig("gated_ready"), 1)
            dve.wait_ge(*at("gated_transposed", 1))
            dve.tensor_copy(gated_t[:], ps[0:E, 7, 0:P]).then_inc(sig("gated_t_ready"), 1)
            dve.wait_ge(*at("be2_shared", 1))
            dve.tensor_tensor(acc[:], x[:], bank(7), ALU.add).then_inc(sig("l2_h2_ready"), 1)
            v_bias(0, 0, 0)
            probabilities(0)
            with dve.Fori(0, E // 2 - 1) as i:
                for u in range(2):
                    expert_dve(i * 2 + u, u, i + u, True)
            expert_dve(E - 2, 0, E // 2 - 1, True)
            expert_dve(E - 1, 1, None, False)

            layer_norm(6)
            settle()
            dve.tensor_tensor(x[:], x[:], gcn_b3[:], ALU.add)
            settle()
            for k in range(3):
                dve.wait_ge(*at("gcn_h_projected", 2 * k + 2))
                dve.tensor_copy(ctxv[:, D // 2:], ps[:, 2, 0:D // 2]).then_inc(sig("gcn_h_ready1"), 1)
                if k < 2:
                    dve.wait_ge(*at("gcn_mixed", 2 * k + 2))
                    for c in range(2):
                        last = dve.tensor_scalar(z_t[:, 2 + c, :], ps[:, 3, c * P:(c + 1) * P],
                                                 cols[:, GCNB1 + k, 2 + c:3 + c], 0.0, ALU.add, ALU.max)
                    last.then_inc(sig("gcn_z_ready1"), 1)
            for half in range(2):
                r = slice(half * D // 2, (half + 1) * D // 2)
                dve.wait_ge(*at("gcn_mixed", 5 + half))
                last = dve.tensor_tensor(x[:, r], x[:, r], ps[:, 1 + 2 * half, 0:D // 2], ALU.add)
            last.then_inc(sig("x_updated"), 1)

            layer_norm(7)
            dve.tensor_scalar(lstm_hb[:], lstm_b[:], 0.5, None, ALU.mult).then_inc(sig("lstm_hb_ready"), 1)
            dve.wait_ge(*at("router_scored", 1))
            dve.tensor_tensor(gate8[:], ps[:, 6, 0:E], router_b[:], ALU.add)
            settle()
            top2()
            dve.tensor_scalar(small[:, 0:1], gtop[:, 0:1], -1.0, None, ALU.mult)
            dve.tensor_copy(gated[:], gtop[:]).then_inc(sig("router_max_ready"), 1)
            dve.wait_ge(*at("router_exp_ready", 1))
            dve.tensor_tensor(small[:, 4:5], gate8[:, 0:1], gate8[:, 1:2], ALU.add)
            dve.tensor_scalar(gated[:], iota_f[:, 0:E], gidxf[:, 0:1], gate8[:, 0:1], ALU.is_equal, ALU.mult)
            dve.tensor_scalar(small[:, 8:16], iota_f[:, 0:E], gidxf[:, 1:2], gate8[:, 1:2], ALU.is_equal, ALU.mult)
            settle()
            dve.reciprocal(small[:, 4:5], small[:, 4:5])
            dve.tensor_tensor(gated[:], gated[:], small[:, 8:16], ALU.add)
            settle()
            dve.tensor_scalar(gated[:], gated[:], small[:, 4:5], None, ALU.mult).then_inc(sig("lstm_gated_ready"), 1)
            settle()
            dve.tensor_scalar(gate8[:], gated[:], 0.5, None, ALU.mult)

            def lstm_cell(n, u):
                dve.wait_ge(*at("l3_gate_ready", n * 3 + 2))
                dve.scalar_tensor_tensor(t1[:], prob[:, 0:4, :].rearrange("p c n -> p (c n)"), 1.0,
                                         prob[:, 4:8, :].rearrange("p c n -> p (c n)"), ALU.add, ALU.mult) \
                    .then_inc(sig("l3_cell_ready"), 1)
                dve.wait_ge(*at("l3_cell_tanh_ready", n + 1))
                dve.scalar_tensor_tensor(h_t[u][:].rearrange("p c n -> p (c n)"),
                                         prob_t[:, 0:4, :].rearrange("p c n -> p (c n)"), 1.0,
                                         prob_t[:, 4:8, :].rearrange("p c n -> p (c n)"), ALU.add, ALU.mult) \
                    .then_inc(sig("l3_h_ready"), 1)

            def lstm_add(n, u):
                settle()
                dve.wait_ge(*at("l3_o_projected", n + 1))
                dve.scalar_tensor_tensor(acc[:], bank(3 + u), gate8[:, bass.ds(n, 1)], acc[:], ALU.mult, ALU.add) \
                    .then_inc(sig("l3_expert_added"), 1)

            dve.sem_inc(sig("l3_h_ready"), 1)
            dve.sem_inc(sig("l3_expert_added"), 1)
            dve.wait_ge(*at("lstm_gated_transposed", 1))
            dve.tensor_copy(gated_t[:], ps[0:E, 5, 0:P]).then_inc(sig("lstm_gated_t_ready"), 1)
            lstm_cell(0, 0)
            dve.wait_ge(*at("lstm_bo_shared", 1))
            dve.tensor_tensor(acc[:], x[:], bank(7), ALU.add)
            settle()
            lstm_cell(1, 1)
            lstm_add(0, 0)
            with dve.Fori(1, E // 2) as i:
                for u in range(2):
                    lstm_cell(i * 2 + u, u)
                    lstm_add(i * 2 + (u - 1), 1 - u)
            settle()
            dve.wait_ge(*at("l3_o_projected", E))
            dve.scalar_tensor_tensor(acc[:], bank(4), gate8[:, E - 1:E], acc[:], ALU.mult, ALU.add) \
                .then_inc(sig("x_updated"), 1)


def lay_out(inputs):
    import numpy as np

    a = {k: np.asarray(v) for k, v in inputs.items()}

    def by_partition(w):
        s = w.shape
        w = w.reshape(*s[:-2], s[-2] // P, P, s[-1])
        return np.moveaxis(w, -3, -2)

    def columns(w):
        return np.moveaxis(w.reshape(*w.shape[:-1], -1, P), -1, 0)

    swap = lambda w: np.swapaxes(w, -1, -2)
    o = {"x": a["x"], "src": a["src"].reshape(P, -1), "dst": a["dst"].reshape(P, -1)}
    o["l0_W"] = by_partition(a["L0_gnn_W"].transpose(1, 0, 2).reshape(D, D))
    o["gat_a"] = a["L0_gnn_a"].reshape(H, 2, DH).transpose(1, 0, 2).reshape(2, D)
    for k in ("wq", "wk", "wv", "wo"):
        stack = np.stack([np.repeat(w.reshape(D, -1, DH), D // w.shape[1], axis=1).reshape(D, D)
                          for w in (a[f"L0_ffn_{k}{n}"] for n in range(3))])
        w = by_partition(stack)
        if k == "wq":
            w = w.reshape(3, P, CH, CH, P).swapaxes(2, 3)
        o[f"gqa_{k}"] = w.reshape(3, P, CH * D)
    o["r_w1"] = by_partition(a["L0_ffn_r_w1"])
    o["r_w2"] = a["L0_ffn_r_w2"]
    o["r_b1"] = a["L0_ffn_r_b1"].reshape(P, 1)
    o["r_b2"] = a["L0_ffn_r_b2"].reshape(1, 3)
    o["conv"] = by_partition(a["L1_gnn_W_conv"])
    for k in ("q", "k", "v", "o"):
        o[f"perf_w{k}"] = by_partition(a[f"L1_gnn_W{k}"])
    o["proj_t"] = swap(a["L1_gnn_proj"])
    o["peer_wq"] = by_partition(a["L1_ffn_w_q"])
    o["keys_t"] = a["L1_ffn_keys"].reshape(2, 4, KEYS, 2, 32).transpose(3, 1, 4, 0, 2).reshape(2, P, 2, KEYS)
    o["peer_down"] = by_partition(swap(a["L1_ffn_weight_down_embed"]))
    o["peer_up"] = a["L1_ffn_weight_up_embed"]
    for k in ("q", "k", "v"):
        o[f"exph_w{k}"] = by_partition(a[f"L2_gnn_W{k}"])
    o["gate_wk"] = by_partition(swap(a["L2_ffn_gate_Wk"]))
    o["eq_t"] = by_partition(swap(a["L2_ffn_expert_queries"]))
    qkv = by_partition(swap(a["L2_ffn_Wqkv"]))
    o["l2_wqk"], o["l2_wv"] = qkv[..., 0:2 * D], qkv[..., 2 * D:]
    o["l2_wo"] = by_partition(swap(a["L2_ffn_Wo"]))
    o["l2_w1"] = by_partition(swap(a["L2_ffn_W1"]))
    o["l2_w2"] = np.concatenate([swap(a["L2_ffn_W2"]), a["L2_ffn_bf2"][:, None, :]], axis=1)
    o["l2_rows"] = np.stack([a["L2_ffn_bqkv"][:, 2 * D:], a["L2_ffn_bo"], a["L2_ffn_g1"], a["L2_ffn_be1"],
                             a["L2_ffn_g2"]], axis=1)
    o["bqk"] = columns(a["L2_ffn_bqkv"][:, 0:2 * D]).reshape(P, -1)
    o["bf1"] = swap(a["L2_ffn_bf1"])
    o["be2"] = a["L2_ffn_be2"]
    for n in range(3):
        o[f"gcn_w{n + 1}"] = by_partition(a[f"L3_gnn_W{n + 1}"])
    o["gcn_b3"] = a["L3_gnn_b3"].reshape(1, D)
    o["router_w"] = by_partition(a["L3_ffn_router_w"])
    o["router_b"] = a["L3_ffn_router_b"].reshape(1, E)
    o["l3_wi"] = by_partition(a["L3_ffn_Wi"])
    o["l3_wo"] = by_partition(a["L3_ffn_Wo"])
    o["lstm_b"] = columns(a["L3_ffn_b"]).reshape(P, -1)
    o["lstm_bo"] = a["L3_ffn_bo"]
    o["cols"] = columns(np.stack([a[k] for k in (
        "L1_gnn_norm1_g", "L1_gnn_norm1_b", "L1_gnn_norm2_g", "L1_gnn_norm2_b", "L1_gnn_b_conv",
        "L2_gnn_bn_gamma", "L2_gnn_bn_beta", "L2_ffn_gate_bk", "L3_gnn_b1", "L3_gnn_b2")]))
    return {k: np.ascontiguousarray(w) for k, w in o.items()}


def kernel(**inputs):
    import concourse.bacc as bacc
    from concourse.bass_utils import run_bass_kernel_spmd

    nc = bacc.Bacc("TRN2", target_bir_lowering=False, num_devices=1)
    arrays, aps = {}, {}
    for name, a in lay_out(inputs).items():
        arrays[f"in_{name}"] = a
        aps[name] = nc.dram_tensor(f"in_{name}", a.shape, mybir.dt.from_np(a.dtype), kind="ExternalInput").ap()
    out = nc.dram_tensor("out_x", (P, D), F32, kind="ExternalOutput").ap()
    build(nc, aps, out)
    r = run_bass_kernel_spmd(nc, [arrays], core_ids=[0])
    return r.results[0]["out_x"]
```
